# Optimizing a Trainium2 kernel written in Bass

```python
import numpy as np
import jax
import jax.numpy as jnp

def _softmax(x, axis=-1):
    return jax.nn.softmax(x, axis=axis)

def _gelu(x):
    return jax.nn.gelu(x, approximate=True)

def _silu(x):
    return jax.nn.silu(x)

def _sigmoid(x):
    return jax.nn.sigmoid(x)

def _layernorm(x, axis=-1, eps=1e-05):
    m = jnp.mean(x, axis=axis, keepdims=True)
    v = jnp.var(x, axis=axis, keepdims=True)
    return (x - m) / jnp.sqrt(v + eps)

def _scatter_add(tgt, idx, src, axis=0):
    return tgt.at[idx].add(src)

def _segment_sum(src, seg, n):
    return jax.ops.segment_sum(src, seg, n)
kernel_name = 'mk_adaln_attn_ffn_d1_seqx_r8_c0a601'

def setup_inputs(seed: int=0):
    np.random.seed(seed)
    _w = jnp.asarray

    def _rec_inputs():
        import jax
        import jax.numpy as jnp
        _rk = jax.random.key(seed)
        x = -0.0005207 + 1.001 * jax.random.normal(jax.random.fold_in(_rk, 1), (32, 32, 512), jnp.float32)
        _lenS = 32 - jax.random.randint(jax.random.fold_in(_rk, 7), (32,), 0, max(1, 32 // 4) + 1, jnp.int32)
        _lenS2 = 32 - jax.random.randint(jax.random.fold_in(_rk, 8), (32,), 0, max(1, 32 // 4) + 1, jnp.int32)
        itok_Bx16_0_63 = jax.random.randint(jax.random.fold_in(_rk, 11), (32, 16), 0, 64, jnp.int32)
        itok_B_207_1644 = jax.random.randint(jax.random.fold_in(_rk, 12), (32,), 207, 1645, jnp.int32)
        itok_B_8_3872 = jax.random.randint(jax.random.fold_in(_rk, 13), (32,), 8, 3873, jnp.int32)
        return (x, itok_Bx16_0_63, itok_B_207_1644, itok_B_8_3872)
    x, itok_Bx16_0_63, itok_B_207_1644, itok_B_8_3872 = _rec_inputs()

    def _L0_cond_setup():
        import jax, jax.numpy as jnp
        import numpy as np
        B, S, HID = (4, 128, 512)
        D, HQ, HK = (128, 32, 8)
        PAGES, PSIZE, NPP = (64, 32, 16)
        THETA = 10000.0
        EPS = 1e-06
        SCALE = 1.0 / float(np.sqrt(D))

        def _rmsnorm(t, w):
            var = jnp.mean(t * t, axis=-1, keepdims=True)
            return t * jax.lax.rsqrt(var + EPS) * w

        def _rope(t, pos):
            inv_freq = 1.0 / THETA ** (jnp.arange(0, D, 2, dtype=jnp.float32) / D)
            freqs = pos[..., None].astype(jnp.float32) * inv_freq
            cos = jnp.cos(freqs)[:, :, None, :]
            sin = jnp.sin(freqs)[:, :, None, :]
            t1, t2 = (t[..., :D // 2], t[..., D // 2:])
            return jnp.concatenate([t1 * cos - t2 * sin, t2 * cos + t1 * sin], axis=-1)
        key = jax.random.key(seed)
        ks = jax.random.split(key, 10)
        x = jax.random.normal(ks[0], (B, S, HID), jnp.float32)
        Wq = jax.random.normal(ks[1], (HQ * D, HID), jnp.float32) * 0.02
        Wk = jax.random.normal(ks[2], (HK * D, HID), jnp.float32) * 0.02
        Wv = jax.random.normal(ks[3], (HK * D, HID), jnp.float32) * 0.02
        Wo = jax.random.normal(ks[4], (HID, HQ * D), jnp.float32) * 0.02
        q_norm_w = jax.random.uniform(ks[5], (D,), jnp.float32)
        k_norm_w = jax.random.uniform(ks[6], (D,), jnp.float32)
        k_cache = jax.random.normal(ks[7], (PAGES, PSIZE, HK, D), jnp.float32)
        v_cache = jax.random.normal(ks[8], (PAGES, PSIZE, HK, D), jnp.float32)
        block_table = jnp.arange(B * NPP, dtype=jnp.int32).reshape(B, NPP)
        cache_seqlens = jax.random.randint(ks[9], (B,), 0, 475).astype(jnp.int32)
        return dict(x=x, Wq=Wq, Wk=Wk, Wv=Wv, Wo=Wo, q_norm_w=q_norm_w, k_norm_w=k_norm_w, k_cache=k_cache, v_cache=v_cache, block_table=block_table, cache_seqlens=cache_seqlens)
    _L0_cond_all = _L0_cond_setup()
    _L0_cond_in = {k: v for k, v in _L0_cond_all.items() if k in ('Wq', 'Wk', 'Wv', 'Wo', 'q_norm_w', 'k_norm_w', 'k_cache', 'v_cache')}
    del _L0_cond_all

    def _L0_attn_setup():
        import jax, jax.numpy as jnp
        import numpy as np
        import math
        D_MODEL = 512
        N_HEADS = 32
        HEAD_DIM = D_MODEL // N_HEADS
        CLIP_QKV = 8.0
        ALIBI_BIAS_MAX = 8
        LN_EPS = 1e-05

        def _alibi_slopes(total_num_heads: int, alibi_bias_max: int) -> jnp.ndarray:
            next_p2 = 2 ** math.ceil(math.log2(total_num_heads))
            m = jnp.arange(1, next_p2 + 1, dtype=jnp.float32) * (alibi_bias_max / next_p2)
            slopes = 1.0 / jnp.power(2.0, m)
            if next_p2 != total_num_heads:
                slopes = jnp.concatenate([slopes[1::2], slopes[::2]])[:total_num_heads]
            return slopes

        def _layer_norm(x, w, b):
            mu = jnp.mean(x, axis=-1, keepdims=True)
            var = jnp.var(x, axis=-1, keepdims=True)
            return (x - mu) * jax.lax.rsqrt(var + LN_EPS) * w + b
        key = jax.random.key(seed)
        k0, k1, k2 = jax.random.split(key, 3)
        B, S = (2, 256)
        return {'hidden_states': jax.random.normal(k0, (B, S, D_MODEL), dtype=jnp.float32), 'w_qkv': jax.random.normal(k1, (3 * D_MODEL, D_MODEL), dtype=jnp.float32) * 0.02, 'q_ln_w': jnp.ones((D_MODEL,), jnp.float32), 'q_ln_b': jnp.zeros((D_MODEL,), jnp.float32), 'k_ln_w': jnp.ones((D_MODEL,), jnp.float32), 'k_ln_b': jnp.zeros((D_MODEL,), jnp.float32), 'w_out': jax.random.normal(k2, (D_MODEL, D_MODEL), dtype=jnp.float32) * 0.02}
    _L0_attn_all = _L0_attn_setup()
    _L0_attn_in = {k: v for k, v in _L0_attn_all.items() if k in ('w_qkv', 'q_ln_w', 'q_ln_b', 'k_ln_w', 'k_ln_b', 'w_out')}
    del _L0_attn_all

    def _L0_cond2_setup():
        import math
        import jax, jax.numpy as jnp
        import numpy as np
        H, N, B, L = (32, 64, 16, 512)
        DT_MIN, DT_MAX = (0.001, 0.1)

        def _get_kernel(log_dt, C, log_A_real, A_imag, length):
            Cc = C[..., 0] + 1j * C[..., 1]
            dt = jnp.exp(log_dt)
            A = -jnp.exp(log_A_real) + 1j * A_imag
            dtA = A * dt[:, None]
            P = dtA[:, :, None] * jnp.arange(length, dtype=jnp.float32)
            Cs = Cc * (jnp.exp(dtA) - 1.0) / A
            K = 2.0 * jnp.einsum('hn,hnl->hl', Cs, jnp.exp(P)).real
            return K
        key = jax.random.key(seed)
        ks = jax.random.split(key, 6)
        u = jax.random.normal(ks[0], (B, H, L), dtype=jnp.float32)
        length = jax.random.randint(ks[1], (B,), 0, L)
        log_dt = jax.random.uniform(ks[2], (H,), dtype=jnp.float32) * (math.log(DT_MAX) - math.log(DT_MIN)) + math.log(DT_MIN)
        C = jax.random.normal(ks[3], (H, N, 2), dtype=jnp.float32)
        log_A_real = jnp.log(0.5 * jnp.ones((H, N), dtype=jnp.float32))
        A_imag = math.pi * jnp.broadcast_to(jnp.arange(N, dtype=jnp.float32), (H, N))
        D = jax.random.normal(ks[4], (H,), dtype=jnp.float32)
        return {'u': u, 'length': length, 'log_dt': log_dt, 'C': C, 'log_A_real': log_A_real, 'A_imag': A_imag, 'D': D}
    _L0_cond2_all = _L0_cond2_setup()
    _L0_cond2_in = {k: v for k, v in _L0_cond2_all.items() if k in ('log_dt', 'C', 'log_A_real', 'A_imag', 'D')}
    del _L0_cond2_all

    def _L0_ffn_setup():
        import jax, jax.numpy as jnp
        import numpy as np

        def sparsemax(z):
            E = z.shape[-1]
            z_sorted = -jnp.sort(-z, axis=-1)
            z_cum = jnp.cumsum(z_sorted, axis=-1)
            k = jnp.arange(1, E + 1, dtype=z.dtype)
            support = 1.0 + k * z_sorted > z_cum
            k_z = jnp.sum(support, axis=-1, keepdims=True)
            tau_sum = jnp.take_along_axis(z_cum, k_z.astype(jnp.int32) - 1, axis=-1)
            tau = (tau_sum - 1.0) / k_z.astype(z.dtype)
            return jnp.maximum(z - tau, 0.0)
        key = jax.random.key(seed)
        ks = jax.random.split(key, 6)
        B, S, D_IN, D_OUT, E, R = (8, 256, 512, 512, 8, 16)
        x = jax.random.normal(ks[0], (B, S, D_IN), dtype=jnp.float32)
        W_base = jax.random.normal(ks[1], (D_OUT, D_IN), dtype=jnp.float32) * D_IN ** (-0.5)
        b_base = jax.random.normal(ks[2], (D_OUT,), dtype=jnp.float32) * 0.01
        W_router = jax.random.normal(ks[3], (E, D_IN), dtype=jnp.float32) * D_IN ** (-0.5)
        b_router = jnp.zeros((E,), dtype=jnp.float32)
        lora_A = jax.random.normal(ks[4], (E, D_IN, R), dtype=jnp.float32) * D_IN ** (-0.5)
        lora_B = jnp.zeros((E, R, D_OUT), dtype=jnp.float32)
        return {'x': x, 'W_base': W_base, 'b_base': b_base, 'W_router': W_router, 'b_router': b_router, 'lora_A': lora_A, 'lora_B': lora_B}
    _L0_ffn_all = _L0_ffn_setup()
    _L0_ffn_in = {k: v for k, v in _L0_ffn_all.items() if k in ('W_base', 'b_base', 'W_router', 'b_router', 'lora_A', 'lora_B')}
    del _L0_ffn_all
    return {'x': x, 'itok_Bx16_0_63': itok_Bx16_0_63, 'itok_B_207_1644': itok_B_207_1644, 'itok_B_8_3872': itok_B_8_3872, 'L0_cond_Wq': _L0_cond_in['Wq'], 'L0_cond_Wk': _L0_cond_in['Wk'], 'L0_cond_Wv': _L0_cond_in['Wv'], 'L0_cond_Wo': _L0_cond_in['Wo'], 'L0_cond_q_norm_w': _L0_cond_in['q_norm_w'], 'L0_cond_k_norm_w': _L0_cond_in['k_norm_w'], 'L0_cond_k_cache': _L0_cond_in['k_cache'], 'L0_cond_v_cache': _L0_cond_in['v_cache'], 'L0_attn_w_qkv': _L0_attn_in['w_qkv'], 'L0_attn_q_ln_w': _L0_attn_in['q_ln_w'], 'L0_attn_q_ln_b': _L0_attn_in['q_ln_b'], 'L0_attn_k_ln_w': _L0_attn_in['k_ln_w'], 'L0_attn_k_ln_b': _L0_attn_in['k_ln_b'], 'L0_attn_w_out': _L0_attn_in['w_out'], 'L0_cond2_log_dt': _L0_cond2_in['log_dt'], 'L0_cond2_C': _L0_cond2_in['C'], 'L0_cond2_log_A_real': _L0_cond2_in['log_A_real'], 'L0_cond2_A_imag': _L0_cond2_in['A_imag'], 'L0_cond2_D': _L0_cond2_in['D'], 'L0_ffn_W_base': _L0_ffn_in['W_base'], 'L0_ffn_b_base': _L0_ffn_in['b_base'], 'L0_ffn_W_router': _L0_ffn_in['W_router'], 'L0_ffn_b_router': _L0_ffn_in['b_router'], 'L0_ffn_lora_A': _L0_ffn_in['lora_A'], 'L0_ffn_lora_B': _L0_ffn_in['lora_B']}

def reference(x, itok_Bx16_0_63, itok_B_207_1644, itok_B_8_3872, L0_cond_Wq, L0_cond_Wk, L0_cond_Wv, L0_cond_Wo, L0_cond_q_norm_w, L0_cond_k_norm_w, L0_cond_k_cache, L0_cond_v_cache, L0_attn_w_qkv, L0_attn_q_ln_w, L0_attn_q_ln_b, L0_attn_k_ln_w, L0_attn_k_ln_b, L0_attn_w_out, L0_cond2_log_dt, L0_cond2_C, L0_cond2_log_A_real, L0_cond2_A_imag, L0_cond2_D, L0_ffn_W_base, L0_ffn_b_base, L0_ffn_W_router, L0_ffn_b_router, L0_ffn_lora_A, L0_ffn_lora_B):
    import jax
    import jax.numpy as jnp

    def _L0_cond_ref(x, Wq, Wk, Wv, Wo, q_norm_w, k_norm_w, k_cache, v_cache, block_table, cache_seqlens):
        import jax, jax.numpy as jnp
        import numpy as np
        B, S, HID = (4, 128, 512)
        D, HQ, HK = (128, 32, 8)
        PAGES, PSIZE, NPP = (64, 32, 16)
        THETA = 10000.0
        EPS = 1e-06
        SCALE = 1.0 / float(np.sqrt(D))

        def _rmsnorm(t, w):
            var = jnp.mean(t * t, axis=-1, keepdims=True)
            return t * jax.lax.rsqrt(var + EPS) * w

        def _rope(t, pos):
            inv_freq = 1.0 / THETA ** (jnp.arange(0, D, 2, dtype=jnp.float32) / D)
            freqs = pos[..., None].astype(jnp.float32) * inv_freq
            cos = jnp.cos(freqs)[:, :, None, :]
            sin = jnp.sin(freqs)[:, :, None, :]
            t1, t2 = (t[..., :D // 2], t[..., D // 2:])
            return jnp.concatenate([t1 * cos - t2 * sin, t2 * cos + t1 * sin], axis=-1)
        bsz, seqlen, _ = x.shape
        q = jnp.einsum('bsd,ed->bse', x, Wq).reshape(bsz, seqlen, HQ, D)
        k = jnp.einsum('bsd,ed->bse', x, Wk).reshape(bsz, seqlen, HK, D)
        v = jnp.einsum('bsd,ed->bse', x, Wv).reshape(bsz, seqlen, HK, D)
        q = _rmsnorm(q, q_norm_w)
        k = _rmsnorm(k, k_norm_w)
        pos = cache_seqlens[:, None] + jnp.arange(seqlen)[None, :]
        q = _rope(q, pos)
        k = _rope(k, pos)
        L = NPP * PSIZE
        kc = k_cache[block_table].reshape(bsz, L, HK, D)
        vc = v_cache[block_table].reshape(bsz, L, HK, D)
        k_all = jnp.concatenate([kc, k], axis=1)
        v_all = jnp.concatenate([vc, v], axis=1)
        valid_c = jnp.arange(L)[None, :] < cache_seqlens[:, None]
        valid = jnp.concatenate([valid_c, jnp.ones((bsz, seqlen), dtype=bool)], axis=1)
        rep = HQ // HK
        k_all = jnp.repeat(k_all, rep, axis=2)
        v_all = jnp.repeat(v_all, rep, axis=2)
        scores = jnp.einsum('bqhd,bkhd->bhqk', q, k_all) * SCALE
        scores = jnp.where(valid[:, None, None, :], scores, -1e+30)
        probs = jax.nn.softmax(scores, axis=-1)
        o = jnp.einsum('bhqk,bkhd->bqhd', probs, v_all)
        o = o.reshape(bsz, seqlen, HQ * D)
        return jnp.einsum('bse,de->bsd', o, Wo)

    def _L0_attn_ref(hidden_states, w_qkv, q_ln_w, q_ln_b, k_ln_w, k_ln_b, w_out):
        import jax, jax.numpy as jnp
        import numpy as np
        import math
        D_MODEL = 512
        N_HEADS = 32
        HEAD_DIM = D_MODEL // N_HEADS
        CLIP_QKV = 8.0
        ALIBI_BIAS_MAX = 8
        LN_EPS = 1e-05

        def _alibi_slopes(total_num_heads: int, alibi_bias_max: int) -> jnp.ndarray:
            next_p2 = 2 ** math.ceil(math.log2(total_num_heads))
            m = jnp.arange(1, next_p2 + 1, dtype=jnp.float32) * (alibi_bias_max / next_p2)
            slopes = 1.0 / jnp.power(2.0, m)
            if next_p2 != total_num_heads:
                slopes = jnp.concatenate([slopes[1::2], slopes[::2]])[:total_num_heads]
            return slopes

        def _layer_norm(x, w, b):
            mu = jnp.mean(x, axis=-1, keepdims=True)
            var = jnp.var(x, axis=-1, keepdims=True)
            return (x - mu) * jax.lax.rsqrt(var + LN_EPS) * w + b
        B, S, D = hidden_states.shape
        qkv = jnp.einsum('bsd,ed->bse', hidden_states, w_qkv)
        qkv = jnp.clip(qkv, -CLIP_QKV, CLIP_QKV)
        q, k, v = jnp.split(qkv, 3, axis=-1)
        q = _layer_norm(q, q_ln_w, q_ln_b)
        k = _layer_norm(k, k_ln_w, k_ln_b)
        q = q.reshape(B, S, N_HEADS, HEAD_DIM)
        k = k.reshape(B, S, N_HEADS, HEAD_DIM)
        v = v.reshape(B, S, N_HEADS, HEAD_DIM)
        scale = HEAD_DIM ** (-0.5)
        scores = jnp.einsum('bqhd,bkhd->bhqk', q, k) * scale
        pos = jnp.arange(S)
        rel = pos[None, :] - pos[:, None]
        slopes = _alibi_slopes(N_HEADS, ALIBI_BIAS_MAX)
        bias = slopes[:, None, None] * rel.astype(jnp.float32)
        causal = rel <= 0
        scores = jnp.where(causal[None, None], scores + bias[None], -jnp.inf)
        probs = jax.nn.softmax(scores, axis=-1)
        attn = jnp.einsum('bhqk,bkhd->bqhd', probs, v).reshape(B, S, D)
        return jnp.einsum('bsd,ed->bse', attn, w_out)

    def _L0_cond2_ref(u, length, log_dt, C, log_A_real, A_imag, D):
        import math
        import jax, jax.numpy as jnp
        import numpy as np
        H, N, B, L = (32, 64, 16, 512)
        DT_MIN, DT_MAX = (0.001, 0.1)

        def _get_kernel(log_dt, C, log_A_real, A_imag, length):
            Cc = C[..., 0] + 1j * C[..., 1]
            dt = jnp.exp(log_dt)
            A = -jnp.exp(log_A_real) + 1j * A_imag
            dtA = A * dt[:, None]
            P = dtA[:, :, None] * jnp.arange(length, dtype=jnp.float32)
            Cs = Cc * (jnp.exp(dtA) - 1.0) / A
            K = 2.0 * jnp.einsum('hn,hnl->hl', Cs, jnp.exp(P)).real
            return K
        Bq, Hq, Lq = u.shape
        mask = (jnp.arange(Lq) < length[:, None]).astype(u.dtype)
        u_m = u * mask[:, None, :]
        kernel = _get_kernel(log_dt, C, log_A_real, A_imag, Lq)
        n = 2 * Lq
        k_f = jnp.fft.rfft(kernel, n=n)
        u_f = jnp.fft.rfft(u_m, n=n)
        y = jnp.fft.irfft(u_f * k_f, n=n)[..., :Lq]
        y = y + u_m * D[:, None]
        return y * mask[:, None, :]

    def _L0_ffn_ref(x, W_base, b_base, W_router, b_router, lora_A, lora_B):
        import jax, jax.numpy as jnp
        import numpy as np

        def sparsemax(z):
            E = z.shape[-1]
            z_sorted = -jnp.sort(-z, axis=-1)
            z_cum = jnp.cumsum(z_sorted, axis=-1)
            k = jnp.arange(1, E + 1, dtype=z.dtype)
            support = 1.0 + k * z_sorted > z_cum
            k_z = jnp.sum(support, axis=-1, keepdims=True)
            tau_sum = jnp.take_along_axis(z_cum, k_z.astype(jnp.int32) - 1, axis=-1)
            tau = (tau_sum - 1.0) / k_z.astype(z.dtype)
            return jnp.maximum(z - tau, 0.0)
        base_out = jnp.einsum('bsd,od->bso', x, W_base) + b_base
        logits = jnp.einsum('bsd,ed->bse', x, W_router) + b_router
        weights = sparsemax(logits)
        h = jnp.einsum('bsd,edr->bser', x, lora_A)
        expert_out = jnp.einsum('bser,bse,ero->bso', h, weights, lora_B)
        return base_out + expert_out
    x = x + _L0_attn_ref(_L0_cond_ref(x, L0_cond_Wq, L0_cond_Wk, L0_cond_Wv, L0_cond_Wo, L0_cond_q_norm_w, L0_cond_k_norm_w, L0_cond_k_cache, L0_cond_v_cache, itok_Bx16_0_63, itok_B_207_1644), L0_attn_w_qkv, L0_attn_q_ln_w, L0_attn_q_ln_b, L0_attn_k_ln_w, L0_attn_k_ln_b, L0_attn_w_out)
    x = x + _L0_ffn_ref(_L0_cond2_ref(x, itok_B_8_3872, L0_cond2_log_dt, L0_cond2_C, L0_cond2_log_A_real, L0_cond2_A_imag, L0_cond2_D), L0_ffn_W_base, L0_ffn_b_base, L0_ffn_W_router, L0_ffn_b_router, L0_ffn_lora_A, L0_ffn_lora_B)
    return x

_drawn_inputs = setup_inputs


def setup_inputs(seed=0):
    import zlib

    import numpy as np

    out = dict(_drawn_inputs(seed))
    spreads = {'L0_attn_q_ln_w': (1.0, 0.6),
     'L0_attn_q_ln_b': (0.0, 0.8),
     'L0_attn_k_ln_w': (1.0, 0.6),
     'L0_attn_k_ln_b': (0.0, 2.0),
     'L0_cond2_log_A_real': (-0.6931471824645996, 0.2),
     'L0_ffn_b_router': (0.0, 1.557),
     'L0_ffn_lora_B': (0.0, 0.1)}
    factors = {'L0_cond_Wq': 8.0,
     'L0_cond_Wk': 8.0,
     'L0_cond_Wv': 8.0,
     'L0_cond_Wo': 3.906,
     'L0_cond_q_norm_w': 8.0,
     'L0_cond_k_norm_w': 8.0,
     'L0_cond_k_cache': 8.0,
     'L0_cond_v_cache': 3.839,
     'L0_attn_w_qkv': 3.95,
     'L0_attn_w_out': 3.776,
     'L0_ffn_b_base': 64.0}
    for name, (base, spread) in spreads.items():
        noise = np.random.default_rng([zlib.crc32(name.encode()), seed]).standard_normal(out[name].shape)
        drawn = base * np.exp(spread * noise) if base else spread * noise
        out[name] = jnp.asarray(drawn.astype(out[name].dtype))
    for name, factor in factors.items():
        out[name] = (out[name] * factor).astype(out[name].dtype)
    return out
```

```python
import numpy as np
from contextlib import ExitStack

import concourse.bass as bass
from concourse import mybir

F32 = mybir.dt.float32
I32 = mybir.dt.int32
ALU = mybir.AluOpType
ACT = mybir.ActivationFunctionType
AX = mybir.AxisListType

P = 128
B, S, DM = 32, 32, 512
TOK = B * S
TILES = TOK // P
BPT = P // S
KT = DM // P
HQ, HK, D = 32, 8, 128
REP = HQ // HK
PAGES, PSIZE, NPP = 64, 32, 16
L = NPP * PSIZE
LA = L + S
HALF = HK // 2
THETA = 10000.0
EPS_RMS = 1e-6
SCALE = 1.0 / float(np.sqrt(D))
NH2, HD2 = 32, 16
SCALE2 = HD2 ** -0.5
EPS_LN = 1e-5
CLIP = 8.0
NEG = -1e30
SSM_N = 64
SA, SB2 = 16, 32
EXP, RANK = 8, 16
ER = EXP * RANK
RL = EXP + ER

TWO_PI = 2.0 * np.pi
PI_A = 6.28125
PI_B = float(np.float32(np.round((TWO_PI - PI_A) * 2**20) / 2**20))
PI_C = float(np.float32(TWO_PI - PI_A - PI_B))
MAGIC = 1.5 * 2.0**23
LEAD = 16
PI_LOW = 3.1415925

C_ID = 0
C_KEY = C_ID + P
C_ALIBI = C_KEY + L
C_HM = C_ALIBI + NH2 * S
C_FREQ = C_HM + 8
C_LA = C_FREQ + D // 2
C_LB = C_LA + SA
C_REV = C_LB + SB2
C_S = C_REV + KT
C_QTR = C_S + 1
C_LAST = C_QTR + 1
C_END = C_LAST + 1


def constants():
    c = np.zeros((P, C_END), np.float32)
    p = np.arange(P)
    c[:, C_ID:C_ID + P] = np.eye(P)
    c[:, C_KEY:C_KEY + L] = np.arange(L)
    slopes = 1.0 / np.power(2.0, np.arange(1, NH2 + 1, dtype=np.float32) * np.float32(8 / NH2))
    rel = np.arange(S)[None, :] - (p % S)[:, None]
    bias = slopes[None, :, None].astype(np.float32) * rel[:, None, :].astype(np.float32)
    c[:, C_ALIBI:C_ALIBI + NH2 * S] = np.where(rel[:, None, :] <= 0, bias, NEG).reshape(P, -1)
    c[:, C_HM:C_HM + 8] = (p[:, None] // HD2) == np.arange(8)[None, :]
    inv = 1.0 / np.float32(THETA) ** (np.arange(0, D, 2, dtype=np.float32) / np.float32(D))
    c[:, C_FREQ:C_FREQ + D // 2] = inv.astype(np.float32)
    c[:, C_LA:C_LA + SA] = SB2 * (SA - 1 - np.arange(SA))
    c[:, C_LB:C_LB + SB2] = SB2 - 1 - np.arange(SB2)
    c[:, C_REV:C_REV + KT] = np.arange(KT)[None, :] * P + (P - 1 - p)[:, None]
    c[:, C_S] = p % S
    c[:, C_QTR] = np.where(p < P // 2, 0.25, 0.0)
    c[:, C_LAST] = p == SA - 1
    return c


def link_on(eng, sem):
    at = {"from": 0, "base": 0, "n": 0}

    def link(ins):
        at["n"] += 1
        ins.then_inc(sem, 1)
        eng.wait_ge(sem, at["base"] + at["n"])

    def begin(i, each):
        at["from"], at["each"] = at["base"] + at["n"], each
        at["base"], at["n"] = i * each + at["from"], 0

    def end(count):
        assert at["n"] == at["each"], (at["n"], at["each"])
        at["base"], at["n"] = at["from"] + count * at["each"], 0

    link.begin, link.end, link.count = begin, end, lambda: at["base"] + at["n"]
    return link


def row_of(ap, n):
    return bass.AP(ap.tensor, 0, [[0, P], [1, n]])


class Plan:
    pass


def apart(eng, m):
    eng.sem_inc(m.passed, 1)


def build(nc, t):
    ctx = ExitStack()
    with ctx:
        m = Plan()
        ctx.enter_context(nc.allow_non_contiguous_dma(reason="single columns and vectors, a few KB in all"))
        m.sem = lambda name: ctx.enter_context(nc.semaphore(name))

        def scratch(name, shape):
            return nc.dram_tensor(name, shape, F32, kind="Internal").ap()

        def sbuf(name, shape, dt=F32):
            return ctx.enter_context(nc.sbuf_tensor(name, shape, dt))

        m.q_dram = scratch("q_dram", [B, D, HQ * S])
        m.k_dram = scratch("k_dram", [2, B, D, HALF * S])
        m.v_dram = scratch("v_dram", [2, TOK, HALF * D])
        m.lag_dram = scratch("lag_dram", [S, L + P])

        m.big = sbuf("big", [P, HQ * TOK])
        m.kv = sbuf("kv", [P, 2 * (NPP + 1) * HALF * S + 2 * (KT + 1) * HALF * D])
        m.qb = sbuf("qb", [P, 2 * HQ * S])
        m.wk = sbuf("wk", [P, 8 * LA + 2 * 5 * P])
        m.ident = sbuf("ident", [P, P])[:, :]
        m.keys = sbuf("keys", [P, L])[:, :]
        m.small = sbuf("small", [P, 256])
        m.idx = sbuf("idx", [P, 2, B, KT], I32)
        m.idx_now = sbuf("idx_now", [P, 2, KT], I32)
        m.pages = sbuf("pages", [1, B * NPP], I32)
        m.psum = ctx.enter_context(nc.psum_tensor("psum", [P, 8 * 512], F32))

        m.passed = m.sem("passed")
        m.lens = m.small[:, 0:B]
        m.lens2_rows = m.small[:, 40:40 + TILES]
        m.lens2 = m.small[:, 96:96 + B]
        project_all(nc, t, m)
        attend_pages(nc, t, m)
        project_out(nc, t, m)
        attend_own(nc, t, m)
        convolve(nc, t, m)
        feed_forward(nc, t, m)


def bank(m, i, w=512):
    return m.psum[:, i * 512:i * 512 + w]


def turns_off(nc, link, turn_count, angle, quarter, dst, add):
    link(nc.vector.tensor_scalar(turn_count, angle, 1.0 / TWO_PI, quarter, ALU.mult, ALU.add))
    link(nc.vector.tensor_scalar(turn_count, turn_count, MAGIC, MAGIC, ALU.add, ALU.subtract))
    link(nc.vector.scalar_tensor_tensor(dst, turn_count, -PI_A, angle, ALU.mult, ALU.add))
    link(nc.vector.scalar_tensor_tensor(dst, turn_count, -PI_B, dst, ALU.mult, ALU.add))
    link(nc.vector.scalar_tensor_tensor(dst, turn_count, -PI_C, dst, ALU.mult, ALU.add))
    link(nc.vector.tensor_scalar(dst, dst, add, PI_LOW, ALU.add, ALU.min))
    return nc.vector.tensor_scalar(dst, dst, -PI_LOW, None, ALU.max)


def project_all(nc, t, m):
    sem = m.sem
    CQ = HQ * D // 512
    CK = HK * D // 512
    CH = CQ + 2 * CK
    ROPE = CQ + CK
    RING = 5
    USES = ROPE // RING
    H2 = D // 2
    big, kv, qb, wk = m.big, m.kv, m.qb, m.wk
    o = KT * CH * 512
    w1 = big[:, 0:o].rearrange("p (k n) -> p k n", k=KT)
    x_tile = big[:, o:o + 2 * DM].rearrange("p (s k n) -> p s k n", s=2, k=KT)
    o += 2 * DM
    rope_t = big[:, o:o + 4 * TILES * D].rearrange("p (w t d) -> p w t d", w=4, t=TILES)
    o += 4 * TILES * D
    raw = big[:, o:o + RING * 512].rearrange("p (s n) -> p s n", s=RING)
    roped = kv[:, 0:5 * 512].rearrange("p (s n) -> p s n", s=RING)
    stage_q = kv[:, 5 * 512:10 * 512].rearrange("p (s n) -> p s n", s=RING)
    stage_v = kv[:, 10 * 512:12 * 512].rearrange("p (s n) -> p s n", s=2)
    prod_s = kv[:, 12 * 512:14 * 512].rearrange("p (s n) -> p s n", s=2)
    junk = kv[:, 14 * 512:15 * 512]
    AW = TILES * H2
    ang = [qb[:, i * AW:(i + 1) * AW] for i in range(4)]
    cs = wk[:, 0:2 * AW].rearrange("p (w n) -> p w n", w=2)
    normw = wk[:, 2 * AW:2 * AW + 2 * D].rearrange("p (w d) -> p w d", w=2)
    cfreq = wk[:, 1536:1536 + H2]
    csid = wk[:, 1600:1601]
    eps_rms = wk[:, 1602:1603]
    ssq, rms, rinv = (wk[:, 1616 + 16 * i:1632 + 16 * i] for i in range(3))
    pages_b = wk[:, 2048:2048 + B * NPP].bitcast(I32)
    lens_i = wk[:, 2560:2560 + B].bitcast(I32)
    pos_i = wk[:, 2600:2600 + TILES].bitcast(I32)
    len2_i = wk[:, 2608:2608 + TILES].bitcast(I32)
    len2b_i = wk[:, 2616:2616 + B].bitcast(I32)
    poscol = wk[:, 2660:2660 + TILES]

    tables_in, w_in = sem("tables_in"), sem("w_in")
    x_in = [sem("x_in0"), sem("x_in1")]
    vector_order, scalar_order = sem("vector_order1"), sem("scalar_order1")
    angles_ready, trig_ready = sem("angles_ready"), sem("trig_ready")
    projected = sem("projected")
    norms_ready = sem("norms_ready")
    released = sem("released")
    rotated = sem("rotated")
    turned = sem("turned")
    staged = sem("staged")
    q_out = [sem(f"q_out{i}") for i in range(RING)]
    v_out = [sem(f"v_out{i}") for i in range(CK)]
    TABLES = 16 * (8 + 2 * BPT + 2)

    with nc.Block() as block:
        @block.gpsimd
        def _(pool):
            with pool.Fori(0, TILES // 2) as it:
                for j in range(2):
                    pool.wait_ge(projected, CH * (2 * it + j) + LEAD - CH)
                    pool.dma_start(x_tile[:, j, :, :].rearrange("p k n -> p (k n)"),
                                   t["xT"][bass.ds(2 * it + j, 1), :, :].rearrange("o p n -> p (o n)")).then_inc(x_in[j], 16)

        @block.sync
        def _(sp):
            for i in range(RING):
                sp.sem_inc(q_out[i], 16)
            for i in range(CK):
                sp.sem_inc(v_out[i], 16)
            sp.dma_start(m.ident, t["consts"][:, C_ID:C_ID + P]).then_inc(tables_in, 16)
            sp.dma_start(m.keys, t["consts"][:, C_KEY:C_KEY + L]).then_inc(tables_in, 16)
            sp.dma_start(cfreq, t["consts"][:, C_FREQ:C_FREQ + H2]).then_inc(tables_in, 16)
            sp.dma_start(csid, t["consts"][:, C_S:C_S + 1]).then_inc(tables_in, 16)
            for w, name in enumerate(("q_norm", "k_norm")):
                sp.dma_start(normw[:, w, :], row_of(t[name], D)).then_inc(tables_in, 16)
            sp.dma_start(lens_i, row_of(t["lens"], B)).then_inc(tables_in, 16)
            sp.dma_start(len2b_i, row_of(t["lens2"], B)).then_inc(tables_in, 16)
            for b in range(BPT):
                for dst, name in ((pos_i, "lens"), (len2_i, "lens2")):
                    sp.dma_start(dst[b * S:(b + 1) * S, :],
                                 bass.AP(t[name].tensor, b, [[0, S], [BPT, TILES]])).then_inc(tables_in, 16)
            sp.dma_start(pages_b, row_of(t["table"], B * NPP)).then_inc(tables_in, 16)
            sp.dma_start(m.pages[:, :], bass.AP(t["table"].tensor, 0, [[0, 1], [1, B * NPP]])).then_inc(tables_in, 16)
            for k in range(KT):
                sp.dma_start(w1[:, k, :], t["w1"][:, k, :]).then_inc(w_in, 16)
            with sp.Fori(0, TILES // 2) as it:
                for j in range(2):
                    b0 = (2 * it + j) * BPT
                    for c in range(CH):
                        if c < ROPE:
                            sp.wait_ge(staged, (2 * it + j) * ROPE + c + 1 + LEAD)
                            src = stage_q[:, c % RING, :].rearrange("p (b n) -> p b n", b=BPT)
                            if c < CQ:
                                dst = m.q_dram[bass.ds(b0, BPT), :, c * P:(c + 1) * P]
                            else:
                                dst = m.k_dram[c - CQ, bass.ds(b0, BPT), :, :]
                            sp.dma_start(dst.rearrange("b p n -> p b n"), src).then_inc(q_out[c % RING], 16)
                        else:
                            sp.wait_ge(released, (2 * it + j) * CH + c + 1 + LEAD)
                            sp.dma_start(m.v_dram[c - ROPE, bass.ds((2 * it + j) * P, P), :],
                                         stage_v[:, c - ROPE, :]).then_inc(v_out[c - ROPE], 16)
            for i in range(RING):
                sp.wait_ge(q_out[i], 16 + 16 * USES * TILES)
            for i in range(CK):
                sp.wait_ge(v_out[i], 16 + 16 * TILES)

        @block.scalar
        def _(act):
            act.sem_inc(norms_ready, LEAD)
            act.sem_inc(staged, LEAD)
            act.sem_inc(released, LEAD)
            act.wait_ge(angles_ready, 1)
            nc.scalar.activation(cs[:, 0, :], ang[1], ACT.Sin).then_inc(trig_ready, 1)
            act.wait_ge(angles_ready, 2)
            nc.scalar.activation(cs[:, 1, :], ang[2], ACT.Sin).then_inc(trig_ready, 1)
            link = link_on(act, scalar_order)
            with act.Fori(0, TILES // 2) as it:
                link.begin(it, 2 * ROPE)
                for j in range(2):
                    for c in range(CH):
                        u, r = (2 * it + j) * CH + c, (2 * it + j) * ROPE + c
                        act.wait_ge(projected, u + 1 + LEAD)
                        if c >= ROPE:
                            act.wait_ge(v_out[c - ROPE], (2 * it + j) * 16 + 16)
                            nc.scalar.activation(stage_v[:, c - ROPE, :], bank(m, c % 3), ACT.Copy).then_inc(released, 1)
                        else:
                            act.wait_ge(rotated, r + 1 - RING + LEAD)
                            nc.scalar.activation(raw[:, c % RING, :], bank(m, c % 3), ACT.Copy).then_inc(released, 1)
                            act.wait_ge(released, u + 1 + LEAD)
                            g = c % 4
                            for h in range(4):
                                ins = nc.scalar.activation(junk[:, h * P:(h + 1) * P], raw[:, c % RING, h * P:(h + 1) * P],
                                                           ACT.Square, accum_out=ssq[:, 4 * g + h:4 * g + h + 1])
                            link(ins)
                            nc.scalar.activation(rms[:, 4 * g:4 * g + 4], ssq[:, 4 * g:4 * g + 4], ACT.Sqrt,
                                                 scale=1.0 / D, bias=eps_rms).then_inc(norms_ready, 1)
                        if c >= 2:
                            e = c - 2
                            act.wait_ge(turned, (2 * it + j) * ROPE + e + 1 + LEAD)
                            act.wait_ge(q_out[e % RING], ((2 * it + j) * USES + e // RING) * 16 + 16)
                            nc.scalar.activation(
                                stage_q[:, e % RING, :].rearrange("p (b h s) -> p h b s", b=BPT, h=4),
                                bank(m, 3 + e % 2).rearrange("p (h b s) -> p h b s", h=4, b=BPT), ACT.Copy).then_inc(staged, 1)
                link.end(TILES // 2)

        @block.vector
        def _(dve):
            dve.sem_inc(rotated, LEAD)
            link = link_on(dve, vector_order)
            dve.wait_ge(tables_in, TABLES)
            nc.vector.memset(eps_rms, EPS_RMS)
            nc.vector.tensor_copy(m.lens, lens_i)
            nc.vector.tensor_copy(m.lens2, len2b_i)
            nc.vector.tensor_copy(m.lens2_rows, len2_i)
            link(nc.vector.tensor_scalar(poscol, pos_i, csid, None, ALU.add))
            by_quarter = pages_b.rearrange("p (b k r) -> p b k r", b=B, r=BPT)
            for r in range(BPT):
                rows = slice(r * S, (r + 1) * S)
                link(nc.vector.tensor_scalar(m.idx[rows, 0, :, :], by_quarter[rows, :, :, r], float(PSIZE), csid[rows, :],
                                             ALU.mult, ALU.add))
            nc.vector.tensor_scalar(m.idx[:, 1, :, :], m.idx[:, 0, :, :], float(PAGES * PSIZE), None, ALU.add)
            link(nc.vector.tensor_tensor(ang[0].rearrange("p (t d) -> p t d", t=TILES),
                                         poscol.unsqueeze(2).broadcast_to([P, TILES, H2]),
                                         cfreq.unsqueeze(1).broadcast_to([P, TILES, H2]), ALU.mult))
            for quarter, dst in ((0.0, ang[1]), (0.25, ang[2])):
                turns_off(nc, link, ang[3], ang[0], quarter, dst, quarter * TWO_PI).then_inc(angles_ready, 1)
            dve.wait_ge(trig_ready, 2)
            sin, cos = (cs[:, i, :].rearrange("p (t d) -> p t d", t=TILES) for i in range(2))
            for w in range(2):
                for lo in range(2):
                    own = normw[:, w, lo * H2:(lo + 1) * H2].unsqueeze(1).broadcast_to([P, TILES, H2])
                    other = normw[:, w, (1 - lo) * H2:(2 - lo) * H2].unsqueeze(1).broadcast_to([P, TILES, H2])
                    nc.vector.tensor_tensor(rope_t[:, 2 * w, :, lo * H2:(lo + 1) * H2], cos, own, ALU.mult)
                    link(nc.vector.tensor_tensor(rope_t[:, 2 * w + 1, :, lo * H2:(lo + 1) * H2], sin, other, ALU.mult))
                half_s = rope_t[:, 2 * w + 1, :, 0:H2]
                link(nc.vector.tensor_scalar(half_s, half_s, -1.0, None, ALU.mult))

            with dve.Fori(0, TILES // 2) as it:
                link.begin(it, 2 * ROPE * 4)
                for j in range(2):
                    for c in range(ROPE):
                        r = (2 * it + j) * ROPE + c
                        w = 0 if c < CQ else 1
                        dve.wait_ge(released, (2 * it + j) * CH + c + 1 + LEAD)
                        rot = raw[:, c % RING, :].rearrange("p (h d) -> p h d", h=4)
                        ps = prod_s[:, c % 2, :].rearrange("p (h d) -> p h d", h=4)
                        cos_t, sin_t = (rope_t[:, 2 * w + i, bass.ds(2 * it + j, 1), :] for i in range(2))
                        nc.vector.tensor_tensor(ps[:, :, 0:H2], rot[:, :, H2:D], sin_t[:, :, 0:H2].broadcast_to([P, 4, H2]), ALU.mult)
                        link(nc.vector.tensor_tensor(ps[:, :, H2:D], rot[:, :, 0:H2], sin_t[:, :, H2:D].broadcast_to([P, 4, H2]), ALU.mult))
                        dve.wait_ge(norms_ready, r + 1 + LEAD)
                        link(nc.vector.tensor_tensor(rot, rot, cos_t.broadcast_to([P, 4, D]), ALU.mult))
                        link(nc.vector.tensor_tensor(raw[:, c % RING, :], raw[:, c % RING, :], prod_s[:, c % 2, :], ALU.add))
                        g = c % 4
                        link(nc.vector.reciprocal(rinv[:, 4 * g:4 * g + 4], rms[:, 4 * g:4 * g + 4]))
                        dve.wait_ge(turned, r + 1 - RING + LEAD)
                        nc.vector.tensor_tensor(roped[:, c % RING, :].rearrange("p (h d) -> p h d", h=4), rot,
                                                rinv[:, 4 * g:4 * g + 4].unsqueeze(2).broadcast_to([P, 4, D]),
                                                ALU.mult).then_inc(rotated, 1)
                link.end(TILES // 2)

        @block.tensor
        def _(pe):
            pe.sem_inc(projected, LEAD)
            pe.sem_inc(turned, LEAD)
            pe.wait_ge(w_in, 16 * KT)
            pe.wait_ge(tables_in, TABLES)
            with pe.Fori(0, TILES // 2) as it:
                for j in range(2):
                    pe.wait_ge(x_in[j], 16 * it + 16)
                    for c in range(CH):
                        pe.wait_ge(released, (2 * it + j) * CH + c + 1 - 3 + LEAD)
                        for k in range(KT):
                            ins = nc.tensor.matmul(bank(m, c % 3), x_tile[:, j, k, :], w1[:, k, c * 512:(c + 1) * 512],
                                                   start=(k == 0), stop=(k == KT - 1))
                        ins.then_inc(projected, 1)
                        if c >= 2:
                            e = c - 2
                            r = (2 * it + j) * ROPE + e
                            pe.wait_ge(rotated, r + 1 + LEAD)
                            pe.wait_ge(staged, r + 1 - 2 + LEAD)
                            for h in range(4):
                                ins = nc.tensor.transpose(bank(m, 3 + e % 2)[:, h * P:(h + 1) * P],
                                                          roped[:, e % RING, h * P:(h + 1) * P], m.ident)
                            ins.then_inc(turned, 1)


def attend_pages(nc, t, m):
    sem = m.sem
    KW = (NPP + 1) * HALF * S
    kg = m.kv[:, 0:2 * KW].rearrange("p (s g h k) -> p s g h k", s=2, g=NPP + 1, h=HALF)
    vg = m.kv[:, 2 * KW:].rearrange("p (s t h d) -> p s t h d", s=2, t=KT + 1, h=HALF)
    q_t = m.qb[:, :].rearrange("p (s h n) -> p s h n", s=2, h=HK)
    tiles = m.wk[:, 0:8 * LA].rearrange("p (s n) -> p s n", s=8)
    mask, masked, probs = tiles[:, 0:2], tiles[:, 2:4], tiles[:, 4:8]
    probs_t = m.wk[:, 8 * LA:].rearrange("p (s n) -> p s n", s=2)
    out_t = m.big[:, :].rearrange("p (h n) -> p h n", h=HQ)
    row_max, bias, row_sum, inv_sum = (m.small[:, 128 + 4 * i:132 + 4 * i] for i in range(4))
    UNITS = B * HK
    PER = 16
    ITERS = UNITS // PER

    k_in = [sem("k_in0"), sem("k_in1")]
    v_in = [sem("v_in0"), sem("v_in1")]
    q_in = [sem("q_in0"), sem("q_in1")]
    rows_ready = sem("rows_ready")
    vector_order = sem("vector_order2")
    scored = sem("scored")
    maxed = sem("maxed")
    biased = sem("biased")
    exped = sem("exped")
    inverted = sem("inverted")
    normed = sem("normed")
    p_turned = sem("p_turned")
    p_copied = sem("p_copied")
    summed = sem("summed")
    stored = sem("stored")
    K_DMAS, V_DMAS = 16 * (NPP + 1), 16 * (KT + 1)

    def scores_bank(j):
        return m.psum[:, (j % 2) * 1024:(j % 2) * 1024 + LA]

    with nc.Block() as block:
        @block.sync
        def _(sp):
            regs = [sp.alloc_register(f"page{i}") for i in range(NPP)]
            with sp.Fori(0, ITERS) as it:
                for jh in range(4):
                    hb = 4 * it + jh
                    n = 2 * it + jh // 2
                    slot, half = jh % 2, jh % 2
                    if half == 0:
                        sp.wait_ge(scored, n * HK - HK + LEAD)
                        sp.dma_start(q_t[:, (jh // 2) % 2, :, :].rearrange("p h n -> p (h n)"),
                                     m.q_dram[bass.ds(n, 1), :, :].rearrange("o p n -> p (o n)")).then_inc(q_in[(jh // 2) % 2], 16)
                    sp.wait_ge(scored, hb * HALF - HALF + LEAD)
                    sp.dma_start(kg[:, slot, NPP, :, :].rearrange("p h k -> p (h k)"),
                                 m.k_dram[half, bass.ds(n, 1), :, :].rearrange("o p n -> p (o n)")).then_inc(k_in[slot], 16)
                    if half == 0:
                        sp.reg_load(regs, m.pages[0:1, bass.ds(n * NPP, NPP)])
                        batch_pages = [sp.snap(r, min_val=0, max_val=PAGES - 1) for r in regs]
                    for g, page in enumerate(batch_pages):
                        sp.dma_start(kg[:, slot, g, :, :].rearrange("p h k -> p (h k)"),
                                     t["kT"][half, bass.ds(page, 1), :, :].rearrange("o p n -> p (o n)")).then_inc(k_in[slot], 16)

        @block.gpsimd
        def _(pool):
            v_rows = t["v"].rearrange("a g k n -> (a g k) n")

            def gather(hb, n, half):
                slot = half
                pool.wait_ge(summed, hb * HALF - HALF + LEAD)
                nc.gpsimd.tensor_copy(m.idx_now[:, slot, :], m.idx[:, half, bass.ds(n, 1), :].rearrange("p o k -> p (o k)")).then_inc(rows_ready, 1)
                pool.wait_ge(rows_ready, hb + 1)
                apart(pool, m)
                for k in range(KT):
                    pool.indirect_dma_start(out=vg[:, slot, k, :, :].rearrange("p h d -> p (h d)"), out_offset=None, in_=v_rows,
                                            in_offset=bass.IndirectOffsetOnAxis(ap=m.idx_now[:, slot, k:k + 1], axis=0)).then_inc(v_in[slot], 16)
                pool.dma_start(vg[0:S, slot, KT, :, :].rearrange("p h d -> p (h d)"),
                               m.v_dram[half, bass.ds(n * S, S), :]).then_inc(v_in[slot], 16)

            with pool.Fori(0, B) as n:
                for half in range(2):
                    gather(2 * n + half, n, half)

        @block.tensor
        def _(pe):
            for s in (scored, p_turned, summed):
                pe.sem_inc(s, LEAD)

            def scores(it, j):
                u, slot, h = PER * it + j, (j // HALF) % 2, j % HALF
                if j % HK == 0:
                    pe.wait_ge(q_in[(j // HK) % 2], 16 * it + 16)
                if j % HALF == 0:
                    pe.wait_ge(k_in[slot], (2 * it + j // HK) * K_DMAS + K_DMAS)
                pe.wait_ge(maxed, u + 1 - 2 + LEAD)
                lhs = q_t[:, (j // HK) % 2, j % HK, :]
                nc.tensor.matmul(scores_bank(j)[:, 0:L], lhs, kg[:, slot, 0:NPP, h, :], start=True, stop=True)
                nc.tensor.matmul(scores_bank(j)[:, L:LA], lhs, kg[:, slot, NPP, h, :], start=True, stop=True).then_inc(scored, 1)

            def turn(u, j):
                pe.wait_ge(normed, u + 1 + LEAD)
                pe.wait_ge(p_copied, u + LEAD)
                for k in range(KT):
                    nc.tensor.transpose(bank(m, 4)[:, k * P:(k + 1) * P], probs[:, j % 4, k * P:(k + 1) * P], m.ident)
                nc.tensor.transpose(bank(m, 5)[0:S, 0:P], probs[:, j % 4, L:LA], m.ident).then_inc(p_turned, 1)

            def output(it, u, j):
                slot, h = (j // HALF) % 2, j % HALF
                if j % HALF == 0:
                    pe.wait_ge(v_in[slot], (2 * it + j // HK) * V_DMAS + V_DMAS)
                pe.wait_ge(p_copied, u + 1 + LEAD)
                pe.wait_ge(stored, u + 1 - 2 + LEAD)
                for k in range(KT):
                    nc.tensor.matmul(bank(m, 6 + j % 2)[:, 0:P], vg[:, slot, k, h, :], probs_t[:, j % 2, k * P:(k + 1) * P],
                                     start=(k == 0), stop=False)
                nc.tensor.matmul(bank(m, 6 + j % 2)[:, 0:P], vg[0:S, slot, KT, h, :], probs_t[0:S, j % 2, L:L + P],
                                 start=False, stop=True).then_inc(summed, 1)

            def iteration(it, first):
                for j in range(PER):
                    scores(it, j)
                    if not (first and j < 2):
                        turn(PER * it + j - 2, (j - 2) % PER)
                    if not (first and j < 3):
                        output(it if j >= 3 else it - 1, PER * it + j - 3, (j - 3) % PER)

            iteration(0, True)
            with pe.Fori(1, ITERS) as it:
                iteration(it, False)
            output(ITERS - 1, UNITS - 3, PER - 3)
            turn(UNITS - 2, PER - 2)
            output(ITERS - 1, UNITS - 2, PER - 2)
            turn(UNITS - 1, PER - 1)
            output(ITERS - 1, UNITS - 1, PER - 1)

        @block.vector
        def _(dve):
            for s in (maxed, biased, inverted, normed):
                dve.sem_inc(s, LEAD)
            link = link_on(dve, vector_order)
            link(nc.vector.memset(mask[:, :, L:LA], 0.0))

            def normalise(u, j):
                dve.wait_ge(exped, u + 1 + LEAD)
                nc.vector.reciprocal(inv_sum[:, j % 4:j % 4 + 1], row_sum[:, j % 4:j % 4 + 1]).then_inc(inverted, 1)
                dve.wait_ge(inverted, u + 1 + LEAD)
                nc.vector.tensor_scalar(probs[:, j % 4, :], probs[:, j % 4, :], inv_sum[:, j % 4:j % 4 + 1], None,
                                        ALU.mult).then_inc(normed, 1)

            def iteration(it, first):
                link.begin(0 if first else it - 1, 2)
                for j in range(PER):
                    u = PER * it + j
                    if j % HK == 0:
                        n = 2 * it + j // HK
                        link(nc.vector.tensor_scalar(mask[:, j // HK, 0:L], m.keys, m.lens[:, bass.ds(n, 1)], NEG, ALU.is_ge, ALU.mult))
                    dve.wait_ge(scored, u + 1 + LEAD)
                    dve.wait_ge(exped, u + 1 - 2 + LEAD)
                    apart(dve, m)
                    nc.vector.tensor_tensor_reduce(out=masked[:, j % 2, :], in0=scores_bank(j), in1=mask[:, j // HK, :], scale=1.0,
                                                   scalar=-3.0e38, op0=ALU.add, op1=ALU.max,
                                                   accum_out=row_max[:, j % 4:j % 4 + 1]).then_inc(maxed, 1)
                    dve.wait_ge(maxed, u + 1 + LEAD)
                    nc.vector.tensor_scalar(bias[:, j % 4:j % 4 + 1], row_max[:, j % 4:j % 4 + 1], -SCALE, None, ALU.mult).then_inc(biased, 1)
                    if not (first and j < 1):
                        normalise(u - 1, (j - 1) % PER)

            iteration(0, True)
            link.end(1)
            with dve.Fori(1, ITERS) as it:
                iteration(it, False)
            normalise(UNITS - 1, PER - 1)

        @block.scalar
        def _(act):
            for s in (exped, p_copied, stored):
                act.sem_inc(s, LEAD)

            def exponentials(u, j):
                act.wait_ge(biased, u + 1 + LEAD)
                act.wait_ge(p_turned, u + 1 - 4 + LEAD)
                nc.scalar.activation(probs[:, j % 4, :], masked[:, j % 2, :], ACT.Exp, bias=bias[:, j % 4:j % 4 + 1], scale=SCALE,
                                     accum_out=row_sum[:, j % 4:j % 4 + 1]).then_inc(exped, 1)

            def copy_turned(u, j):
                act.wait_ge(p_turned, u + 1 + LEAD)
                act.wait_ge(summed, u + 1 - 2 + LEAD)
                nc.scalar.activation(probs_t[:, j % 2, 0:L], bank(m, 4), ACT.Copy)
                nc.scalar.activation(probs_t[0:S, j % 2, L:L + P], bank(m, 5)[0:S, 0:P], ACT.Copy).then_inc(p_copied, 1)

            def store(n, u, j):
                act.wait_ge(summed, u + 1 + LEAD)
                h = j % HK
                nc.scalar.activation(out_t[:, h * REP:(h + 1) * REP, bass.ds(n * S, S)],
                                     bank(m, 6 + j % 2)[:, 0:P].rearrange("p (g s) -> p g s", g=REP), ACT.Copy).then_inc(stored, 1)

            def iteration(it, first):
                for j in range(PER):
                    u = PER * it + j
                    exponentials(u, j)
                    if not (first and j < 2):
                        copy_turned(u - 2, (j - 2) % PER)
                    if not (first and j < 4):
                        store(2 * it + (j - 4) // HK, u - 4, (j - 4) % PER)

            iteration(0, True)
            with act.Fori(1, ITERS) as it:
                iteration(it, False)
            store(B - 1, UNITS - 4, PER - 4)
            copy_turned(UNITS - 2, PER - 2)
            store(B - 1, UNITS - 3, PER - 3)
            copy_turned(UNITS - 1, PER - 1)
            store(B - 1, UNITS - 2, PER - 2)
            store(B - 1, UNITS - 1, PER - 1)


def project_out(nc, t, m):
    sem = m.sem
    RING = 4
    wo = m.kv[:, 0:RING * DM].rearrange("p (s n) -> p s n", s=RING)
    m.w_qkv = m.kv[:, RING * DM:RING * DM + KT * 3 * DM].rearrange("p (k n) -> p k n", k=KT)
    out_t = m.big[:, :].rearrange("p (h n) -> p h n", h=HQ)
    m.cond_t = m.big[:, 0:KT * TOK].rearrange("p (k n) -> p k n", k=KT)
    HT = TOK // 512
    wo_in = [sem(f"wo_in{i}") for i in range(RING)]
    w_qkv_in, ssm_in = sem("w_qkv_in"), sem("ssm_in")
    head_done = sem("head_done")
    cond_copied = sem("cond_copied")
    gen_v, gen_s = sem("gen_vector"), sem("gen_scalar")

    c = [m.wk[:, 32 * i:32 * i + 32] for i in range(40)]
    log_dt, log_a, a_im, c_re, c_im = c[0:5]
    dt, a_re, re, im, half_re, half_im = c[5:11]
    th, em1, sh, ch, cosm1, e_re, e_im, den, g_re, g_im = c[11:21]
    t0, t1, w_re, w_im, f1, f2, arg_s, arg_c, cnt = c[21:30]
    tab = m.wk[:, 1280:1280 + 128]
    lag_a, lag_b, quarter = tab[:, 0:SA], tab[:, SA:SA + SB2], tab[:, 64:65]
    quarter_angle = tab[:, 65:66]
    m.fac_a = m.wk[:, 1408:1408 + S * SA]
    m.fac_b = m.qb[:, 0:S * SB2]
    mag_b, ang_b, cnt_b = (m.wk[:, 1920 + 1024 * i:2944 + 1024 * i] for i in range(3))
    gen = {}
    mag_a, ang_a, cnt_a = (m.qb[:, 1024:1536], m.wk[:, 4992:5504], m.qb[:, 1536:2048])

    with nc.Block() as block:
        @block.sync
        def _(sp):
            with sp.Fori(0, HQ // RING) as it:
                for i in range(RING):
                    sp.wait_ge(head_done, RING * it + i + 1 - RING + LEAD)
                    sp.dma_start(wo[:, i, :], t["wo"][bass.ds(RING * it + i, 1), :, :].rearrange("o p n -> p (o n)")).then_inc(wo_in[i], 16)
            sp.dma_start(m.w_qkv, t["w_qkv"]).then_inc(w_qkv_in, 16)
            sp.wait_ge(w_qkv_in, 16)

        @block.gpsimd
        def _(pool):
            pool.dma_start(log_dt, row_of(t["log_dt"], S)).then_inc(ssm_in, 16)
            for dst, name in ((log_a, "log_a"), (a_im, "a_imag"), (c_re, "c_re"), (c_im, "c_im")):
                pool.dma_start(dst, t[name]).then_inc(ssm_in, 16)
            pool.dma_start(tab[:, 0:SA + SB2], t["consts"][:, C_LA:C_LB + SB2]).then_inc(ssm_in, 16)
            pool.dma_start(quarter, t["consts"][:, C_QTR:C_QTR + 1]).then_inc(ssm_in, 16)
            pool.wait_ge(ssm_in, 16 * 7)

        @block.tensor
        def _(pe):
            pe.sem_inc(head_done, LEAD)

            def heads(it, first, last):
                for i in range(RING):
                    pe.wait_ge(wo_in[i], 16 * it + 16)
                    for n in range(KT):
                        for h in range(HT):
                            rhs = out_t[:, bass.ds(RING * it + i, 1), h * 512:(h + 1) * 512].rearrange("p o n -> p (o n)")
                            ins = nc.tensor.matmul(bank(m, n * HT + h), wo[:, i, n * P:(n + 1) * P], rhs,
                                                   start=first and i == 0, stop=last and i == RING - 1)
                    ins.then_inc(head_done, 1)

            heads(0, True, False)
            with pe.Fori(1, HQ // RING - 1) as it:
                heads(it, False, False)
            heads(HQ // RING - 1, False, True)

        @block.vector
        def _(dve):
            link = link_on(dve, gen_v)
            at = gen
            tt, ts, stt = nc.vector.tensor_tensor, nc.vector.tensor_scalar, nc.vector.scalar_tensor_tensor

            def mark(name):
                at[name] = link.count()

            def per_s(x, n):
                return x.unsqueeze(2).broadcast_to([P, S, n])

            def lags(x, n):
                return x.unsqueeze(1).broadcast_to([P, S, n])

            def grid(x, n):
                return x.rearrange("p (s n) -> p s n", s=S)

            dve.wait_ge(ssm_in, 16 * 7)
            dve.wait_ge(gen_s, 2)
            link(tt(re, a_re, dt, ALU.mult))
            link(ts(re, re, -1.0, None, ALU.mult))
            link(tt(im, a_im, dt, ALU.mult))
            link(ts(half_re, re, 0.5, None, ALU.mult))
            mark("half_re")
            link(tt(grid(mag_b, SB2), per_s(re, SB2), lags(lag_b, SB2), ALU.mult))
            mark("mag_b")
            link(tt(grid(mag_a, SA), per_s(re, SA), lags(lag_a, SA), ALU.mult))
            mark("mag_a")
            link(ts(half_im, im, 0.5, None, ALU.mult))
            link(turns_off(nc, link, cnt, half_im, 0.0, arg_s, 0.0))
            mark("sh")
            link(turns_off(nc, link, cnt, half_im, 0.25, arg_c, 0.25 * TWO_PI))
            mark("ch")
            link(ts(quarter_angle, quarter, TWO_PI, None, ALU.mult))
            link(tt(grid(ang_b, SB2), per_s(im, SB2), lags(lag_b, SB2), ALU.mult))
            link(turns_off(nc, link, cnt_b, ang_b, quarter, ang_b, quarter_angle))
            mark("ang_b")
            link(tt(grid(ang_a, SA), per_s(im, SA), lags(lag_a, SA), ALU.mult))
            link(turns_off(nc, link, cnt_a, ang_a, 0.25, ang_a, 0.25 * TWO_PI))
            mark("ang_a")
            dve.wait_ge(gen_s, 7)
            link(ts(t0, th, -1.0, 1.0, ALU.mult, ALU.add))
            link(nc.vector.reciprocal(t0, t0))
            link(ts(t1, th, 2.0, None, ALU.mult))
            link(tt(em1, t1, t0, ALU.mult))
            link(tt(cosm1, sh, sh, ALU.mult))
            link(ts(cosm1, cosm1, -2.0, None, ALU.mult))
            link(ts(t0, em1, 1.0, None, ALU.add))
            link(tt(t1, cosm1, t0, ALU.mult))
            link(tt(e_re, em1, t1, ALU.add))
            link(tt(t1, sh, ch, ALU.mult))
            link(tt(t1, t1, t0, ALU.mult))
            link(ts(e_im, t1, 2.0, None, ALU.mult))
            link(tt(t0, a_re, a_re, ALU.mult))
            link(tt(t1, a_im, a_im, ALU.mult))
            link(tt(den, t0, t1, ALU.add))
            link(nc.vector.reciprocal(den, den))
            link(tt(t0, e_re, a_re, ALU.mult))
            link(tt(t1, e_im, a_im, ALU.mult))
            link(tt(g_re, t1, t0, ALU.subtract))
            link(tt(g_re, g_re, den, ALU.mult))
            link(tt(t0, e_re, a_im, ALU.mult))
            link(tt(t1, e_im, a_re, ALU.mult))
            link(tt(g_im, t0, t1, ALU.add))
            link(stt(g_im, g_im, -1.0, den, ALU.mult, ALU.mult))
            link(tt(t0, c_re, g_re, ALU.mult))
            link(tt(t1, c_im, g_im, ALU.mult))
            link(tt(w_re, t0, t1, ALU.subtract))
            link(tt(t0, c_re, g_im, ALU.mult))
            link(tt(t1, c_im, g_re, ALU.mult))
            link(tt(w_im, t0, t1, ALU.add))
            lo, hi = slice(0, SSM_N), slice(SSM_N, P)
            link(ts(f1[lo, :], w_re[lo, :], 2.0, None, ALU.mult))
            link(ts(f2[lo, :], w_im[lo, :], -2.0, None, ALU.mult))
            link(ts(f1[hi, :], w_im[hi, :], -2.0, None, ALU.mult))
            link(ts(f2[hi, :], w_re[hi, :], -2.0, None, ALU.mult))
            dve.wait_ge(gen_s, 9)
            link(tt(m.fac_b, m.fac_b, mag_b, ALU.mult))
            link(tt(grid(cnt_b[:, 0:S * SA], SA), grid(mag_a, SA), per_s(f1, SA), ALU.mult))
            link(tt(grid(ang_a, SA), per_s(im, SA), lags(lag_a, SA), ALU.mult))
            link(turns_off(nc, link, cnt_a, ang_a, 0.0, ang_a, 0.0))
            mark("ang_a2")
            dve.wait_ge(gen_s, 10)
            link(tt(grid(cnt_a, SA), grid(cnt_a, SA), per_s(f2, SA), ALU.mult))
            link(tt(cnt_b[:, 0:S * SA], cnt_b[:, 0:S * SA], cnt_a, ALU.add))
            link(tt(m.fac_a, m.fac_a, cnt_b[:, 0:S * SA], ALU.mult))
            dve.wait_ge(head_done, HQ + LEAD)
            for n in range(1, KT * HT, 2):
                link(nc.vector.tensor_copy(m.cond_t[:, n // HT, (n % HT) * 512:(n % HT) * 512 + 512], bank(m, n)))

        @block.scalar
        def _(act):
            def f(n, dst, src, func, **kw):
                act.wait_ge(gen_v, n)
                link(nc.scalar.activation(dst, src, func, **kw))

            link = link_on(act, gen_s)
            act.wait_ge(ssm_in, 16 * 7)
            link(nc.scalar.activation(dt, log_dt, ACT.Exp))
            link(nc.scalar.activation(a_re, log_a, ACT.Exp))
            f(gen["half_re"], th, half_re, ACT.Tanh)
            f(gen["mag_b"], m.fac_b, mag_b, ACT.Exp)
            f(gen["mag_a"], m.fac_a, mag_a, ACT.Exp)
            f(gen["sh"], sh, arg_s, ACT.Sin)
            f(gen["ch"], ch, arg_c, ACT.Sin)
            f(gen["ang_b"], mag_b, ang_b, ACT.Sin)
            f(gen["ang_a"], mag_a, ang_a, ACT.Sin)
            f(gen["ang_a2"], cnt_a, ang_a, ACT.Sin)
            act.wait_ge(head_done, HQ + LEAD)
            for n in range(0, KT * HT, 2):
                nc.scalar.activation(m.cond_t[:, n // HT, (n % HT) * 512:(n % HT) * 512 + 512], bank(m, n), ACT.Copy).then_inc(cond_copied, 1)
            act.wait_ge(cond_copied, KT * HT // 2)


def attend_own(nc, t, m):
    sem = m.sem
    o = KT * TOK
    region = {}
    for name, cols in (("alibi", NH2 * S), ("x", TILES * DM), ("ct", DM), ("qkv", 3 * DM), ("norm", 2 * DM), ("qT", DM), ("kT", DM),
                       ("keys", 4 * 8 * P), ("vals", 4 * 8 * 64), ("soft", NH2 * S), ("pexp", NH2 * S), ("pT", NH2 * S), ("aT", DM),
                       ("w_out", KT * DM), ("um", DM), ("umT", KT * TOK)):
        region[name] = m.big[:, o:o + cols]
        o += cols
    assert o <= HQ * TOK
    alibi = region["alibi"].rearrange("p (h k) -> p h k", h=NH2)
    m.x = region["x"].rearrange("p (t n) -> p t n", t=TILES)
    m.um_t = region["umT"].rearrange("p (k n) -> p k n", k=KT)
    ct = region["ct"].rearrange("p (k n) -> p k n", k=KT)
    qkv = region["qkv"].rearrange("p (c n) -> p c n", c=3)
    norm = region["norm"].rearrange("p (c n) -> p c n", c=2)
    q_t, k_t = (region[n].rearrange("p (k n) -> p k n", k=KT) for n in ("qT", "kT"))
    key_blocks = region["keys"].rearrange("p (k b h n) -> p k b h n", k=KT, b=BPT, h=8)
    val_blocks = region["vals"].rearrange("p (b g h d) -> p b g h d", b=BPT, g=8, h=4)
    soft, pexp, p_t = (region[n] for n in ("soft", "pexp", "pT"))
    a_t = region["aT"].rearrange("p (k n) -> p k n", k=KT)
    w_out = region["w_out"].rearrange("p (k n) -> p k n", k=KT)
    um = region["um"]
    o = 0
    def cols(n):
        nonlocal o
        o += n
        return m.wk[:, 2048 + o - n:2048 + o]
    stats, mv, var, std, rstd, hmax, hsum, hinv = cols(12), cols(4), cols(2), cols(2), cols(2), cols(NH2), cols(NH2), cols(NH2)
    head_mask, ln, eps = cols(8), cols(4 * KT), cols(1)
    ln = ln.rearrange("p (w k) -> p w k", w=4)
    stats = stats.rearrange("p (c n) -> p c n", c=2)
    lags = cols(S * SB2)
    skip, last_row = cols(S), cols(1)
    zero = cols(P)

    parts_in = sem("parts_in4")
    lag_ready, lag_out, zeroed = sem("lag_ready"), sem("lag_out"), sem("zeroed")
    lag_made = sem("lag_made")
    vector_order, scalar_order, pool_order = sem("vector_order4"), sem("scalar_order4"), sem("pool_order4")
    tile_in = sem("tile_in")
    made = sem("made")
    clipped = sem("clipped")
    var_ready, std_ready = sem("var_ready"), sem("std_ready")
    normed = sem("ln_normed")
    qk_turned = sem("qk_turned")
    q_scaled, k_scaled = sem("q_scaled"), sem("k_scaled")
    blocks_v, blocks_p = sem("key_blocks_v"), sem("key_blocks_p")
    vals_ready = sem("vals_ready")
    scored = sem("scored4")
    shifted = sem("shifted")
    exped = sem("exped4")
    probs_ready = sem("probs_ready")
    p_turned, p_copied = sem("p_turned4"), sem("p_copied4")
    attended, att_copied = sem("attended"), sem("att_copied")
    out_ready, x_ready = sem("out_ready4"), sem("x_ready")
    masked = sem("um_masked")
    um_turned, um_copied = sem("um_turned"), sem("um_copied")
    PARTS = 16 * 7
    QKV, SC, TR, AO = 0, 3, 5, 7

    with nc.Block() as block:
        @block.sync
        def _(sp):
            sp.dma_start(region["alibi"], t["consts"][:, C_ALIBI:C_ALIBI + NH2 * S]).then_inc(parts_in, 16)
            sp.dma_start(head_mask, t["consts"][:, C_HM:C_HM + 8]).then_inc(parts_in, 16)
            sp.dma_start(ln.rearrange("p w k -> p (w k)"), t["ln"].rearrange("p w k -> p (w k)")).then_inc(parts_in, 16)
            sp.dma_start(skip, row_of(t["d_skip"], S)).then_inc(parts_in, 16)
            sp.dma_start(last_row, t["consts"][:, C_LAST:C_LAST + 1]).then_inc(parts_in, 16)
            sp.dma_start(w_out, t["w_out"]).then_inc(parts_in, 16)
            sp.dma_start(m.x, t["x"].rearrange("(t p) n -> p t n", p=P)).then_inc(parts_in, 16)
            sp.wait_ge(lag_made, 1)
            sp.dma_start(m.lag_dram[:, 0:L].rearrange("s (a b) -> a s b", a=SA), lags[0:SA, :].rearrange("p (s b) -> p s b", s=S)).then_inc(lag_out, 16)
            sp.dma_start(m.lag_dram[:, L:L + P], zero[0:S, :]).then_inc(lag_out, 16)
            sp.wait_ge(lag_out, 32)

        @block.gpsimd
        def _(pool):
            pool.sem_inc(tile_in, LEAD)
            pool.sem_inc(blocks_p, LEAD)
            pool.wait_ge(parts_in, PARTS)

            def hidden(tile):
                pool.wait_ge(made, 3 * tile + LEAD)
                nc.gpsimd.tensor_copy(ct, m.cond_t[:, :, bass.ds(tile * P, P)]).then_inc(tile_in, 1)

            def blocks(tile):
                pool.wait_ge(k_scaled, tile + 1 + LEAD)
                pool.wait_ge(scored, tile + LEAD)
                apart(pool, m)
                for h in range(4, 8):
                    ins = nc.gpsimd.tensor_scalar(key_blocks[:, :, :, h, :], k_t.rearrange("p k (b n) -> p k b n", b=BPT),
                                                  head_mask[:, h:h + 1], 1.0, ALU.mult, ALU.mult)
                ins.then_inc(blocks_p, 1)

            hidden(0)
            with pool.Fori(0, TILES - 1) as tile:
                hidden(tile + 1)
                blocks(tile)
            blocks(TILES - 1)

        @block.tensor
        def _(pe):
            for s in (made, qk_turned, scored, p_turned, attended, out_ready, um_turned):
                pe.sem_inc(s, LEAD)
            for s in range(S):
                ins = nc.tensor.matmul(bank(m, QKV + 3 + s // 16)[0:SA, (s % 16) * SB2:(s % 16 + 1) * SB2],
                                       m.fac_a[:, s * SA:(s + 1) * SA], m.fac_b[:, s * SB2:(s + 1) * SB2], start=True, stop=True)
            ins.then_inc(lag_ready, 1)
            pe.wait_ge(parts_in, PARTS)

            def project(tile):
                pe.wait_ge(tile_in, tile + 1 + LEAD)
                for c in range(3):
                    pe.wait_ge(clipped, 3 * tile + c + 1 - 3 + LEAD)
                    for k in range(KT):
                        ins = nc.tensor.matmul(bank(m, QKV + c), ct[:, k, :], m.w_qkv[:, k, c * DM:(c + 1) * DM],
                                               start=(k == 0), stop=(k == KT - 1))
                    ins.then_inc(made, 1)

            def attend(tile, last):
                pe.wait_ge(normed, 2 * tile + 2 + LEAD)
                pe.wait_ge(p_copied, tile + LEAD)
                for c in range(2):
                    for k in range(KT):
                        ins = nc.tensor.transpose(bank(m, TR + c)[:, k * P:(k + 1) * P], norm[:, c, k * P:(k + 1) * P], m.ident)
                ins.then_inc(qk_turned, 1)
                pe.wait_ge(q_scaled, tile + 1 + LEAD)
                pe.wait_ge(blocks_v, tile + 1 + LEAD)
                pe.wait_ge(blocks_p, tile + 1 + LEAD)
                pe.wait_ge(shifted, tile + LEAD)
                for b in range(BPT):
                    for k in range(KT):
                        ins = nc.tensor.matmul(bank(m, SC + k // 2)[b * S:(b + 1) * S, (k % 2) * 256:(k % 2) * 256 + 256],
                                               q_t[:, k, b * S:(b + 1) * S], key_blocks[:, k, b, :, :], start=True, stop=True,
                                               skip_group_check=True)
                ins.then_inc(scored, 1)
                if not last:
                    project(tile + 1)
                pe.wait_ge(probs_ready, tile + 1 + LEAD)
                for g in range(8):
                    ins = nc.tensor.transpose(bank(m, TR + g // 4)[:, (g % 4) * P:(g % 4 + 1) * P], pexp[:, g * P:(g + 1) * P], m.ident)
                ins.then_inc(p_turned, 1)
                pe.wait_ge(p_copied, tile + 1 + LEAD)
                pe.wait_ge(vals_ready, tile + 1 + LEAD)
                pe.wait_ge(um_copied, tile + LEAD)
                for b in range(BPT):
                    for g in range(8):
                        r = 64 * (g % 2)
                        ins = nc.tensor.matmul(bank(m, AO)[r:r + 64, (g // 2) * P + b * S:(g // 2) * P + (b + 1) * S],
                                               val_blocks[:, b, g, :, :].rearrange("p h d -> p (h d)"),
                                               p_t[:, g * P + b * S:g * P + (b + 1) * S], start=True, stop=True, skip_group_check=True)
                ins.then_inc(attended, 1)
                pe.wait_ge(att_copied, tile + 1 + LEAD)
                for k in range(KT):
                    ins = nc.tensor.matmul(bank(m, AO), a_t[:, k, :], w_out[:, k, :], start=(k == 0), stop=(k == KT - 1))
                ins.then_inc(out_ready, 1)
                pe.wait_ge(masked, tile + 1 + LEAD)
                for k in range(KT):
                    ins = nc.tensor.transpose(bank(m, AO)[:, k * P:(k + 1) * P], um[:, k * P:(k + 1) * P], m.ident)
                ins.then_inc(um_turned, 1)

            pe.wait_ge(lag_made, 1)
            project(0)
            with pe.Fori(0, TILES - 1) as tile:
                attend(tile, False)
            attend(TILES - 1, True)

        @block.scalar
        def _(act):
            for s in (std_ready, q_scaled, exped, p_copied, vals_ready, um_copied):
                act.sem_inc(s, LEAD)
            link = link_on(act, scalar_order)
            act.wait_ge(parts_in, PARTS)
            act.wait_ge(zeroed, 1)

            def roots(tile):
                act.wait_ge(var_ready, tile + 1 + LEAD)
                nc.scalar.activation(std, var, ACT.Sqrt).then_inc(std_ready, 1)

            def values(tile):
                act.wait_ge(clipped, 3 * tile + 3 + LEAD)
                act.wait_ge(attended, tile + LEAD)
                for b in range(BPT):
                    for h in range(4):
                        src = qkv[b * S:(b + 1) * S, 2, :].rearrange("p (g h d) -> p g h d", g=8, h=4)[:, :, h, :]
                        ins = nc.scalar.activation(val_blocks[h * S:(h + 1) * S, b, :, h, :], src, ACT.Copy)
                ins.then_inc(vals_ready, 1)

            def tile_steps(tile, last):
                act.wait_ge(qk_turned, tile + 1 + LEAD)
                act.wait_ge(scored, tile + LEAD)
                for k in range(KT):
                    ins = nc.scalar.activation(q_t[:, k, :], bank(m, TR)[:, k * P:(k + 1) * P], ACT.Identity,
                                               scale=ln[:, 0, k:k + 1], bias=ln[:, 1, k:k + 1])
                ins.then_inc(q_scaled, 1)
                values(tile)
                act.wait_ge(shifted, tile + 1 + LEAD)
                nc.scalar.activation(pexp, soft, ACT.Exp).then_inc(exped, 1)
                act.wait_ge(p_turned, tile + 1 + LEAD)
                nc.scalar.activation(p_t[:, 0:512], bank(m, TR), ACT.Copy)
                nc.scalar.activation(p_t[:, 512:1024], bank(m, TR + 1), ACT.Copy).then_inc(p_copied, 1)
                if not last:
                    roots(tile + 1)
                act.wait_ge(um_turned, tile + 1 + LEAD)
                nc.scalar.activation(m.um_t[:, :, bass.ds(tile * P, P)], bank(m, AO).rearrange("p (k n) -> p k n", k=KT), ACT.Copy).then_inc(um_copied, 1)

            roots(0)
            with act.Fori(0, TILES - 1) as tile:
                tile_steps(tile, False)
            tile_steps(TILES - 1, True)

        @block.vector
        def _(dve):
            for s in (clipped, var_ready, normed, k_scaled, blocks_v, shifted, probs_ready, att_copied, x_ready, masked):
                dve.sem_inc(s, LEAD)
            tt, ts = nc.vector.tensor_tensor, nc.vector.tensor_scalar
            link = link_on(dve, vector_order)
            nc.vector.memset(region["vals"], 0.0).then_inc(zeroed, 1)
            dve.wait_ge(parts_in, PARTS)
            link(nc.vector.memset(zero, 0.0))
            dve.wait_ge(lag_ready, 1)
            for i in range(2):
                link(nc.vector.tensor_copy(lags[0:SA, i * 512:(i + 1) * 512], bank(m, 3 + i)[0:SA, :]))
            lag0 = lags[0:SA, :].rearrange("p (s b) -> p s b", s=S)[:, :, SB2 - 1]
            nc.vector.scalar_tensor_tensor(lag0, skip[0:SA, :], last_row[0:SA, :], lag0, ALU.mult, ALU.add).then_inc(lag_made, 1)

            def clip(tile, c):
                dve.wait_ge(made, 3 * tile + c + 1 + LEAD)
                if c == 2:
                    dve.wait_ge(vals_ready, tile + LEAD)
                ts(qkv[:, c, :], bank(m, QKV + c), CLIP, -CLIP, ALU.min, ALU.max).then_inc(clipped, 1)

            def layer_norm(tile):
                dve.wait_ge(clipped, 3 * tile + 3 + LEAD)
                nc.vector.bn_stats(stats[:, 0, :], qkv[:, 0, :])
                link(nc.vector.bn_stats(stats[:, 1, :], qkv[:, 1, :]))
                apart(dve, m)
                nc.vector.bn_aggr(mv[:, 0:2], stats[:, 0, :])
                link(nc.vector.bn_aggr(mv[:, 2:4], stats[:, 1, :]))
                apart(dve, m)
                ts(var, mv.rearrange("p (c n) -> p c n", c=2)[:, :, 1], EPS_LN, None, ALU.add).then_inc(var_ready, 1)
                dve.wait_ge(std_ready, tile + 1 + LEAD)
                link(nc.vector.reciprocal(rstd, std))
                dve.wait_ge(qk_turned, tile + LEAD)
                for c in range(2):
                    ts(norm[:, c, :], qkv[:, c, :], mv[:, 2 * c:2 * c + 1], rstd[:, c:c + 1], ALU.subtract, ALU.mult).then_inc(normed, 1)

            def tile_steps(tile, last, n):
                link.begin(n, 6 if last else 9)
                dve.wait_ge(qk_turned, tile + 1 + LEAD)
                dve.wait_ge(blocks_p, tile + LEAD)
                for k in range(KT):
                    ins = ts(k_t[:, k, :], bank(m, TR + 1)[:, k * P:(k + 1) * P], ln[:, 2, k:k + 1], ln[:, 3, k:k + 1], ALU.mult, ALU.add)
                ins.then_inc(k_scaled, 1)
                dve.wait_ge(k_scaled, tile + 1 + LEAD)
                dve.wait_ge(scored, tile + LEAD)
                for h in range(4):
                    ins = ts(key_blocks[:, :, :, h, :], k_t.rearrange("p k (b n) -> p k b n", b=BPT), head_mask[:, h:h + 1], None, ALU.mult)
                ins.then_inc(blocks_v, 1)
                dve.wait_ge(scored, tile + 1 + LEAD)
                s3 = soft.rearrange("p (h k) -> p h k", h=NH2)
                e3 = pexp.rearrange("p (h k) -> p h k", h=NH2)
                for i in range(2):
                    half = slice(i * 512, (i + 1) * 512)
                    ins = nc.vector.scalar_tensor_tensor(soft[:, half], bank(m, SC + i), SCALE2, region["alibi"][:, half], ALU.mult, ALU.add)
                link(ins)
                link(nc.vector.tensor_reduce(hmax, s3, AX.X, ALU.max))
                tt(s3, s3, hmax.unsqueeze(2).broadcast_to([P, NH2, S]), ALU.subtract).then_inc(shifted, 1)
                if not last:
                    clip(tile + 1, 0)
                dve.wait_ge(exped, tile + 1 + LEAD)
                link(nc.vector.tensor_reduce(hsum, e3, AX.X, ALU.add))
                link(nc.vector.reciprocal(hinv, hsum))
                tt(e3, e3, hinv.unsqueeze(2).broadcast_to([P, NH2, S]), ALU.mult).then_inc(probs_ready, 1)
                if not last:
                    clip(tile + 1, 1)
                    clip(tile + 1, 2)
                dve.wait_ge(attended, tile + 1 + LEAD)
                nc.vector.tensor_copy(a_t.rearrange("p k n -> p (k n)"), bank(m, AO)).then_inc(att_copied, 1)
                if not last:
                    layer_norm(tile + 1)
                dve.wait_ge(out_ready, tile + 1 + LEAD)
                row = m.x[:, bass.ds(tile, 1), :].rearrange("p o n -> p (o n)")
                link(tt(row, row, bank(m, AO), ALU.add))
                link(ts(um, m.keys, m.lens2_rows[:, bass.ds(tile, 1)], None, ALU.is_lt))
                tt(um, um, row, ALU.mult).then_inc(masked, 1)

            for c in range(3):
                clip(0, c)
            layer_norm(0)
            with dve.Fori(0, TILES - 1) as tile:
                tile_steps(tile, False, tile)
            link.end(TILES - 1)
            tile_steps(TILES - 1, True, 0)


def convolve(nc, t, m):
    sem = m.sem
    RING = 4
    toep = m.kv[:, 0:RING * L].rearrange("p (s n) -> p s n", s=RING)
    m.ffn_w = m.kv[:, RING * L:RING * L + KT * (DM + RL) + 2 * DM + EXP]
    m.y_t = m.big[:, 0:KT * TOK].rearrange("p (k n) -> p k n", k=KT)
    rev = m.wk[:, 0:KT]
    mask = m.wk[:, 128:128 + KT * B].rearrange("p (k b) -> p k b", k=KT)
    o = 0
    m.w_base = m.ffn_w[:, o:o + KT * DM].rearrange("p (k n) -> p k n", k=KT); o += KT * DM
    m.w_rl = m.ffn_w[:, o:o + KT * RL].rearrange("p (k n) -> p k n", k=KT); o += KT * RL
    m.lora_b = m.ffn_w[:, o:o + DM]; o += DM
    m.b_base = m.ffn_w[:, o:o + DM]; o += DM
    m.b_router = m.ffn_w[:, o:o + EXP]
    toep_in = [sem(f"toep_in{i}") for i in range(RING)]
    rev_in, ffn_in = sem("rev_in"), sem("ffn_in")
    convolved, copied, order = sem("convolved"), sem("conv_copied"), sem("vector_order5")
    u_t = m.um_t.rearrange("p k (b s) -> p k b s", b=B)
    y_t = m.y_t.rearrange("p k (b s) -> p k b s", b=B)

    with nc.Block() as block:
        @block.sync
        def _(sp):
            sp.dma_start(rev, t["consts"][:, C_REV:C_REV + KT]).then_inc(rev_in, 16)
            with sp.Fori(0, S // RING) as it:
                for i in range(RING):
                    sp.wait_ge(convolved, RING * it + i + 1 - RING + LEAD)
                    src = bass.AP(m.lag_dram.tensor, (RING * it + i) * (L + P), [[1, P], [1, L]])
                    sp.dma_start(toep[:, i, :], src).then_inc(toep_in[i], 16)
            sp.dma_start(m.w_base, t["w_base"]).then_inc(ffn_in, 16)
            sp.dma_start(m.w_rl, t["w_rl"]).then_inc(ffn_in, 16)
            sp.dma_start(m.lora_b, t["lora_b"]).then_inc(ffn_in, 16)
            sp.dma_start(m.b_base, row_of(t["b_base"], DM)).then_inc(ffn_in, 16)
            sp.dma_start(m.b_router, row_of(t["b_router"], EXP)).then_inc(ffn_in, 16)
            sp.wait_ge(ffn_in, 16 * 5)

        @block.tensor
        def _(pe):
            pe.sem_inc(convolved, LEAD)
            with pe.Fori(0, S // RING) as it:
                for i in range(RING):
                    s = RING * it + i
                    pe.wait_ge(toep_in[i], 16 * it + 16)
                    pe.wait_ge(copied, s + 1 - RING + LEAD)
                    for d in range(KT):
                        ins = nc.tensor.matmul(bank(m, i)[:, d * B:KT * B], toep[:, i, L - (d + 1) * P:L - d * P],
                                               u_t[:, 0:KT - d, :, bass.ds(s, 1)].rearrange("p k b o -> p k (b o)"),
                                               start=(d == 0), stop=(d == KT - 1), skip_group_check=True)
                    ins.then_inc(convolved, 1)

        @block.vector
        def _(dve):
            dve.sem_inc(copied, LEAD)
            link = link_on(dve, order)
            dve.wait_ge(rev_in, 16)
            link(nc.vector.tensor_tensor(mask, rev.unsqueeze(2).broadcast_to([P, KT, B]), m.lens2.unsqueeze(1).broadcast_to([P, KT, B]), ALU.is_lt))
            with dve.Fori(0, S // RING) as it:
                for i in range(RING):
                    s = RING * it + i
                    dve.wait_ge(convolved, s + 1 + LEAD)
                    nc.vector.tensor_tensor(y_t[:, :, :, bass.ds(s, 1)].rearrange("p k b o -> p k (b o)"),
                                            bank(m, i)[:, 0:KT * B].rearrange("p (k b) -> p k b", k=KT), mask, ALU.mult).then_inc(copied, 1)
            dve.wait_ge(copied, S + LEAD)


def feed_forward(nc, t, m):
    sem = m.sem
    o = 0
    def cols(n, slots=2):
        nonlocal o
        o += n * slots
        return m.wk[:, o - n * slots:o].rearrange("p (s n) -> p s n", s=slots)
    y_tile, rest, lora_t = cols(DM), cols(DM), cols(P)
    lora_w = cols(P)
    logits, tau, weights = cols(EXP), cols(2), cols(EXP)
    pairs, pair_sums, count, sums, taus = cols(EXP * EXP), cols(EXP * EXP), cols(EXP), cols(EXP), cols(EXP)
    result = m.qb[:, 0:2 * DM].rearrange("p (s n) -> p s n", s=2)
    order = sem("vector_order6")
    tile_ready = sem("y_tile_ready")
    routed, based = sem("routed"), sem("based")
    weighted = sem("weighted")
    l_turned, l_copied, summed = sem("l_turned"), sem("l_copied"), sem("summed6")
    finished = sem("finished")
    out_done = [sem("out_done0"), sem("out_done1")]

    with nc.Block() as block:
        @block.scalar
        def _(act):
            for s in (tile_ready, l_copied):
                act.sem_inc(s, LEAD)

            def fetch(tile, j):
                act.wait_ge(based, tile + 1 - 2 + LEAD)
                nc.scalar.activation(y_tile[:, j, :].rearrange("p (k n) -> p k n", k=KT), m.y_t[:, :, bass.ds(tile * P, P)], ACT.Copy).then_inc(tile_ready, 1)

            def lora(tile, j):
                act.wait_ge(l_turned, tile + 1 + LEAD)
                act.wait_ge(summed, tile + 1 - 2 + LEAD)
                nc.scalar.activation(lora_t[:, j, :], bank(m, 6 + j)[:, 0:P], ACT.Copy).then_inc(l_copied, 1)

            def iteration(it, last):
                fetch(2 * it + 1, 1)
                lora(2 * it, 0)
                lora(2 * it + 1, 1)
                if not last:
                    fetch(2 * it + 2, 0)

            fetch(0, 0)
            with act.Fori(0, TILES // 2 - 1) as it:
                iteration(it, False)
            iteration(TILES // 2 - 1, True)

        @block.tensor
        def _(pe):
            for s in (routed, based, l_turned, summed):
                pe.sem_inc(s, LEAD)
            with pe.Fori(0, TILES // 2) as it:
                for j in range(2):
                    tile = 2 * it + j
                    pe.wait_ge(tile_ready, tile + 1 + LEAD)
                    pe.wait_ge(finished, tile + 1 - 2 + LEAD)
                    y = y_tile[:, j, :].rearrange("p (k n) -> p k n", k=KT)
                    for k in range(KT):
                        ins = nc.tensor.matmul(bank(m, 4 + j)[:, 0:RL], y[:, k, :], m.w_rl[:, k, :], start=(k == 0), stop=(k == KT - 1))
                    ins.then_inc(routed, 1)
                    for k in range(KT):
                        ins = nc.tensor.matmul(bank(m, 2 * j), y[:, k, :], m.w_base[:, k, :], start=(k == 0), stop=False)
                    ins.then_inc(based, 1)
                    pe.wait_ge(weighted, tile + 1 + LEAD)
                    nc.tensor.transpose(bank(m, 6 + j)[:, 0:P], lora_w[:, j, :], m.ident).then_inc(l_turned, 1)
                    pe.wait_ge(l_copied, tile + 1 + LEAD)
                    nc.tensor.matmul(bank(m, 2 * j), lora_t[:, j, :], m.lora_b, start=False, stop=True).then_inc(summed, 1)

        @block.vector
        def _(dve):
            for s in (weighted, finished):
                dve.sem_inc(s, LEAD)
            tt, ts = nc.vector.tensor_tensor, nc.vector.tensor_scalar
            link = link_on(dve, order)
            with dve.Fori(0, TILES // 2) as it:
                link.begin(it, 2 * 9)
                for j in range(2):
                    tile = 2 * it + j
                    dve.wait_ge(routed, tile + 1 + LEAD)
                    z, w = logits[:, j, :], weights[:, j, :]
                    pair = pairs[:, j, :].rearrange("p (i k) -> p i k", i=EXP)
                    psum_ = pair_sums[:, j, :].rearrange("p (i k) -> p i k", i=EXP)
                    link(tt(z, bank(m, 4 + j)[:, 0:EXP], m.b_router, ALU.add))
                    zk, zi = z.unsqueeze(1).broadcast_to([P, EXP, EXP]), z.unsqueeze(2).broadcast_to([P, EXP, EXP])
                    link(tt(pair, zk, zi, ALU.is_ge))
                    tt(psum_, pair, zk, ALU.mult)
                    link(nc.vector.tensor_reduce(count[:, j, :], pair, AX.X, ALU.add))
                    link(nc.vector.tensor_reduce(sums[:, j, :], psum_, AX.X, ALU.add))
                    link(nc.vector.reciprocal(count[:, j, :], count[:, j, :]))
                    link(nc.vector.scalar_tensor_tensor(taus[:, j, :], sums[:, j, :], -1.0, count[:, j, :], ALU.add, ALU.mult))
                    link(nc.vector.tensor_reduce(tau[:, j, 0:1], taus[:, j, :], AX.X, ALU.max))
                    link(ts(w, z, tau[:, j, 0:1], 0.0, ALU.subtract, ALU.max))
                    tt(lora_w[:, j, :].rearrange("p (e r) -> p e r", e=EXP), bank(m, 4 + j)[:, EXP:RL].rearrange("p (e r) -> p e r", e=EXP),
                       w.unsqueeze(2).broadcast_to([P, EXP, RANK]), ALU.mult).then_inc(weighted, 1)
                    row = m.x[:, bass.ds(tile, 1), :].rearrange("p o n -> p (o n)")
                    link(tt(rest[:, j, :], row, m.b_base, ALU.add))
                    dve.wait_ge(summed, tile + 1 + LEAD)
                    dve.wait_ge(out_done[j], 16 * it + 16)
                    tt(result[:, j, :], rest[:, j, :], bank(m, 2 * j), ALU.add).then_inc(finished, 1)
            link.end(TILES // 2)

        @block.sync
        def _(sp):
            for s in out_done:
                sp.sem_inc(s, 16)
            with sp.Fori(0, TILES // 2) as it:
                for j in range(2):
                    sp.wait_ge(finished, 2 * it + j + 1 + LEAD)
                    sp.dma_start(t["out"][bass.ds((2 * it + j) * P, P), :], result[:, j, :]).then_inc(out_done[j], 16)
            for s in out_done:
                sp.wait_ge(s, 16 * (TILES // 2) + 16)


def layouts(i):
    def kt(w):
        return w.reshape(w.shape[0], KT, P).transpose(2, 1, 0)

    x = i["x"].reshape(TOK, DM)
    back = i["L0_ffn_W_base"][:, :].reshape(DM, KT, P)[:, :, ::-1].transpose(2, 1, 0)
    router = i["L0_ffn_W_router"].reshape(EXP, KT, P)[:, :, ::-1].transpose(2, 1, 0)
    lora = i["L0_ffn_lora_A"].transpose(0, 2, 1).reshape(ER, KT, P)[:, :, ::-1].transpose(2, 1, 0)
    twice = lambda a: np.concatenate([a, a], 0)
    return {
        "x": x,
        "xT": x.reshape(TILES, P, KT, P).transpose(0, 3, 2, 1).reshape(TILES, P, DM),
        "table": i["itok_Bx16_0_63"], "lens": i["itok_B_207_1644"], "lens2": i["itok_B_8_3872"],
        "w1": kt(np.concatenate([i["L0_cond_Wq"], i["L0_cond_Wk"], i["L0_cond_Wv"]], 0)),
        "q_norm": i["L0_cond_q_norm_w"], "k_norm": i["L0_cond_k_norm_w"],
        "kT": i["L0_cond_k_cache"].reshape(PAGES, PSIZE, 2, HALF, D).transpose(2, 0, 4, 3, 1).reshape(2, PAGES, D, HALF * PSIZE),
        "v": i["L0_cond_v_cache"].reshape(PAGES, PSIZE, 2, HALF * D).transpose(2, 0, 1, 3),
        "wo": i["L0_cond_Wo"].reshape(DM, HQ, D).transpose(1, 2, 0),
        "w_qkv": kt(i["L0_attn_w_qkv"]), "w_out": kt(i["L0_attn_w_out"]),
        "ln": np.stack([i["L0_attn_" + n].reshape(KT, P).T for n in ("q_ln_w", "q_ln_b", "k_ln_w", "k_ln_b")], 1),
        "log_dt": i["L0_cond2_log_dt"], "log_a": twice(i["L0_cond2_log_A_real"].T), "a_imag": twice(i["L0_cond2_A_imag"].T),
        "c_re": twice(i["L0_cond2_C"][:, :, 0].T), "c_im": twice(i["L0_cond2_C"][:, :, 1].T), "d_skip": i["L0_cond2_D"],
        "w_base": back, "b_base": i["L0_ffn_b_base"], "w_rl": np.concatenate([router, lora], 2),
        "b_router": i["L0_ffn_b_router"], "lora_b": i["L0_ffn_lora_B"].reshape(ER, DM),
        "consts": constants(),
    }


def kernel(**inputs):
    import concourse.bacc as _bacc
    from concourse.bass_utils import run_bass_kernel_spmd as _run

    nc = _bacc.Bacc("TRN2", target_bir_lowering=False, num_devices=1)
    arrays = {n: np.ascontiguousarray(a) for n, a in layouts({n: np.asarray(a) for n, a in inputs.items()}).items()}
    t = {n: nc.dram_tensor("in_" + n, a.shape, mybir.dt.from_np(a.dtype), kind="ExternalInput").ap() for n, a in arrays.items()}
    t["out"] = nc.dram_tensor("out_x", [TOK, DM], F32, kind="ExternalOutput").ap()
    build(nc, t)
    r = _run(nc, [{"in_" + n: a for n, a in arrays.items()}], core_ids=[0])
    return r.results[0]["out_x"].reshape(B, S, DM)
```

```python
import numpy as np
from contextlib import ExitStack

import concourse.bass as bass
from concourse import mybir

F32 = mybir.dt.float32
I32 = mybir.dt.int32
F32R = mybir.dt.float32r
ALU = mybir.AluOpType
ACT = mybir.ActivationFunctionType
AX = mybir.AxisListType

P = 128
B, S, DM = 32, 32, 512
TOK = B * S
TILES = TOK // P
BPT = P // S
KT = DM // P
HQ, HK, D = 32, 8, 128
REP = HQ // HK
PAGES, PSIZE, NPP = 64, 32, 16
L = NPP * PSIZE
LA = L + S
HALF = HK // 2
THETA = 10000.0
EPS_RMS = 1e-6
SCALE = 1.0 / float(np.sqrt(D))
NH2, HD2 = 32, 16
SCALE2 = HD2 ** -0.5
EPS_LN = 1e-5
CLIP = 8.0
NEG = -1e30
SSM_N = 64
SA, SB2 = 16, 32
TOEP = 16
EXP, RANK = 8, 16
ER = EXP * RANK
RL = EXP + ER

TWO_PI = 2.0 * np.pi
PI_A = 6.28125
PI_B = float(np.float32(np.round((TWO_PI - PI_A) * 2**20) / 2**20))
PI_C = float(np.float32(TWO_PI - PI_A - PI_B))
MAGIC = 1.5 * 2.0**23
LEAD = 16
PI_LOW = 3.1415925

C_ID = 0
C_KEY = C_ID + P
C_ALIBI = C_KEY + L
C_HM = C_ALIBI + NH2 * S
C_FREQ = C_HM + 8
C_LA = C_FREQ + D // 2
C_LB = C_LA + SA
C_REV = C_LB + SB2
C_S = C_REV + KT
C_QTR = C_S + 1
C_LAST = C_QTR + 1
C_END = C_LAST + 1


def constants():
    c = np.zeros((P, C_END), np.float32)
    p = np.arange(P)
    c[:, C_ID:C_ID + P] = np.eye(P)
    c[:, C_KEY:C_KEY + L] = np.arange(L)
    slopes = 1.0 / np.power(2.0, np.arange(1, NH2 + 1, dtype=np.float32) * np.float32(8 / NH2))
    rel = np.arange(S)[None, :] - (p % S)[:, None]
    bias = slopes[None, :, None].astype(np.float32) * rel[:, None, :].astype(np.float32)
    c[:, C_ALIBI:C_ALIBI + NH2 * S] = np.where(rel[:, None, :] <= 0, bias, NEG).reshape(P, -1)
    c[:, C_HM:C_HM + 8] = (p[:, None] // HD2) == np.arange(8)[None, :]
    inv = 1.0 / np.float32(THETA) ** (np.arange(0, D, 2, dtype=np.float32) / np.float32(D))
    c[:, C_FREQ:C_FREQ + D // 2] = inv.astype(np.float32)
    c[:, C_LA:C_LA + SA] = SB2 * (SA - 1 - np.arange(SA))
    c[:, C_LB:C_LB + SB2] = SB2 - 1 - np.arange(SB2)
    c[:, C_REV:C_REV + KT] = np.arange(KT)[None, :] * P + (P - 1 - p)[:, None]
    c[:, C_S] = p % S
    c[:, C_QTR] = np.where(p < P // 2, 0.25, 0.0)
    c[:, C_LAST] = p == SA - 1
    return c


def link_on(eng, sem):
    at = {"from": 0, "base": 0, "n": 0}

    def link(ins):
        at["n"] += 1
        ins.then_inc(sem, 1)
        eng.wait_ge(sem, at["base"] + at["n"])

    def begin(i, each):
        at["from"], at["each"] = at["base"] + at["n"], each
        at["base"], at["n"] = i * each + at["from"], 0

    def end(count):
        assert at["n"] == at["each"], (at["n"], at["each"])
        at["base"], at["n"] = at["from"] + count * at["each"], 0

    link.begin, link.end, link.count = begin, end, lambda: at["base"] + at["n"]
    return link


def row_of(ap, n):
    return bass.AP(ap.tensor, 0, [[0, P], [1, n]])


class Plan:
    pass


def apart(eng, m):
    eng.sem_inc(m.passed, 1)


def build(nc, t):
    ctx = ExitStack()
    with ctx:
        m = Plan()
        ctx.enter_context(nc.allow_non_contiguous_dma(reason="single columns and vectors, a few KB in all"))
        m.sem = lambda name: ctx.enter_context(nc.semaphore(name))

        def scratch(name, shape):
            return nc.dram_tensor(name, shape, F32, kind="Internal").ap()

        def sbuf(name, shape, dt=F32):
            return ctx.enter_context(nc.sbuf_tensor(name, shape, dt))

        m.q_dram = scratch("q_dram", [B, D, HQ * S])
        m.k_dram = scratch("k_dram", [2, B, D, HALF * S])
        m.v_dram = scratch("v_dram", [2, TOK, HALF * D])
        m.lag_dram = scratch("lag_dram", [S, L + P])

        m.qb = sbuf("qb", [P, 2 * HQ * S])
        m.wk = sbuf("wk", [P, 8 * LA + 2 * 5 * P])
        m.ident = sbuf("ident", [P, P])[:, :]
        m.keys = sbuf("keys", [P, L])[:, :]
        m.small = sbuf("small", [P, 256])
        m.idx = sbuf("idx", [P, 2, B, KT], I32)
        m.idx_now = sbuf("idx_now", [P, 2, KT], I32)
        m.pages = sbuf("pages", [1, B * NPP], I32)
        m.wo_raw = sbuf("wo_raw", [P, 2, DM])
        m.wo_in = [m.sem("wo_in0"), m.sem("wo_in1")]
        m.psum = ctx.enter_context(nc.psum_tensor("psum", [P, 8 * 512], F32))

        m.passed = m.sem("passed")
        m.lens = m.small[:, 0:B]
        m.lens2_rows = m.small[:, 40:40 + TILES]
        m.lens2 = m.small[:, 96:96 + B]
        project_all(nc, t, m)
        m.big = sbuf("big", [P, HQ * TOK])
        attend_pages(nc, t, m)
        project_out(nc, t, m)
        m.kv = sbuf("kv", [P, KT * (DM + RL) + 2 * DM + EXP + 3 * NH2 * S])
        attend_own(nc, t, m)
        convolve(nc, t, m)
        feed_forward(nc, t, m)


def bank(m, i, w=512):
    return m.psum[:, i * 512:i * 512 + w]


def turns_off(nc, link, turn_count, angle, quarter, dst, add):
    link(nc.vector.tensor_scalar(turn_count, angle, 1.0 / TWO_PI, quarter, ALU.mult, ALU.add))
    link(nc.vector.tensor_scalar(turn_count, turn_count, MAGIC, MAGIC, ALU.add, ALU.subtract))
    link(nc.vector.scalar_tensor_tensor(dst, turn_count, -PI_A, angle, ALU.mult, ALU.add))
    link(nc.vector.scalar_tensor_tensor(dst, turn_count, -PI_B, dst, ALU.mult, ALU.add))
    link(nc.vector.scalar_tensor_tensor(dst, turn_count, -PI_C, dst, ALU.mult, ALU.add))
    link(nc.vector.tensor_scalar(dst, dst, add, PI_LOW, ALU.add, ALU.min))
    return nc.vector.tensor_scalar(dst, dst, -PI_LOW, None, ALU.max)


def exact(ap):
    return ap.bitcast(F32R)


def project_all(nc, t, m):
    sem = m.sem
    CQ = HQ * D // 512
    CK = HK * D // 512
    CH = CQ + 2 * CK
    PAIR = 2 * TILES
    VU = CK * TILES
    UNITS = (CQ + CK) * TILES
    ITERS = CQ // 2
    LAG = 3
    RING = 4
    H2 = D // 2
    AW = TILES * H2
    qb, wk = m.qb, m.wk
    scope = ExitStack()

    def region(name, shape):
        return scope.enter_context(nc.sbuf_tensor(name, [P] + shape, F32))

    x_high, x_low = region("x_high", [TILES, DM]), region("x_low", [TILES, DM])
    w_high, w_low = region("w1_high", [2, KT * 512]), region("w1_low", [2, KT * 512])
    w_raw, x_raw = region("w1_raw", [2, KT * 512]), region("x_raw", [TILES, DM])
    rope_t = region("rope_tables", [4, TILES, D])
    raw, roped = region("raw", [RING, 512]), region("roped", [RING, 512])
    stage_q, stage_v = region("stage_q", [RING, 512]), region("stage_v", [RING, 512])
    prod_s, junk = region("prod_s", [2, 512]), region("junk", [512])
    ang = [qb[:, i * AW:(i + 1) * AW] for i in range(4)]
    cs = wk[:, 0:2 * AW].rearrange("p (w n) -> p w n", w=2)
    normw = wk[:, 2 * AW:2 * AW + 2 * D].rearrange("p (w d) -> p w d", w=2)
    cfreq = wk[:, 1536:1536 + H2]
    csid = wk[:, 1600:1601]
    eps_rms = wk[:, 1602:1603]
    ssq, rms, rinv = (wk[:, 1616 + 16 * i:1632 + 16 * i] for i in range(3))
    pages_b = wk[:, 2048:2048 + B * NPP].bitcast(I32)
    lens_i = wk[:, 2560:2560 + B].bitcast(I32)
    pos_i = wk[:, 2600:2600 + TILES].bitcast(I32)
    len2_i = wk[:, 2608:2608 + TILES].bitcast(I32)
    len2b_i = wk[:, 2616:2616 + B].bitcast(I32)
    poscol = wk[:, 2660:2660 + TILES]

    tables_in = sem("tables_in")
    x_in = [sem(f"x_in{i}") for i in range(TILES)]
    w_in = [sem("w_in0"), sem("w_in1")]
    x_high_ready, x_low_ready = sem("x_high_ready"), sem("x_low_ready")
    w_high_ready, w_low_ready = sem("w_high_ready"), sem("w_low_ready")
    vector_order, scalar_order = sem("vector_order1"), sem("scalar_order1")
    angles_ready, trig_ready = sem("angles_ready"), sem("trig_ready")
    projected = sem("projected")
    released = sem("released")
    norms_ready = sem("norms_ready")
    rotated = sem("rotated")
    scaled = sem("scaled")
    turned = sem("turned")
    staged = sem("staged")
    q_out = [sem(f"q_out{i}") for i in range(RING)]
    v_out = [sem(f"v_out{i}") for i in range(RING)]
    TABLES = 16 * (8 + 2 * BPT + 2)

    def chunk_of(it, i):
        return CK + 2 * it + i // TILES

    with scope, nc.Block() as block:
        @block.sync
        def _(sp):
            for i in range(RING):
                sp.sem_inc(q_out[i], 16)
                sp.sem_inc(v_out[i], 16)

            def load_weights(c, slot):
                sp.dma_start(w_raw[:, slot, :], t["w1"][bass.ds(c, 1), :, :].rearrange("o p n -> p (o n)")).then_inc(w_in[slot], 16)

            def load_x(tile):
                sp.dma_start(x_raw[:, tile, :], t["xT"][tile, :, :]).then_inc(x_in[tile], 16)

            load_x(0)
            load_weights(0, 0)
            for tile in range(1, TILES):
                load_x(tile)
            load_weights(1, 1)
            for u in range(VU):
                if u % TILES == 1:
                    c = u // TILES + 2
                    sp.wait_ge(w_low_ready, KT * (c - 1))
                    load_weights(c, c % 2)
                sp.wait_ge(released, u + 1 + LEAD)
                sp.dma_start(m.v_dram[u // TILES, (u % TILES) * P:(u % TILES + 1) * P, :], stage_v[:, u % RING, :]).then_inc(v_out[u % RING], 16)

            def iteration(it, keys):
                for i in range(PAIR):
                    tile, c = i % TILES, 2 * it + i // TILES
                    if tile == 1 and not keys:
                        sp.wait_ge(w_low_ready, KT * (c + CK + 1))
                        load_weights(c + CK + 2, (CK + i // TILES) % 2)
                    sp.wait_ge(staged, PAIR * it + i + 1 + LEAD)
                    src = stage_q[:, i % RING, :].rearrange("p (b n) -> p b n", b=BPT)
                    rows = slice(tile * BPT, (tile + 1) * BPT)
                    dst = m.k_dram[i // TILES, rows, :, :] if keys else m.q_dram[rows, :, bass.ds(c * P, P)]
                    sp.dma_start(dst.rearrange("b p n -> p b n"), src).then_inc(q_out[i % RING], 16)

            with sp.Fori(0, ITERS) as it:
                iteration(it, False)
            iteration(ITERS, True)
            for i in range(RING):
                sp.wait_ge(q_out[i], 16 + 16 * UNITS // RING)
                sp.wait_ge(v_out[i], 16 + 16 * VU // RING)

        @block.gpsimd
        def _(pool):
            pool.sem_inc(scaled, LEAD)
            pool.dma_start(m.ident, t["consts"][:, C_ID:C_ID + P]).then_inc(tables_in, 16)
            for b in range(BPT):
                for dst, name in ((pos_i, "lens"), (len2_i, "lens2")):
                    pool.dma_start(dst[b * S:(b + 1) * S, :],
                                   bass.AP(t[name].tensor, b, [[0, S], [BPT, TILES]])).then_inc(tables_in, 16)
            pool.dma_start(csid, t["consts"][:, C_S:C_S + 1]).then_inc(tables_in, 16)
            pool.dma_start(cfreq, t["consts"][:, C_FREQ:C_FREQ + H2]).then_inc(tables_in, 16)
            for w, name in enumerate(("q_norm", "k_norm")):
                pool.dma_start(normw[:, w, :], row_of(t[name], D)).then_inc(tables_in, 16)
            pool.dma_start(lens_i, row_of(t["lens"], B)).then_inc(tables_in, 16)
            pool.dma_start(len2b_i, row_of(t["lens2"], B)).then_inc(tables_in, 16)
            pool.dma_start(pages_b, row_of(t["table"], B * NPP)).then_inc(tables_in, 16)
            pool.dma_start(m.keys, t["consts"][:, C_KEY:C_KEY + L]).then_inc(tables_in, 16)
            pool.dma_start(m.pages[:, :], bass.AP(t["table"].tensor, 0, [[0, 1], [1, B * NPP]])).then_inc(tables_in, 16)
            with pool.Fori(0, ITERS + 1) as it:
                for i in range(PAIR):
                    pool.wait_ge(rotated, PAIR * it + i + 1 + LEAD)
                    pool.wait_ge(turned, PAIR * it + i + 1 - RING + LEAD)
                    apart(pool, m)
                    g = i % RING
                    for h in range(4):
                        ins = nc.gpsimd.tensor_scalar(roped[:, g, h * P:(h + 1) * P], raw[:, g, h * P:(h + 1) * P],
                                                      rinv[:, 4 * g + h:4 * g + h + 1], 1.0, ALU.mult, ALU.mult)
                    ins.then_inc(scaled, 1)

        @block.scalar
        def _(act):
            for s in (released, norms_ready, staged):
                act.sem_inc(s, LEAD)

            def split_x(tile):
                act.wait_ge(x_in[tile], 16)
                nc.scalar.activation(exact(x_high[:, tile, :]), x_raw[:, tile, :], ACT.Copy).then_inc(x_high_ready, 1)

            def split_weights(uses, slot, k):
                act.wait_ge(w_in[slot], 16 * uses)
                cols = slice(k * 512, (k + 1) * 512)
                nc.scalar.activation(exact(w_high[:, slot, cols]), w_raw[:, slot, cols], ACT.Copy).then_inc(w_high_ready, 1)

            split_x(0)
            for k in range(KT):
                split_weights(1, 0, k)
            for tile in range(1, TILES // 2):
                split_x(tile)
            for u in range(VU):
                act.wait_ge(projected, u + 1 + LEAD)
                act.wait_ge(v_out[u % RING], 16 * (u // RING) + 16)
                nc.scalar.activation(stage_v[:, u % RING, :], bank(m, u % RING), ACT.Copy).then_inc(released, 1)
                if u < TILES // 2:
                    split_x(u + TILES // 2)
                c, tile = u // TILES, u % TILES
                if tile % 2 == 1:
                    split_weights((c + 1) // 2 + 1, (c + 1) % 2, tile // 2)
                if u == VU // 2 + 2:
                    act.wait_ge(angles_ready, 1)
                    nc.scalar.activation(cs[:, 0, :], ang[1], ACT.Sin).then_inc(trig_ready, 1)
                    act.wait_ge(angles_ready, 2)
                    nc.scalar.activation(cs[:, 1, :], ang[2], ACT.Sin).then_inc(trig_ready, 1)
            link = link_on(act, scalar_order)

            def release(it, i, last):
                r, g = PAIR * it + i, i % RING
                act.wait_ge(projected, VU + r + 1 + LEAD)
                act.wait_ge(scaled, r + 1 - RING + LEAD)
                nc.scalar.activation(raw[:, g, :], bank(m, g), ACT.Copy).then_inc(released, 1)
                act.wait_ge(released, VU + r + 1 + LEAD)
                for h in range(4):
                    ins = nc.scalar.activation(junk[:, h * P:(h + 1) * P], raw[:, g, h * P:(h + 1) * P],
                                               ACT.Square, accum_out=ssq[:, 4 * g + h:4 * g + h + 1])
                link(ins)
                nc.scalar.activation(rms[:, 4 * g:4 * g + 4], ssq[:, 4 * g:4 * g + 4], ACT.Sqrt,
                                     scale=1.0 / D, bias=eps_rms).then_inc(norms_ready, 1)
                if i % 2 == 0 and not (last and i >= TILES):
                    c = CK + i // TILES + 1
                    split_weights(it + c // 2 + 1, c % 2, (i % TILES) // 2)

            def stage(it, i):
                act.wait_ge(turned, PAIR * it + i + 1 + LEAD)
                act.wait_ge(q_out[i % RING], (PAIR // RING * it + i // RING) * 16 + 16)
                nc.scalar.activation(
                    stage_q[:, i % RING, :].rearrange("p (b h s) -> p h b s", b=BPT, h=4),
                    bank(m, 4 + i % RING).rearrange("p (h b s) -> p h b s", h=4, b=BPT), ACT.Copy).then_inc(staged, 1)

            def iteration(it, last):
                for i in range(PAIR):
                    ahead = i + LAG
                    if ahead < PAIR:
                        release(it, ahead, last)
                    elif not last:
                        release(it + 1, ahead - PAIR, False)
                    stage(it, i)

            for i in range(LAG):
                release(0, i, False)
            with act.Fori(0, ITERS) as it:
                link.begin(it, PAIR)
                iteration(it, False)
            link.end(ITERS)
            iteration(ITERS, True)

        @block.vector
        def _(dve):
            dve.sem_inc(rotated, LEAD)
            link = link_on(dve, vector_order)

            def split_x(tile):
                dve.wait_ge(x_high_ready, tile + 1)
                nc.vector.tensor_tensor(exact(x_low[:, tile, :]), x_raw[:, tile, :], x_high[:, tile, :], ALU.subtract).then_inc(x_low_ready, 1)

            def split_weights(c, slot, k):
                dve.wait_ge(w_high_ready, KT * c + k + 1)
                cols = slice(k * 512, (k + 1) * 512)
                nc.vector.tensor_tensor(exact(w_low[:, slot, cols]), w_raw[:, slot, cols], w_high[:, slot, cols], ALU.subtract).then_inc(w_low_ready, 1)

            split_x(0)
            for k in range(KT):
                split_weights(0, 0, k)
            for tile in range(1, TILES // 2):
                split_x(tile)
            dve.wait_ge(tables_in, TABLES)
            nc.vector.memset(eps_rms, EPS_RMS)
            nc.vector.tensor_copy(m.lens, lens_i)
            nc.vector.tensor_copy(m.lens2, len2b_i)
            nc.vector.tensor_copy(m.lens2_rows, len2_i)
            link(nc.vector.tensor_scalar(poscol, pos_i, csid, None, ALU.add))
            for tile in range(TILES // 2, TILES):
                split_x(tile)
            by_quarter = pages_b.rearrange("p (b k r) -> p b k r", b=B, r=BPT)
            for r in range(BPT):
                rows = slice(r * S, (r + 1) * S)
                link(nc.vector.tensor_scalar(m.idx[rows, 0, :, :], by_quarter[rows, :, :, r], float(PSIZE), csid[rows, :],
                                             ALU.mult, ALU.add))
            nc.vector.tensor_scalar(m.idx[:, 1, :, :], m.idx[:, 0, :, :], float(PAGES * PSIZE), None, ALU.add)
            link(nc.vector.tensor_tensor(ang[0].rearrange("p (t d) -> p t d", t=TILES),
                                         poscol.unsqueeze(2).broadcast_to([P, TILES, H2]),
                                         cfreq.unsqueeze(1).broadcast_to([P, TILES, H2]), ALU.mult))
            for quarter, dst in ((0.0, ang[1]), (0.25, ang[2])):
                turns_off(nc, link, ang[3], ang[0], quarter, dst, quarter * TWO_PI).then_inc(angles_ready, 1)
            for k in range(KT):
                split_weights(1, 1, k)
            dve.wait_ge(trig_ready, 2)
            sin, cos = (cs[:, i, :].rearrange("p (t d) -> p t d", t=TILES) for i in range(2))
            for w in range(2):
                for lo in range(2):
                    own = normw[:, w, lo * H2:(lo + 1) * H2].unsqueeze(1).broadcast_to([P, TILES, H2])
                    other = normw[:, w, (1 - lo) * H2:(2 - lo) * H2].unsqueeze(1).broadcast_to([P, TILES, H2])
                    nc.vector.tensor_tensor(rope_t[:, 2 * w, :, lo * H2:(lo + 1) * H2], cos, own, ALU.mult)
                    link(nc.vector.tensor_tensor(rope_t[:, 2 * w + 1, :, lo * H2:(lo + 1) * H2], sin, other, ALU.mult))
                half_s = rope_t[:, 2 * w + 1, :, 0:H2]
                link(nc.vector.tensor_scalar(half_s, half_s, -1.0, None, ALU.mult))
            for k in range(KT):
                split_weights(2, 0, k)

            def rotate(it, i, w):
                r, tile, g = PAIR * it + i, i % TILES, i % RING
                dve.wait_ge(released, VU + r + 1 + LEAD)
                rot = raw[:, g, :].rearrange("p (h d) -> p h d", h=4)
                ps = prod_s[:, i % 2, :].rearrange("p (h d) -> p h d", h=4)
                cos_t, sin_t = (rope_t[:, 2 * w + n, tile:tile + 1, :] for n in range(2))
                nc.vector.tensor_tensor(ps[:, :, 0:H2], rot[:, :, H2:D], sin_t[:, :, 0:H2].broadcast_to([P, 4, H2]), ALU.mult)
                link(nc.vector.tensor_tensor(ps[:, :, H2:D], rot[:, :, 0:H2], sin_t[:, :, H2:D].broadcast_to([P, 4, H2]), ALU.mult))
                dve.wait_ge(norms_ready, r + 1 + LEAD)
                nc.vector.reciprocal(rinv[:, 4 * g:4 * g + 4], rms[:, 4 * g:4 * g + 4])
                link(nc.vector.tensor_tensor(rot, rot, cos_t.broadcast_to([P, 4, D]), ALU.mult))
                nc.vector.tensor_tensor(raw[:, g, :], raw[:, g, :], prod_s[:, i % 2, :], ALU.add).then_inc(rotated, 1)

            def iteration(it, w):
                for i in range(PAIR):
                    rotate(it, i, w)
                    if i % 2 == 0 and not (w == 1 and i >= TILES):
                        c = chunk_of(it, i) + 1
                        split_weights(c, (CK + i // TILES + 1) % 2, (i % TILES) // 2)

            with dve.Fori(0, ITERS) as it:
                link.begin(it, 2 * PAIR)
                iteration(it, 0)
            link.end(ITERS)
            iteration(ITERS, 1)

        @block.tensor
        def _(pe):
            pe.sem_inc(projected, LEAD)
            pe.sem_inc(turned, LEAD)

            def project(u, tile, slot, c, first):
                if first:
                    pe.wait_ge(x_low_ready, tile + 1)
                if tile == 0:
                    pe.wait_ge(w_low_ready, KT * c + KT)
                pe.wait_ge(released, u + 1 - RING + LEAD)
                out = bank(m, tile % RING)
                for k in range(KT):
                    xk, wk_ = slice(k * P, (k + 1) * P), slice(k * 512, (k + 1) * 512)
                    nc.tensor.matmul(out, exact(x_high[:, tile, xk]), exact(w_high[:, slot, wk_]), start=(k == 0), stop=False)
                    nc.tensor.matmul(out, exact(x_high[:, tile, xk]), exact(w_low[:, slot, wk_]), start=False, stop=False)
                    ins = nc.tensor.matmul(out, exact(x_low[:, tile, xk]), exact(w_high[:, slot, wk_]), start=False, stop=(k == KT - 1))
                ins.then_inc(projected, 1)

            def rope_unit(it, i):
                project(VU + PAIR * it + i, i % TILES, (CK + i // TILES) % 2, chunk_of(it, i), False)

            def turn(it, i):
                r = PAIR * it + i
                pe.wait_ge(scaled, r + 1 + LEAD)
                pe.wait_ge(staged, r + 1 - RING + LEAD)
                for h in range(4):
                    ins = nc.tensor.transpose(bank(m, 4 + i % RING)[:, h * P:(h + 1) * P],
                                              roped[:, i % RING, h * P:(h + 1) * P], m.ident)
                ins.then_inc(turned, 1)

            def iteration(it, last):
                for i in range(PAIR):
                    ahead = i + LAG
                    if ahead < PAIR:
                        rope_unit(it, ahead)
                    elif not last:
                        rope_unit(it + 1, ahead - PAIR)
                    turn(it, i)

            for u in range(VU):
                project(u, u % TILES, u // TILES, u // TILES, u < TILES)
            for i in range(LAG):
                rope_unit(0, i)
            pe.wait_ge(tables_in, TABLES)
            with pe.Fori(0, ITERS) as it:
                iteration(it, False)
            iteration(ITERS, True)


def attend_pages(nc, t, m):
    sem = m.sem
    scope = ExitStack()
    kg = scope.enter_context(nc.sbuf_tensor("gathered_keys", [P, 2, NPP + 1, HALF, S], F32))
    vg = scope.enter_context(nc.sbuf_tensor("gathered_values", [P, 2, KT + 1, HALF, D], F32))
    q_t = m.qb[:, :].rearrange("p (s h n) -> p s h n", s=2, h=HK)
    tiles = m.wk[:, 0:8 * LA].rearrange("p (s n) -> p s n", s=8)
    mask, masked, probs = tiles[:, 0:2], tiles[:, 2:4], tiles[:, 4:8]
    probs_t = m.wk[:, 8 * LA:].rearrange("p (s n) -> p s n", s=2)
    out_t = m.big[:, :].rearrange("p (h n) -> p h n", h=HQ)
    row_max, bias, row_sum, inv_sum = (m.small[:, 128 + 4 * i:132 + 4 * i] for i in range(4))
    UNITS = B * HK
    PER = 16
    ITERS = UNITS // PER

    k_in = [sem("k_in0"), sem("k_in1")]
    v_in = [sem("v_in0"), sem("v_in1")]
    q_in = [sem("q_in0"), sem("q_in1")]
    rows_ready = sem("rows_ready")
    vector_order = sem("vector_order2")
    scored = sem("scored")
    maxed = sem("maxed")
    biased = sem("biased")
    exped = sem("exped")
    inverted = sem("inverted")
    normed = sem("normed")
    p_turned = sem("p_turned")
    p_copied = sem("p_copied")
    summed = sem("summed")
    stored = sem("stored")
    K_DMAS, V_DMAS = 16 * (NPP + 1), 16 * (KT + 1)

    def scores_bank(j):
        return m.psum[:, (j % 2) * 1024:(j % 2) * 1024 + LA]

    with scope, nc.Block() as block:
        @block.sync
        def _(sp):
            regs = [sp.alloc_register(f"page{i}") for i in range(NPP)]
            with sp.Fori(0, ITERS) as it:
                for jh in range(4):
                    hb = 4 * it + jh
                    n = 2 * it + jh // 2
                    slot, half = jh % 2, jh % 2
                    if half == 0:
                        sp.wait_ge(scored, n * HK - HK + LEAD)
                        sp.dma_start(q_t[:, (jh // 2) % 2, :, :].rearrange("p h n -> p (h n)"),
                                     m.q_dram[bass.ds(n, 1), :, :].rearrange("o p n -> p (o n)")).then_inc(q_in[(jh // 2) % 2], 16)
                    sp.wait_ge(scored, hb * HALF - HALF + LEAD)
                    sp.dma_start(kg[:, slot, NPP, :, :].rearrange("p h k -> p (h k)"),
                                 m.k_dram[half, bass.ds(n, 1), :, :].rearrange("o p n -> p (o n)")).then_inc(k_in[slot], 16)
                    if half == 0:
                        sp.reg_load(regs, m.pages[0:1, bass.ds(n * NPP, NPP)])
                        batch_pages = [sp.snap(r, min_val=0, max_val=PAGES - 1) for r in regs]
                    for g, page in enumerate(batch_pages):
                        sp.dma_start(kg[:, slot, g, :, :].rearrange("p h k -> p (h k)"),
                                     t["kT"][half, bass.ds(page, 1), :, :].rearrange("o p n -> p (o n)")).then_inc(k_in[slot], 16)

            for i in range(2):
                sp.dma_start(m.wo_raw[:, i, :], t["wo"][i, :, :]).then_inc(m.wo_in[i], 16)

        @block.gpsimd
        def _(pool):
            v_rows = t["v"].rearrange("a g k n -> (a g k) n")

            def gather(hb, n, half):
                slot = half
                pool.wait_ge(summed, hb * HALF - HALF + LEAD)
                nc.gpsimd.tensor_copy(m.idx_now[:, slot, :], m.idx[:, half, bass.ds(n, 1), :].rearrange("p o k -> p (o k)")).then_inc(rows_ready, 1)
                pool.wait_ge(rows_ready, hb + 1)
                apart(pool, m)
                for k in range(KT):
                    pool.indirect_dma_start(out=vg[:, slot, k, :, :].rearrange("p h d -> p (h d)"), out_offset=None, in_=v_rows,
                                            in_offset=bass.IndirectOffsetOnAxis(ap=m.idx_now[:, slot, k:k + 1], axis=0)).then_inc(v_in[slot], 16)
                pool.dma_start(vg[0:S, slot, KT, :, :].rearrange("p h d -> p (h d)"),
                               m.v_dram[half, bass.ds(n * S, S), :]).then_inc(v_in[slot], 16)

            with pool.Fori(0, B) as n:
                for half in range(2):
                    gather(2 * n + half, n, half)

        @block.tensor
        def _(pe):
            for s in (scored, p_turned, summed):
                pe.sem_inc(s, LEAD)

            def scores(it, j):
                u, slot, h = PER * it + j, (j // HALF) % 2, j % HALF
                if j % HK == 0:
                    pe.wait_ge(q_in[(j // HK) % 2], 16 * it + 16)
                if j % HALF == 0:
                    pe.wait_ge(k_in[slot], (2 * it + j // HK) * K_DMAS + K_DMAS)
                pe.wait_ge(maxed, u + 1 - 2 + LEAD)
                lhs = q_t[:, (j // HK) % 2, j % HK, :]
                nc.tensor.matmul(scores_bank(j)[:, 0:L], lhs, kg[:, slot, 0:NPP, h, :], start=True, stop=True)
                nc.tensor.matmul(scores_bank(j)[:, L:LA], lhs, kg[:, slot, NPP, h, :], start=True, stop=True).then_inc(scored, 1)

            def turn(u, j):
                pe.wait_ge(normed, u + 1 + LEAD)
                pe.wait_ge(p_copied, u + LEAD)
                for k in range(KT):
                    nc.tensor.transpose(bank(m, 4)[:, k * P:(k + 1) * P], probs[:, j % 4, k * P:(k + 1) * P], m.ident)
                nc.tensor.transpose(bank(m, 5)[0:S, 0:P], probs[:, j % 4, L:LA], m.ident).then_inc(p_turned, 1)

            def output(it, u, j):
                slot, h = (j // HALF) % 2, j % HALF
                if j % HALF == 0:
                    pe.wait_ge(v_in[slot], (2 * it + j // HK) * V_DMAS + V_DMAS)
                pe.wait_ge(p_copied, u + 1 + LEAD)
                pe.wait_ge(stored, u + 1 - 2 + LEAD)
                for k in range(KT):
                    nc.tensor.matmul(bank(m, 6 + j % 2)[:, 0:P], vg[:, slot, k, h, :], probs_t[:, j % 2, k * P:(k + 1) * P],
                                     start=(k == 0), stop=False)
                nc.tensor.matmul(bank(m, 6 + j % 2)[:, 0:P], vg[0:S, slot, KT, h, :], probs_t[0:S, j % 2, L:L + P],
                                 start=False, stop=True).then_inc(summed, 1)

            def iteration(it, first):
                for j in range(PER):
                    scores(it, j)
                    if not (first and j < 2):
                        turn(PER * it + j - 2, (j - 2) % PER)
                    if not (first and j < 3):
                        output(it if j >= 3 else it - 1, PER * it + j - 3, (j - 3) % PER)

            iteration(0, True)
            with pe.Fori(1, ITERS) as it:
                iteration(it, False)
            output(ITERS - 1, UNITS - 3, PER - 3)
            turn(UNITS - 2, PER - 2)
            output(ITERS - 1, UNITS - 2, PER - 2)
            turn(UNITS - 1, PER - 1)
            output(ITERS - 1, UNITS - 1, PER - 1)

        @block.vector
        def _(dve):
            for s in (maxed, biased, inverted, normed):
                dve.sem_inc(s, LEAD)
            link = link_on(dve, vector_order)
            link(nc.vector.memset(mask[:, :, L:LA], 0.0))

            def normalise(u, j):
                dve.wait_ge(exped, u + 1 + LEAD)
                nc.vector.reciprocal(inv_sum[:, j % 4:j % 4 + 1], row_sum[:, j % 4:j % 4 + 1]).then_inc(inverted, 1)
                dve.wait_ge(inverted, u + 1 + LEAD)
                nc.vector.tensor_scalar(probs[:, j % 4, :], probs[:, j % 4, :], inv_sum[:, j % 4:j % 4 + 1], None,
                                        ALU.mult).then_inc(normed, 1)

            def iteration(it, first):
                link.begin(0 if first else it - 1, 2)
                for j in range(PER):
                    u = PER * it + j
                    if j % HK == 0:
                        n = 2 * it + j // HK
                        link(nc.vector.tensor_scalar(mask[:, j // HK, 0:L], m.keys, m.lens[:, bass.ds(n, 1)], NEG, ALU.is_ge, ALU.mult))
                    dve.wait_ge(scored, u + 1 + LEAD)
                    dve.wait_ge(exped, u + 1 - 2 + LEAD)
                    apart(dve, m)
                    nc.vector.tensor_tensor_reduce(out=masked[:, j % 2, :], in0=scores_bank(j), in1=mask[:, j // HK, :], scale=1.0,
                                                   scalar=-3.0e38, op0=ALU.add, op1=ALU.max,
                                                   accum_out=row_max[:, j % 4:j % 4 + 1]).then_inc(maxed, 1)
                    dve.wait_ge(maxed, u + 1 + LEAD)
                    nc.vector.tensor_scalar(bias[:, j % 4:j % 4 + 1], row_max[:, j % 4:j % 4 + 1], -SCALE, None, ALU.mult).then_inc(biased, 1)
                    if not (first and j < 1):
                        normalise(u - 1, (j - 1) % PER)

            iteration(0, True)
            link.end(1)
            with dve.Fori(1, ITERS) as it:
                iteration(it, False)
            normalise(UNITS - 1, PER - 1)

        @block.scalar
        def _(act):
            for s in (exped, p_copied, stored):
                act.sem_inc(s, LEAD)

            def exponentials(u, j):
                act.wait_ge(biased, u + 1 + LEAD)
                act.wait_ge(p_turned, u + 1 - 4 + LEAD)
                nc.scalar.activation(probs[:, j % 4, :], masked[:, j % 2, :], ACT.Exp, bias=bias[:, j % 4:j % 4 + 1], scale=SCALE,
                                     accum_out=row_sum[:, j % 4:j % 4 + 1]).then_inc(exped, 1)

            def copy_turned(u, j):
                act.wait_ge(p_turned, u + 1 + LEAD)
                act.wait_ge(summed, u + 1 - 2 + LEAD)
                nc.scalar.activation(probs_t[:, j % 2, 0:L], bank(m, 4), ACT.Copy)
                nc.scalar.activation(probs_t[0:S, j % 2, L:L + P], bank(m, 5)[0:S, 0:P], ACT.Copy).then_inc(p_copied, 1)

            def store(n, u, j):
                act.wait_ge(summed, u + 1 + LEAD)
                h = j % HK
                nc.scalar.activation(out_t[:, h * REP:(h + 1) * REP, bass.ds(n * S, S)],
                                     bank(m, 6 + j % 2)[:, 0:P].rearrange("p (g s) -> p g s", g=REP), ACT.Copy).then_inc(stored, 1)

            def iteration(it, first):
                for j in range(PER):
                    u = PER * it + j
                    exponentials(u, j)
                    if not (first and j < 2):
                        copy_turned(u - 2, (j - 2) % PER)
                    if not (first and j < 4):
                        store(2 * it + (j - 4) // HK, u - 4, (j - 4) % PER)

            iteration(0, True)
            with act.Fori(1, ITERS) as it:
                iteration(it, False)
            store(B - 1, UNITS - 4, PER - 4)
            copy_turned(UNITS - 2, PER - 2)
            store(B - 1, UNITS - 3, PER - 3)
            copy_turned(UNITS - 1, PER - 1)
            store(B - 1, UNITS - 2, PER - 2)
            store(B - 1, UNITS - 1, PER - 1)


def project_out(nc, t, m):
    sem = m.sem
    RING = 3
    scope = ExitStack()

    def parts(name, cols):
        return scope.enter_context(nc.sbuf_tensor(name, [P, RING, cols], F32))

    wo_high, wo_low, out_high, out_low = parts("wo_high", DM), parts("wo_low", DM), parts("out_high", TOK), parts("out_low", TOK)
    out_t = m.big[:, :].rearrange("p (h n) -> p h n", h=HQ)
    m.cond_t = m.big[:, 0:KT * TOK].rearrange("p (k n) -> p k n", k=KT)
    o = KT * TOK
    m.w_qkv = m.big[:, o:o + KT * 3 * DM].rearrange("p (k n) -> p k n", k=KT)
    o += KT * 3 * DM
    m.alibi = m.big[:, o:o + NH2 * S]
    o += NH2 * S
    m.x = m.big[:, o:o + TILES * DM].rearrange("p (t n) -> p t n", t=TILES)
    o += TILES * DM
    m.w_out = m.big[:, o:o + KT * DM].rearrange("p (k n) -> p k n", k=KT)
    o += KT * DM
    m.own_from = o
    FREED = -(-o // TOK)
    m.own_in = sem("own_in")
    HT = TOK // 512
    ssm_in = sem("ssm_in")
    high_ready, low_ready = sem("high_ready"), sem("low_ready")
    head_done = sem("head_done")
    cond_copied = sem("cond_copied")
    gen_v, gen_s = sem("gen_vector"), sem("gen_scalar")

    c = [m.wk[:, 32 * i:32 * i + 32] for i in range(40)]
    log_dt, log_a, a_im, c_re, c_im = c[0:5]
    dt, a_re, re, im, half_re, half_im = c[5:11]
    th, em1, sh, ch, cosm1, e_re, e_im, den, g_re, g_im = c[11:21]
    t0, t1, w_re, w_im, f1, f2, arg_s, arg_c, cnt = c[21:30]
    tab = m.wk[:, 1280:1280 + 128]
    lag_a, lag_b, quarter = tab[:, 0:SA], tab[:, SA:SA + SB2], tab[:, 64:65]
    quarter_angle = tab[:, 65:66]
    m.fac_a = m.wk[:, 1408:1408 + S * SA]
    m.fac_b = m.qb[:, 0:S * SB2]
    mag_b, ang_b, cnt_b = (m.wk[:, 1920 + 1024 * i:2944 + 1024 * i] for i in range(3))
    PEELED, PER = 8, 6
    LOOPS = (HQ - PEELED) // PER
    gen = {}
    mag_a, ang_a, cnt_a = (m.qb[:, 1024:1536], m.wk[:, 4992:5504], m.qb[:, 1536:2048])

    with scope, nc.Block() as block:
        @block.sync
        def _(sp):
            with sp.Fori(1, HQ // 2) as it:
                for i in range(2):
                    sp.wait_ge(low_ready, 2 * it + i - 2 + 1)
                    sp.dma_start(m.wo_raw[:, i, :], t["wo"][bass.ds(2 * it + i, 1), :, :].rearrange("o p n -> p (o n)")).then_inc(m.wo_in[i], 16)
            sp.wait_ge(head_done, FREED)
            sp.dma_start(m.w_qkv, t["w_qkv"]).then_inc(m.own_in, 16)
            sp.dma_start(m.alibi, t["consts"][:, C_ALIBI:C_ALIBI + NH2 * S]).then_inc(m.own_in, 16)
            sp.dma_start(m.w_out, t["w_out"]).then_inc(m.own_in, 16)
            sp.dma_start(m.x, t["x"].rearrange("(t p) n -> p t n", p=P)).then_inc(m.own_in, 16)

        @block.gpsimd
        def _(pool):
            pool.dma_start(log_dt, row_of(t["log_dt"], S)).then_inc(ssm_in, 16)
            for dst, name in ((log_a, "log_a"), (a_im, "a_imag"), (c_re, "c_re"), (c_im, "c_im")):
                pool.dma_start(dst, t[name]).then_inc(ssm_in, 16)
            pool.dma_start(tab[:, 0:SA + SB2], t["consts"][:, C_LA:C_LB + SB2]).then_inc(ssm_in, 16)
            pool.dma_start(quarter, t["consts"][:, C_QTR:C_QTR + 1]).then_inc(ssm_in, 16)

            def split(h, i, n):
                pool.wait_ge(high_ready, 2 * h + 1)
                out_row = out_t[:, bass.ds(h, 1), :].rearrange("p o n -> p (o n)")
                nc.gpsimd.tensor_tensor(exact(out_low[:, n, :]), out_row, out_high[:, n, :], ALU.subtract)
                pool.wait_ge(high_ready, 2 * h + 2)
                nc.gpsimd.tensor_tensor(exact(wo_low[:, n, :]), m.wo_raw[:, i, :], wo_high[:, n, :], ALU.subtract).then_inc(low_ready, 1)

            for h in range(PEELED):
                split(h, h % 2, h % RING)
            with pool.Fori(0, LOOPS) as it:
                for j in range(PER):
                    split(PER * it + (PEELED + j), (PEELED + j) % 2, (PEELED + j) % RING)
            pool.wait_ge(ssm_in, 16 * 7)

        @block.tensor
        def _(pe):
            def multiply(h, n, first, last):
                pe.wait_ge(low_ready, h + 1)
                for j in range(KT):
                    cols = slice(j * P, (j + 1) * P)
                    for weights, outs in ((wo_high, (out_high, out_low)), (wo_low, (out_high,))):
                        for o in outs:
                            for half in range(HT):
                                ins = nc.tensor.matmul(bank(m, j * HT + half), exact(weights[:, n, cols]),
                                                       exact(o[:, n, half * 512:(half + 1) * 512]),
                                                       start=first and weights is wo_high and o is out_high,
                                                       stop=last and weights is wo_low)
                ins.then_inc(head_done, 1)

            for h in range(PEELED):
                multiply(h, h % RING, h == 0, False)
            with pe.Fori(0, LOOPS - 1) as it:
                for j in range(PER):
                    multiply(PER * it + (PEELED + j), (PEELED + j) % RING, False, False)
            for h in range(HQ - PER, HQ):
                multiply(h, h % RING, False, h == HQ - 1)

        @block.vector
        def _(dve):
            link = link_on(dve, gen_v)
            at = gen
            tt, ts, stt = nc.vector.tensor_tensor, nc.vector.tensor_scalar, nc.vector.scalar_tensor_tensor

            def mark(name):
                at[name] = link.count()

            def per_s(x, n):
                return x.unsqueeze(2).broadcast_to([P, S, n])

            def lags(x, n):
                return x.unsqueeze(1).broadcast_to([P, S, n])

            def grid(x, n):
                return x.rearrange("p (s n) -> p s n", s=S)

            dve.wait_ge(ssm_in, 16 * 7)
            dve.wait_ge(gen_s, 2)
            link(tt(re, a_re, dt, ALU.mult))
            link(ts(re, re, -1.0, None, ALU.mult))
            link(tt(im, a_im, dt, ALU.mult))
            link(ts(half_re, re, 0.5, None, ALU.mult))
            mark("half_re")
            link(tt(grid(mag_b, SB2), per_s(re, SB2), lags(lag_b, SB2), ALU.mult))
            mark("mag_b")
            link(tt(grid(mag_a, SA), per_s(re, SA), lags(lag_a, SA), ALU.mult))
            mark("mag_a")
            link(ts(half_im, im, 0.5, None, ALU.mult))
            link(turns_off(nc, link, cnt, half_im, 0.0, arg_s, 0.0))
            mark("sh")
            link(turns_off(nc, link, cnt, half_im, 0.25, arg_c, 0.25 * TWO_PI))
            mark("ch")
            link(ts(quarter_angle, quarter, TWO_PI, None, ALU.mult))
            link(tt(grid(ang_b, SB2), per_s(im, SB2), lags(lag_b, SB2), ALU.mult))
            link(turns_off(nc, link, cnt_b, ang_b, quarter, ang_b, quarter_angle))
            mark("ang_b")
            link(tt(grid(ang_a, SA), per_s(im, SA), lags(lag_a, SA), ALU.mult))
            link(turns_off(nc, link, cnt_a, ang_a, 0.25, ang_a, 0.25 * TWO_PI))
            mark("ang_a")
            dve.wait_ge(gen_s, 7)
            link(ts(t0, th, -1.0, 1.0, ALU.mult, ALU.add))
            link(nc.vector.reciprocal(t0, t0))
            link(ts(t1, th, 2.0, None, ALU.mult))
            link(tt(em1, t1, t0, ALU.mult))
            link(tt(cosm1, sh, sh, ALU.mult))
            link(ts(cosm1, cosm1, -2.0, None, ALU.mult))
            link(ts(t0, em1, 1.0, None, ALU.add))
            link(tt(t1, cosm1, t0, ALU.mult))
            link(tt(e_re, em1, t1, ALU.add))
            link(tt(t1, sh, ch, ALU.mult))
            link(tt(t1, t1, t0, ALU.mult))
            link(ts(e_im, t1, 2.0, None, ALU.mult))
            link(tt(t0, a_re, a_re, ALU.mult))
            link(tt(t1, a_im, a_im, ALU.mult))
            link(tt(den, t0, t1, ALU.add))
            link(nc.vector.reciprocal(den, den))
            link(tt(t0, e_re, a_re, ALU.mult))
            link(tt(t1, e_im, a_im, ALU.mult))
            link(tt(g_re, t1, t0, ALU.subtract))
            link(tt(g_re, g_re, den, ALU.mult))
            link(tt(t0, e_re, a_im, ALU.mult))
            link(tt(t1, e_im, a_re, ALU.mult))
            link(tt(g_im, t0, t1, ALU.add))
            link(stt(g_im, g_im, -1.0, den, ALU.mult, ALU.mult))
            link(tt(t0, c_re, g_re, ALU.mult))
            link(tt(t1, c_im, g_im, ALU.mult))
            link(tt(w_re, t0, t1, ALU.subtract))
            link(tt(t0, c_re, g_im, ALU.mult))
            link(tt(t1, c_im, g_re, ALU.mult))
            link(tt(w_im, t0, t1, ALU.add))
            lo, hi = slice(0, SSM_N), slice(SSM_N, P)
            link(ts(f1[lo, :], w_re[lo, :], 2.0, None, ALU.mult))
            link(ts(f2[lo, :], w_im[lo, :], -2.0, None, ALU.mult))
            link(ts(f1[hi, :], w_im[hi, :], -2.0, None, ALU.mult))
            link(ts(f2[hi, :], w_re[hi, :], -2.0, None, ALU.mult))
            dve.wait_ge(gen_s, 9)
            link(tt(m.fac_b, m.fac_b, mag_b, ALU.mult))
            link(tt(grid(cnt_b[:, 0:S * SA], SA), grid(mag_a, SA), per_s(f1, SA), ALU.mult))
            link(tt(grid(ang_a, SA), per_s(im, SA), lags(lag_a, SA), ALU.mult))
            link(turns_off(nc, link, cnt_a, ang_a, 0.0, ang_a, 0.0))
            mark("ang_a2")
            dve.wait_ge(gen_s, 10)
            link(tt(grid(cnt_a, SA), grid(cnt_a, SA), per_s(f2, SA), ALU.mult))
            link(tt(cnt_b[:, 0:S * SA], cnt_b[:, 0:S * SA], cnt_a, ALU.add))
            link(tt(m.fac_a, m.fac_a, cnt_b[:, 0:S * SA], ALU.mult))
            dve.wait_ge(head_done, HQ)
            for n in range(1, KT * HT, 2):
                link(nc.vector.tensor_copy(m.cond_t[:, n // HT, (n % HT) * 512:(n % HT) * 512 + 512], bank(m, n)))

        @block.scalar
        def _(act):
            def f(n, dst, src, func):
                act.wait_ge(gen_v, n)
                nc.scalar.activation(dst, src, func).then_inc(gen_s, 1)

            def split(h, i, n, uses):
                if isinstance(h, int) and h < RING:
                    pass
                else:
                    act.wait_ge(head_done, h + 1 - RING)
                out_row = out_t[:, bass.ds(h, 1), :].rearrange("p o n -> p (o n)")
                nc.scalar.activation(exact(out_high[:, n, :]), out_row, ACT.Copy).then_inc(high_ready, 1)
                act.wait_ge(m.wo_in[i], 16 * uses)
                nc.scalar.activation(exact(wo_high[:, n, :]), m.wo_raw[:, i, :], ACT.Copy).then_inc(high_ready, 1)

            functions = [
                (),
                (("half_re", th, half_re, ACT.Tanh), ("mag_b", m.fac_b, mag_b, ACT.Exp), ("mag_a", m.fac_a, mag_a, ACT.Exp)),
                (("sh", sh, arg_s, ACT.Sin), ("ch", ch, arg_c, ACT.Sin)),
                (),
                (("ang_b", mag_b, ang_b, ACT.Sin),),
                (("ang_a", mag_a, ang_a, ACT.Sin),),
                (),
                (("ang_a2", cnt_a, ang_a, ACT.Sin),),
            ]
            split(0, 0, 0, 1)
            act.wait_ge(ssm_in, 16 * 7)
            nc.scalar.activation(dt, log_dt, ACT.Exp).then_inc(gen_s, 1)
            nc.scalar.activation(a_re, log_a, ACT.Exp).then_inc(gen_s, 1)
            for h in range(PEELED):
                if h:
                    split(h, h % 2, h % RING, h // 2 + 1)
                for name, dst, src, func in functions[h]:
                    f(gen[name], dst, src, func)
            with act.Fori(0, LOOPS) as it:
                for j in range(PER):
                    split(PER * it + (PEELED + j), (PEELED + j) % 2, (PEELED + j) % RING, PER // 2 * it + ((PEELED + j) // 2 + 1))
            act.wait_ge(head_done, HQ)
            for n in range(0, KT * HT, 2):
                nc.scalar.activation(m.cond_t[:, n // HT, (n % HT) * 512:(n % HT) * 512 + 512], bank(m, n), ACT.Copy).then_inc(cond_copied, 1)
            act.wait_ge(cond_copied, KT * HT // 2)


def toeplitz(sp, m, s, slot):
    src = bass.AP(m.lag_dram.tensor, s * (L + P), [[1, P], [1, L]])
    sp.dma_start(m.toep[:, slot, :], src).then_inc(m.toep_in[slot], 16)


def attend_own(nc, t, m):
    sem = m.sem
    o = m.own_from
    region = {}
    for name, cols in (("ct", DM), ("qkv", 3 * DM), ("norm", 2 * DM), ("qT", DM), ("kT", DM), ("keys", 4 * 8 * P),
                       ("vals", 4 * 8 * 64), ("aT", DM), ("um", DM), ("umT", KT * TOK)):
        region[name] = m.big[:, o:o + cols]
        o += cols
    soft, pexp, p_t = (m.kv[:, KT * (DM + RL) + 2 * DM + EXP + i * NH2 * S:][:, 0:NH2 * S] for i in range(3))
    assert o <= HQ * TOK
    alibi = m.alibi.rearrange("p (h k) -> p h k", h=NH2)
    m.toep = m.big[:, 0:TOEP * L].rearrange("p (s n) -> p s n", s=TOEP)
    m.toep_in = [sem(f"toep_in{i}") for i in range(TOEP)]
    m.ffn_in = sem("ffn_in")
    m.y_t = region["keys"].rearrange("p (k n) -> p k n", k=KT)
    o = 0
    m.w_base = m.kv[:, o:o + KT * DM].rearrange("p (k n) -> p k n", k=KT); o += KT * DM
    m.w_rl = m.kv[:, o:o + KT * RL].rearrange("p (k n) -> p k n", k=KT); o += KT * RL
    m.lora_b = m.kv[:, o:o + DM]; o += DM
    m.b_base = m.kv[:, o:o + DM]; o += DM
    m.b_router = m.kv[:, o:o + EXP]
    m.um_t = region["umT"].rearrange("p (k n) -> p k n", k=KT)
    ct = region["ct"].rearrange("p (k n) -> p k n", k=KT)
    qkv = region["qkv"].rearrange("p (c n) -> p c n", c=3)
    norm = region["norm"].rearrange("p (c n) -> p c n", c=2)
    q_t, k_t = (region[n].rearrange("p (k n) -> p k n", k=KT) for n in ("qT", "kT"))
    key_blocks = region["keys"].rearrange("p (k b h n) -> p k b h n", k=KT, b=BPT, h=8)
    val_blocks = region["vals"].rearrange("p (b g h d) -> p b g h d", b=BPT, g=8, h=4)
    a_t = region["aT"].rearrange("p (k n) -> p k n", k=KT)
    w_out = m.w_out
    um = region["um"]
    o = 0
    def cols(n):
        nonlocal o
        o += n
        return m.wk[:, 2048 + o - n:2048 + o]
    stats, mv, var, std, rstd, hmax, hsum, hinv = cols(12), cols(4), cols(2), cols(2), cols(2), cols(NH2), cols(NH2), cols(NH2)
    head_mask, ln, eps = cols(8), cols(4 * KT), cols(1)
    ln = ln.rearrange("p (w k) -> p w k", w=4)
    stats = stats.rearrange("p (c n) -> p c n", c=2)
    lags = cols(S * SB2)
    skip, last_row = cols(S), cols(1)
    zero = cols(P)

    parts_in = sem("parts_in4")
    lag_ready, lag_out, zeroed = sem("lag_ready"), sem("lag_out"), sem("zeroed")
    lag_made = sem("lag_made")
    vector_order, scalar_order, pool_order = sem("vector_order4"), sem("scalar_order4"), sem("pool_order4")
    tile_in = sem("tile_in")
    made = sem("made")
    clipped = sem("clipped")
    var_ready, std_ready = sem("var_ready"), sem("std_ready")
    normed = sem("ln_normed")
    qk_turned = sem("qk_turned")
    q_scaled, k_scaled = sem("q_scaled"), sem("k_scaled")
    blocks_v, blocks_p = sem("key_blocks_v"), sem("key_blocks_p")
    vals_ready = sem("vals_ready")
    scored = sem("scored4")
    shifted = sem("shifted")
    exped = sem("exped4")
    probs_ready = sem("probs_ready")
    p_turned, p_copied = sem("p_turned4"), sem("p_copied4")
    attended, att_copied = sem("attended"), sem("att_copied")
    out_ready, x_ready = sem("out_ready4"), sem("x_ready")
    masked = sem("um_masked")
    um_turned, um_copied = sem("um_turned"), sem("um_copied")
    PARTS = 16 * 4
    DVE_BLOCKS = 4
    QKV, SC, TR, AO = 0, 3, 5, 7

    with nc.Block() as block:
        @block.sync
        def _(sp):
            sp.dma_start(head_mask, t["consts"][:, C_HM:C_HM + 8]).then_inc(parts_in, 16)
            sp.dma_start(ln.rearrange("p w k -> p (w k)"), t["ln"].rearrange("p w k -> p (w k)")).then_inc(parts_in, 16)
            sp.dma_start(skip, row_of(t["d_skip"], S)).then_inc(parts_in, 16)
            sp.dma_start(last_row, t["consts"][:, C_LAST:C_LAST + 1]).then_inc(parts_in, 16)
            sp.wait_ge(lag_made, 1)
            sp.dma_start(m.lag_dram[:, 0:L].rearrange("s (a b) -> a s b", a=SA), lags[0:SA, :].rearrange("p (s b) -> p s b", s=S)).then_inc(lag_out, 16)
            sp.dma_start(m.lag_dram[:, L:L + P], zero[0:S, :]).then_inc(lag_out, 16)
            for dst, src in ((m.w_base, t["w_base"]), (m.w_rl, t["w_rl"]), (m.lora_b, t["lora_b"]),
                             (m.b_base, row_of(t["b_base"], DM)), (m.b_router, row_of(t["b_router"], EXP))):
                sp.dma_start(dst, src).then_inc(m.ffn_in, 16)
            sp.wait_ge(lag_out, 32)
            sp.wait_ge(made, 3 * TILES + LEAD)
            for i in range(TOEP):
                toeplitz(sp, m, i, i)

        @block.gpsimd
        def _(pool):
            pool.sem_inc(tile_in, LEAD)
            pool.sem_inc(blocks_p, LEAD)
            pool.wait_ge(parts_in, PARTS)

            def hidden(tile):
                pool.wait_ge(made, 3 * tile + LEAD)
                nc.gpsimd.tensor_copy(ct, m.cond_t[:, :, bass.ds(tile * P, P)]).then_inc(tile_in, 1)

            def blocks(tile):
                pool.wait_ge(k_scaled, tile + 1 + LEAD)
                pool.wait_ge(scored, tile + LEAD)
                apart(pool, m)
                for h in range(DVE_BLOCKS, 8):
                    ins = nc.gpsimd.tensor_scalar(key_blocks[:, :, :, h, :], k_t.rearrange("p k (b n) -> p k b n", b=BPT),
                                                  head_mask[:, h:h + 1], 1.0, ALU.mult, ALU.mult)
                ins.then_inc(blocks_p, 1)

            hidden(0)
            with pool.Fori(0, TILES - 1) as tile:
                hidden(tile + 1)
                blocks(tile)
            blocks(TILES - 1)

        @block.tensor
        def _(pe):
            for s in (made, qk_turned, scored, p_turned, attended, out_ready, um_turned):
                pe.sem_inc(s, LEAD)
            for s in range(S):
                ins = nc.tensor.matmul(bank(m, QKV + 3 + s // 16)[0:SA, (s % 16) * SB2:(s % 16 + 1) * SB2],
                                       m.fac_a[:, s * SA:(s + 1) * SA], m.fac_b[:, s * SB2:(s + 1) * SB2], start=True, stop=True)
            ins.then_inc(lag_ready, 1)
            pe.wait_ge(parts_in, PARTS)
            pe.wait_ge(m.own_in, 16 * 4)

            def project(tile, parts):
                pe.wait_ge(tile_in, tile + 1 + LEAD)
                for c in parts:
                    pe.wait_ge(clipped, 3 * tile + c + 1 - 3 + LEAD)
                    for k in range(KT):
                        ins = nc.tensor.matmul(bank(m, QKV + c), ct[:, k, :], m.w_qkv[:, k, c * DM:(c + 1) * DM],
                                               start=(k == 0), stop=(k == KT - 1))
                    ins.then_inc(made, 1)

            def turn_qk(tile):
                pe.wait_ge(normed, 2 * tile + 2 + LEAD)
                pe.wait_ge(p_copied, tile + LEAD)
                for c in range(2):
                    for k in range(KT):
                        ins = nc.tensor.transpose(bank(m, TR + c)[:, k * P:(k + 1) * P], norm[:, c, k * P:(k + 1) * P], m.ident)
                ins.then_inc(qk_turned, 1)

            def score(tile):
                pe.wait_ge(q_scaled, tile + 1 + LEAD)
                pe.wait_ge(blocks_v, tile + 1 + LEAD)
                pe.wait_ge(blocks_p, tile + 1 + LEAD)
                pe.wait_ge(shifted, tile + LEAD)
                for b in range(BPT):
                    for k in range(KT):
                        ins = nc.tensor.matmul(bank(m, SC + k // 2)[b * S:(b + 1) * S, (k % 2) * 256:(k % 2) * 256 + 256],
                                               q_t[:, k, b * S:(b + 1) * S], key_blocks[:, k, b, :, :], start=True, stop=True,
                                               skip_group_check=True)
                ins.then_inc(scored, 1)

            def turn_probs(tile):
                pe.wait_ge(probs_ready, tile + 1 + LEAD)
                for g in range(8):
                    ins = nc.tensor.transpose(bank(m, TR + g // 4)[:, (g % 4) * P:(g % 4 + 1) * P], pexp[:, g * P:(g + 1) * P], m.ident)
                ins.then_inc(p_turned, 1)

            def attend(tile):
                pe.wait_ge(p_copied, tile + 1 + LEAD)
                pe.wait_ge(vals_ready, tile + 1 + LEAD)
                pe.wait_ge(um_copied, tile + LEAD)
                for b in range(BPT):
                    for g in range(8):
                        r = 64 * (g % 2)
                        ins = nc.tensor.matmul(bank(m, AO)[r:r + 64, (g // 2) * P + b * S:(g // 2) * P + (b + 1) * S],
                                               val_blocks[:, b, g, :, :].rearrange("p h d -> p (h d)"),
                                               p_t[:, g * P + b * S:g * P + (b + 1) * S], start=True, stop=True, skip_group_check=True)
                ins.then_inc(attended, 1)

            def output(tile):
                pe.wait_ge(att_copied, tile + 1 + LEAD)
                for k in range(KT):
                    ins = nc.tensor.matmul(bank(m, AO), a_t[:, k, :], w_out[:, k, :], start=(k == 0), stop=(k == KT - 1))
                ins.then_inc(out_ready, 1)

            def turn_um(tile):
                pe.wait_ge(masked, tile + 1 + LEAD)
                for k in range(KT):
                    ins = nc.tensor.transpose(bank(m, AO)[:, k * P:(k + 1) * P], um[:, k * P:(k + 1) * P], m.ident)
                ins.then_inc(um_turned, 1)

            pe.wait_ge(lag_made, 1)
            project(0, range(3))
            turn_qk(0)
            score(0)
            with pe.Fori(0, TILES - 1) as tile:
                project(tile + 1, (0, 1))
                turn_probs(tile)
                project(tile + 1, (2,))
                attend(tile)
                turn_qk(tile + 1)
                output(tile)
                score(tile + 1)
                turn_um(tile)
            turn_probs(TILES - 1)
            attend(TILES - 1)
            output(TILES - 1)
            turn_um(TILES - 1)

        @block.scalar
        def _(act):
            for s in (std_ready, q_scaled, exped, p_copied, vals_ready, um_copied):
                act.sem_inc(s, LEAD)
            link = link_on(act, scalar_order)
            act.wait_ge(parts_in, PARTS)
            act.wait_ge(m.own_in, 16 * 4)
            act.wait_ge(zeroed, 1)

            def roots(tile):
                act.wait_ge(var_ready, tile + 1 + LEAD)
                nc.scalar.activation(std, var, ACT.Sqrt).then_inc(std_ready, 1)

            def values(tile):
                act.wait_ge(clipped, 3 * tile + 3 + LEAD)
                act.wait_ge(attended, tile + LEAD)
                for b in range(BPT):
                    for h in range(4):
                        src = qkv[b * S:(b + 1) * S, 2, :].rearrange("p (g h d) -> p g h d", g=8, h=4)[:, :, h, :]
                        ins = nc.scalar.activation(val_blocks[h * S:(h + 1) * S, b, :, h, :], src, ACT.Copy)
                ins.then_inc(vals_ready, 1)

            def scale_queries(tile):
                act.wait_ge(qk_turned, tile + 1 + LEAD)
                act.wait_ge(scored, tile + LEAD)
                for k in range(KT):
                    ins = nc.scalar.activation(q_t[:, k, :], bank(m, TR)[:, k * P:(k + 1) * P], ACT.Identity,
                                               scale=ln[:, 0, k:k + 1], bias=ln[:, 1, k:k + 1])
                ins.then_inc(q_scaled, 1)

            def exponentials(tile):
                act.wait_ge(shifted, tile + 1 + LEAD)
                nc.scalar.activation(pexp, soft, ACT.Exp).then_inc(exped, 1)

            def copy_probs(tile):
                act.wait_ge(p_turned, tile + 1 + LEAD)
                nc.scalar.activation(p_t[:, 0:512], bank(m, TR), ACT.Copy)
                nc.scalar.activation(p_t[:, 512:1024], bank(m, TR + 1), ACT.Copy).then_inc(p_copied, 1)

            def copy_attended(tile):
                act.wait_ge(attended, tile + 1 + LEAD)
                nc.scalar.activation(a_t.rearrange("p k n -> p (k n)"), bank(m, AO), ACT.Copy).then_inc(att_copied, 1)

            def copy_um(tile):
                act.wait_ge(um_turned, tile + 1 + LEAD)
                nc.scalar.activation(m.um_t[:, :, bass.ds(tile * P, P)], bank(m, AO).rearrange("p (k n) -> p k n", k=KT), ACT.Copy).then_inc(um_copied, 1)

            roots(0)
            scale_queries(0)
            values(0)
            exponentials(0)
            with act.Fori(0, TILES - 1) as tile:
                copy_probs(tile)
                roots(tile + 1)
                copy_attended(tile)
                scale_queries(tile + 1)
                values(tile + 1)
                copy_um(tile)
                exponentials(tile + 1)
            copy_probs(TILES - 1)
            copy_attended(TILES - 1)
            copy_um(TILES - 1)

        @block.vector
        def _(dve):
            for s in (clipped, var_ready, normed, k_scaled, blocks_v, shifted, probs_ready, att_copied, x_ready, masked):
                dve.sem_inc(s, LEAD)
            tt, ts = nc.vector.tensor_tensor, nc.vector.tensor_scalar
            link = link_on(dve, vector_order)
            nc.vector.memset(region["vals"], 0.0).then_inc(zeroed, 1)
            dve.wait_ge(parts_in, PARTS)
            dve.wait_ge(m.own_in, 16 * 4)
            link(nc.vector.memset(zero, 0.0))
            dve.wait_ge(lag_ready, 1)
            for i in range(2):
                link(nc.vector.tensor_copy(lags[0:SA, i * 512:(i + 1) * 512], bank(m, 3 + i)[0:SA, :]))
            lag0 = lags[0:SA, :].rearrange("p (s b) -> p s b", s=S)[:, :, SB2 - 1]
            nc.vector.scalar_tensor_tensor(lag0, skip[0:SA, :], last_row[0:SA, :], lag0, ALU.mult, ALU.add).then_inc(lag_made, 1)

            def clip(tile, c):
                dve.wait_ge(made, 3 * tile + c + 1 + LEAD)
                if c == 2:
                    dve.wait_ge(vals_ready, tile + LEAD)
                ts(qkv[:, c, :], bank(m, QKV + c), CLIP, -CLIP, ALU.min, ALU.max).then_inc(clipped, 1)

            def layer_norm(tile):
                dve.wait_ge(clipped, 3 * tile + 2 + LEAD)
                nc.vector.bn_stats(stats[:, 0, :], qkv[:, 0, :])
                link(nc.vector.bn_stats(stats[:, 1, :], qkv[:, 1, :]))
                apart(dve, m)
                nc.vector.bn_aggr(mv[:, 0:2], stats[:, 0, :])
                link(nc.vector.bn_aggr(mv[:, 2:4], stats[:, 1, :]))
                apart(dve, m)
                ts(var, mv.rearrange("p (c n) -> p c n", c=2)[:, :, 1], EPS_LN, None, ALU.add).then_inc(var_ready, 1)
                dve.wait_ge(std_ready, tile + 1 + LEAD)
                link(nc.vector.reciprocal(rstd, std))
                dve.wait_ge(qk_turned, tile + LEAD)
                for c in range(2):
                    ts(norm[:, c, :], qkv[:, c, :], mv[:, 2 * c:2 * c + 1], rstd[:, c:c + 1], ALU.subtract, ALU.mult).then_inc(normed, 1)

            def scale_keys(tile):
                dve.wait_ge(qk_turned, tile + 1 + LEAD)
                dve.wait_ge(blocks_p, tile + LEAD)
                for k in range(KT):
                    ins = ts(k_t[:, k, :], bank(m, TR + 1)[:, k * P:(k + 1) * P], ln[:, 2, k:k + 1], ln[:, 3, k:k + 1], ALU.mult, ALU.add)
                ins.then_inc(k_scaled, 1)
                dve.wait_ge(k_scaled, tile + 1 + LEAD)
                dve.wait_ge(scored, tile + LEAD)
                for h in range(DVE_BLOCKS):
                    ins = ts(key_blocks[:, :, :, h, :], k_t.rearrange("p k (b n) -> p k b n", b=BPT), head_mask[:, h:h + 1], None, ALU.mult)
                ins.then_inc(blocks_v, 1)

            s3 = soft.rearrange("p (h k) -> p h k", h=NH2)
            e3 = pexp.rearrange("p (h k) -> p h k", h=NH2)

            def shift(tile):
                dve.wait_ge(scored, tile + 1 + LEAD)
                for i in range(2):
                    half = slice(i * 512, (i + 1) * 512)
                    ins = nc.vector.scalar_tensor_tensor(soft[:, half], bank(m, SC + i), SCALE2, m.alibi[:, half], ALU.mult, ALU.add)
                link(ins)
                link(nc.vector.tensor_reduce(hmax, s3, AX.X, ALU.max))
                tt(s3, s3, hmax.unsqueeze(2).broadcast_to([P, NH2, S]), ALU.subtract).then_inc(shifted, 1)

            def normalise(tile):
                dve.wait_ge(exped, tile + 1 + LEAD)
                link(nc.vector.tensor_reduce(hsum, e3, AX.X, ALU.add))
                link(nc.vector.reciprocal(hinv, hsum))
                tt(e3, e3, hinv.unsqueeze(2).broadcast_to([P, NH2, S]), ALU.mult).then_inc(probs_ready, 1)

            def residual(tile):
                dve.wait_ge(out_ready, tile + 1 + LEAD)
                row = m.x[:, bass.ds(tile, 1), :].rearrange("p o n -> p (o n)")
                link(tt(row, row, bank(m, AO), ALU.add))
                nc.vector.scalar_tensor_tensor(um, m.keys, m.lens2_rows[:, bass.ds(tile, 1)], row, ALU.is_lt, ALU.mult).then_inc(masked, 1)

            clip(0, 0)
            clip(0, 1)
            layer_norm(0)
            clip(0, 2)
            scale_keys(0)
            shift(0)
            with dve.Fori(0, TILES - 1) as tile:
                link.begin(tile, 8)
                clip(tile + 1, 0)
                normalise(tile)
                clip(tile + 1, 1)
                layer_norm(tile + 1)
                clip(tile + 1, 2)
                scale_keys(tile + 1)
                residual(tile)
                shift(tile + 1)
            link.end(TILES - 1)
            normalise(TILES - 1)
            residual(TILES - 1)


def convolve(nc, t, m):
    sem = m.sem
    RING = 8
    rev = m.wk[:, 0:KT]
    mask = m.wk[:, 128:128 + KT * B].rearrange("p (k b) -> p k b", k=KT)
    rev_in = sem("rev_in")
    convolved, copied, order = sem("convolved"), sem("conv_copied"), sem("vector_order5")
    u_t = m.um_t.rearrange("p k (b s) -> p k b s", b=B)
    y_t = m.y_t.rearrange("p k (b s) -> p k b s", b=B)

    with nc.Block() as block:
        @block.sync
        def _(sp):
            sp.dma_start(rev, t["consts"][:, C_REV:C_REV + KT]).then_inc(rev_in, 16)
            for i in range(S - TOEP):
                sp.wait_ge(convolved, i + 1)
                toeplitz(sp, m, TOEP + i, i)

        @block.tensor
        def _(pe):
            with pe.Fori(0, S // TOEP) as it:
                for i in range(TOEP):
                    s = TOEP * it + i
                    pe.wait_ge(m.toep_in[i], 16 * it + 16)
                    pe.wait_ge(copied, s + 1 - RING + LEAD)
                    for d in range(KT):
                        ins = nc.tensor.matmul(bank(m, i % RING)[:, d * B:KT * B], m.toep[:, i, L - (d + 1) * P:L - d * P],
                                               u_t[:, 0:KT - d, :, bass.ds(s, 1)].rearrange("p k b o -> p k (b o)"),
                                               start=(d == 0), stop=(d == KT - 1), skip_group_check=True)
                    ins.then_inc(convolved, 1)

        @block.vector
        def _(dve):
            dve.sem_inc(copied, LEAD)
            link = link_on(dve, order)
            dve.wait_ge(rev_in, 16)
            link(nc.vector.tensor_tensor(mask, rev.unsqueeze(2).broadcast_to([P, KT, B]), m.lens2.unsqueeze(1).broadcast_to([P, KT, B]), ALU.is_lt))
            with dve.Fori(0, S // RING) as it:
                for i in range(RING):
                    s = RING * it + i
                    dve.wait_ge(convolved, s + 1)
                    nc.vector.tensor_tensor(y_t[:, :, :, bass.ds(s, 1)].rearrange("p k b o -> p k (b o)"),
                                            bank(m, i)[:, 0:KT * B].rearrange("p (k b) -> p k b", k=KT), mask, ALU.mult).then_inc(copied, 1)
            dve.wait_ge(copied, S + LEAD)


def feed_forward(nc, t, m):
    sem = m.sem
    o = 0
    def cols(n, slots=2):
        nonlocal o
        o += n * slots
        return m.wk[:, o - n * slots:o].rearrange("p (s n) -> p s n", s=slots)
    y_tile, rest, lora_t = cols(DM), cols(DM), cols(P)
    lora_w = cols(P)
    logits, tau, weights = cols(EXP), cols(2), cols(EXP)
    pairs, pair_sums, count, sums, taus = cols(EXP * EXP), cols(EXP * EXP), cols(EXP), cols(EXP), cols(EXP)
    result = m.qb[:, 0:2 * DM].rearrange("p (s n) -> p s n", s=2)
    order = sem("vector_order6")
    tile_ready = sem("y_tile_ready")
    routed, based = sem("routed"), sem("based")
    weighted = sem("weighted")
    l_turned, l_copied, summed = sem("l_turned"), sem("l_copied"), sem("summed6")
    finished = sem("finished")
    out_done = [sem("out_done0"), sem("out_done1")]

    with nc.Block() as block:
        @block.scalar
        def _(act):
            for s in (tile_ready, l_copied):
                act.sem_inc(s, LEAD)

            def fetch(tile, j):
                act.wait_ge(based, tile + 1 - 2 + LEAD)
                nc.scalar.activation(y_tile[:, j, :].rearrange("p (k n) -> p k n", k=KT), m.y_t[:, :, bass.ds(tile * P, P)], ACT.Copy).then_inc(tile_ready, 1)

            def lora(tile, j):
                act.wait_ge(l_turned, tile + 1 + LEAD)
                act.wait_ge(summed, tile + 1 - 2 + LEAD)
                nc.scalar.activation(lora_t[:, j, :], bank(m, 6 + j)[:, 0:P], ACT.Copy).then_inc(l_copied, 1)

            def iteration(it, last):
                fetch(2 * it + 1, 1)
                lora(2 * it, 0)
                lora(2 * it + 1, 1)
                if not last:
                    fetch(2 * it + 2, 0)

            fetch(0, 0)
            with act.Fori(0, TILES // 2 - 1) as it:
                iteration(it, False)
            iteration(TILES // 2 - 1, True)

        @block.tensor
        def _(pe):
            for s in (routed, based, l_turned, summed):
                pe.sem_inc(s, LEAD)

            def route(tile, j):
                pe.wait_ge(tile_ready, tile + 1 + LEAD)
                pe.wait_ge(finished, tile + 1 - 2 + LEAD)
                for k in range(KT):
                    ins = nc.tensor.matmul(bank(m, 4 + j)[:, 0:RL], y_tile[:, j, k * P:(k + 1) * P], m.w_rl[:, k, :],
                                           start=(k == 0), stop=(k == KT - 1))
                ins.then_inc(routed, 1)

            def base(tile, j):
                for k in range(KT):
                    ins = nc.tensor.matmul(bank(m, 2 * j), y_tile[:, j, k * P:(k + 1) * P], m.w_base[:, k, :], start=(k == 0), stop=False)
                ins.then_inc(based, 1)

            def turn(tile, j):
                pe.wait_ge(weighted, tile + 1 + LEAD)
                nc.tensor.transpose(bank(m, 6 + j)[:, 0:P], lora_w[:, j, :], m.ident).then_inc(l_turned, 1)

            def lora(tile, j):
                pe.wait_ge(l_copied, tile + 1 + LEAD)
                nc.tensor.matmul(bank(m, 2 * j), lora_t[:, j, :], m.lora_b, start=False, stop=True).then_inc(summed, 1)

            def iteration(it, last):
                for j in range(2):
                    tile = 2 * it + j
                    base(tile, j)
                    turn(tile, j)
                    if not (last and j == 1):
                        route(tile + 1, 1 - j)
                    lora(tile, j)

            pe.wait_ge(m.ffn_in, 16 * 5)
            route(0, 0)
            with pe.Fori(0, TILES // 2 - 1) as it:
                iteration(it, False)
            iteration(TILES // 2 - 1, True)

        @block.vector
        def _(dve):
            for s in (weighted, finished):
                dve.sem_inc(s, LEAD)
            tt, ts = nc.vector.tensor_tensor, nc.vector.tensor_scalar
            link = link_on(dve, order)
            dve.wait_ge(m.ffn_in, 16 * 5)
            with dve.Fori(0, TILES // 2) as it:
                link.begin(it, 2 * 9)
                for j in range(2):
                    tile = 2 * it + j
                    dve.wait_ge(routed, tile + 1 + LEAD)
                    z, w = logits[:, j, :], weights[:, j, :]
                    pair = pairs[:, j, :].rearrange("p (i k) -> p i k", i=EXP)
                    psum_ = pair_sums[:, j, :].rearrange("p (i k) -> p i k", i=EXP)
                    link(tt(z, bank(m, 4 + j)[:, 0:EXP], m.b_router, ALU.add))
                    zk, zi = z.unsqueeze(1).broadcast_to([P, EXP, EXP]), z.unsqueeze(2).broadcast_to([P, EXP, EXP])
                    link(tt(pair, zk, zi, ALU.is_ge))
                    tt(psum_, pair, zk, ALU.mult)
                    link(nc.vector.tensor_reduce(count[:, j, :], pair, AX.X, ALU.add))
                    link(nc.vector.tensor_reduce(sums[:, j, :], psum_, AX.X, ALU.add))
                    link(nc.vector.reciprocal(count[:, j, :], count[:, j, :]))
                    link(nc.vector.scalar_tensor_tensor(taus[:, j, :], sums[:, j, :], -1.0, count[:, j, :], ALU.add, ALU.mult))
                    link(nc.vector.tensor_reduce(tau[:, j, 0:1], taus[:, j, :], AX.X, ALU.max))
                    link(ts(w, z, tau[:, j, 0:1], 0.0, ALU.subtract, ALU.max))
                    tt(lora_w[:, j, :].rearrange("p (e r) -> p e r", e=EXP), bank(m, 4 + j)[:, EXP:RL].rearrange("p (e r) -> p e r", e=EXP),
                       w.unsqueeze(2).broadcast_to([P, EXP, RANK]), ALU.mult).then_inc(weighted, 1)
                    row = m.x[:, bass.ds(tile, 1), :].rearrange("p o n -> p (o n)")
                    link(tt(rest[:, j, :], row, m.b_base, ALU.add))
                    dve.wait_ge(summed, tile + 1 + LEAD)
                    dve.wait_ge(out_done[j], 16 * it + 16)
                    tt(result[:, j, :], rest[:, j, :], bank(m, 2 * j), ALU.add).then_inc(finished, 1)
            link.end(TILES // 2)

        @block.sync
        def _(sp):
            for s in out_done:
                sp.sem_inc(s, 16)
            with sp.Fori(0, TILES // 2) as it:
                for j in range(2):
                    sp.wait_ge(finished, 2 * it + j + 1 + LEAD)
                    sp.dma_start(t["out"][bass.ds((2 * it + j) * P, P), :], result[:, j, :]).then_inc(out_done[j], 16)
            for s in out_done:
                sp.wait_ge(s, 16 * (TILES // 2) + 16)


def layouts(i):
    def kt(w):
        return w.reshape(w.shape[0], KT, P).transpose(2, 1, 0)

    x = i["x"].reshape(TOK, DM)
    back = i["L0_ffn_W_base"][:, :].reshape(DM, KT, P)[:, :, ::-1].transpose(2, 1, 0)
    router = i["L0_ffn_W_router"].reshape(EXP, KT, P)[:, :, ::-1].transpose(2, 1, 0)
    lora = i["L0_ffn_lora_A"].transpose(0, 2, 1).reshape(ER, KT, P)[:, :, ::-1].transpose(2, 1, 0)
    twice = lambda a: np.concatenate([a, a], 0)
    return {
        "x": x,
        "xT": x.reshape(TILES, P, KT, P).transpose(0, 3, 2, 1).reshape(TILES, P, DM),
        "table": i["itok_Bx16_0_63"], "lens": i["itok_B_207_1644"], "lens2": i["itok_B_8_3872"],
        "w1": kt(np.concatenate([i["L0_cond_Wv"], i["L0_cond_Wq"], i["L0_cond_Wk"]], 0)).reshape(P, KT, -1, 512)
              .transpose(2, 0, 1, 3).reshape(-1, P, KT * 512),
        "q_norm": i["L0_cond_q_norm_w"], "k_norm": i["L0_cond_k_norm_w"],
        "kT": i["L0_cond_k_cache"].reshape(PAGES, PSIZE, 2, HALF, D).transpose(2, 0, 4, 3, 1).reshape(2, PAGES, D, HALF * PSIZE),
        "v": i["L0_cond_v_cache"].reshape(PAGES, PSIZE, 2, HALF * D).transpose(2, 0, 1, 3),
        "wo": i["L0_cond_Wo"].reshape(DM, HQ, D).transpose(1, 2, 0),
        "w_qkv": kt(i["L0_attn_w_qkv"]), "w_out": kt(i["L0_attn_w_out"]),
        "ln": np.stack([i["L0_attn_" + n].reshape(KT, P).T for n in ("q_ln_w", "q_ln_b", "k_ln_w", "k_ln_b")], 1),
        "log_dt": i["L0_cond2_log_dt"], "log_a": twice(i["L0_cond2_log_A_real"].T), "a_imag": twice(i["L0_cond2_A_imag"].T),
        "c_re": twice(i["L0_cond2_C"][:, :, 0].T), "c_im": twice(i["L0_cond2_C"][:, :, 1].T), "d_skip": i["L0_cond2_D"],
        "w_base": back, "b_base": i["L0_ffn_b_base"], "w_rl": np.concatenate([router, lora], 2),
        "b_router": i["L0_ffn_b_router"], "lora_b": i["L0_ffn_lora_B"].reshape(ER, DM),
        "consts": constants(),
    }


def kernel(**inputs):
    import concourse.bacc as _bacc
    from concourse.bass_utils import run_bass_kernel_spmd as _run

    nc = _bacc.Bacc("TRN2", target_bir_lowering=False, num_devices=1)
    arrays = {n: np.ascontiguousarray(a) for n, a in layouts({n: np.asarray(a) for n, a in inputs.items()}).items()}
    t = {n: nc.dram_tensor("in_" + n, a.shape, mybir.dt.from_np(a.dtype), kind="ExternalInput").ap() for n, a in arrays.items()}
    t["out"] = nc.dram_tensor("out_x", [TOK, DM], F32, kind="ExternalOutput").ap()
    build(nc, t)
    r = _run(nc, [{"in_" + n: a for n, a in arrays.items()}], core_ids=[0])
    return r.results[0]["out_x"].reshape(B, S, DM)
```

```python
import numpy as np
from contextlib import ExitStack

import concourse.bass as bass
from concourse import mybir

F32 = mybir.dt.float32
I32 = mybir.dt.int32
F32R = mybir.dt.float32r
ALU = mybir.AluOpType
ACT = mybir.ActivationFunctionType
AX = mybir.AxisListType

P = 128
B, S, DM = 32, 32, 512
TOK = B * S
TILES = TOK // P
BPT = P // S
KT = DM // P
HQ, HK, D = 32, 8, 128
REP = HQ // HK
PAGES, PSIZE, NPP = 64, 32, 16
L = NPP * PSIZE
LA = L + S
HALF = HK // 2
THETA = 10000.0
EPS_RMS = 1e-6
SCALE = 1.0 / float(np.sqrt(D))
NH2, HD2 = 32, 16
SCALE2 = HD2 ** -0.5
EPS_LN = 1e-5
CLIP = 8.0
NEG = -1e30
SSM_N = 64
SA, SB2 = 16, 32
TOEP = 16
EXP, RANK = 8, 16
ER = EXP * RANK
RL = EXP + ER

TWO_PI = 2.0 * np.pi
PI_A = 6.28125
PI_B = float(np.float32(np.round((TWO_PI - PI_A) * 2**20) / 2**20))
PI_C = float(np.float32(TWO_PI - PI_A - PI_B))
MAGIC = 1.5 * 2.0**23
LEAD = 16
PI_LOW = 3.1415925

C_ID = 0
C_KEY = C_ID + P
C_ALIBI = C_KEY + L
C_HM = C_ALIBI + NH2 * S
C_FREQ = C_HM + 8
C_LA = C_FREQ + D // 2
C_LB = C_LA + SA
C_REV = C_LB + SB2
C_S = C_REV + KT
C_QTR = C_S + 1
C_LAST = C_QTR + 1
C_END = C_LAST + 1


def constants():
    c = np.zeros((P, C_END), np.float32)
    p = np.arange(P)
    c[:, C_ID:C_ID + P] = np.eye(P)
    c[:, C_KEY:C_KEY + L] = np.arange(L)
    slopes = 1.0 / np.power(2.0, np.arange(1, NH2 + 1, dtype=np.float32) * np.float32(8 / NH2))
    rel = np.arange(S)[None, :] - (p % S)[:, None]
    bias = slopes[None, :, None].astype(np.float32) * rel[:, None, :].astype(np.float32)
    c[:, C_ALIBI:C_ALIBI + NH2 * S] = np.where(rel[:, None, :] <= 0, bias, NEG).reshape(P, -1)
    c[:, C_HM:C_HM + 8] = (p[:, None] // HD2) == np.arange(8)[None, :]
    inv = 1.0 / np.float32(THETA) ** (np.arange(0, D, 2, dtype=np.float32) / np.float32(D))
    c[:, C_FREQ:C_FREQ + D // 2] = inv.astype(np.float32)
    c[:, C_LA:C_LA + SA] = SB2 * (SA - 1 - np.arange(SA))
    c[:, C_LB:C_LB + SB2] = SB2 - 1 - np.arange(SB2)
    c[:, C_REV:C_REV + KT] = np.arange(KT)[None, :] * P + (P - 1 - p)[:, None]
    c[:, C_S] = p % S
    c[:, C_QTR] = np.where(p < P // 2, 0.25, 0.0)
    c[:, C_LAST] = p == SA - 1
    return c


def link_on(eng, sem):
    at = {"from": 0, "base": 0, "n": 0}

    def link(ins):
        at["n"] += 1
        ins.then_inc(sem, 1)
        eng.wait_ge(sem, at["base"] + at["n"])

    def begin(i, each):
        at["from"], at["each"] = at["base"] + at["n"], each
        at["base"], at["n"] = i * each + at["from"], 0

    def end(count):
        assert at["n"] == at["each"], (at["n"], at["each"])
        at["base"], at["n"] = at["from"] + count * at["each"], 0

    link.begin, link.end, link.count = begin, end, lambda: at["base"] + at["n"]
    return link


def row_of(ap, n):
    return bass.AP(ap.tensor, 0, [[0, P], [1, n]])


class Plan:
    pass


def apart(eng, m):
    eng.sem_inc(m.passed, 1)


def build(nc, t):
    ctx = ExitStack()
    with ctx:
        m = Plan()
        ctx.enter_context(nc.allow_non_contiguous_dma(reason="single columns and vectors, a few KB in all"))
        m.sem = lambda name: ctx.enter_context(nc.semaphore(name))

        def scratch(name, shape):
            return nc.dram_tensor(name, shape, F32, kind="Internal").ap()

        def sbuf(name, shape, dt=F32):
            return ctx.enter_context(nc.sbuf_tensor(name, shape, dt))

        m.q_dram = scratch("q_dram", [B, D, HQ * S])
        m.k_dram = scratch("k_dram", [2, B, D, HALF * S])
        m.v_dram = scratch("v_dram", [2, TOK, HALF * D])
        m.lag_dram = scratch("lag_dram", [S, L + P])

        m.qb = sbuf("qb", [P, 2 * HQ * S])
        m.wk = sbuf("wk", [P, 8 * LA + 2 * 5 * P])
        m.ident = sbuf("ident", [P, P])[:, :]
        m.keys = sbuf("keys", [P, L])[:, :]
        m.small = sbuf("small", [P, 256])
        m.idx = sbuf("idx", [P, 2, B, KT], I32)
        m.idx_now = sbuf("idx_now", [P, 2, KT], I32)
        m.pages = sbuf("pages", [1, B * NPP], I32)
        m.wo_raw = sbuf("wo_raw", [P, 2, DM])
        m.wo_in = [m.sem("wo_in0"), m.sem("wo_in1")]
        m.psum = ctx.enter_context(nc.psum_tensor("psum", [P, 8 * 512], F32))

        m.passed = m.sem("passed")
        m.lens = m.small[:, 0:B]
        m.lens2_rows = m.small[:, 40:40 + TILES]
        m.lens2 = m.small[:, 96:96 + B]
        gathered = ctx.enter_context(ExitStack())
        m.kg = gathered.enter_context(nc.sbuf_tensor("gathered_keys", [P, 2, NPP + 1, HALF, S], F32, side="right"))
        m.vg = gathered.enter_context(nc.sbuf_tensor("gathered_values", [P, 2, KT + 1, HALF, D], F32, side="right"))
        m.k_in = [m.sem("k_in0"), m.sem("k_in1")]
        m.own_k_in = [m.sem("own_k_in0"), m.sem("own_k_in1")]
        m.v_in = [m.sem("v_in0"), m.sem("v_in1")]
        m.q_in = [m.sem("q_in0"), m.sem("q_in1")]
        m.rows_ready = m.sem("rows_ready")
        project_all(nc, t, m)
        m.big = sbuf("big", [P, HQ * TOK])
        attend_pages(nc, t, m)
        gathered.close()
        project_out(nc, t, m)
        attend_own(nc, t, m)
        m.base_high, m.base_low = (sbuf(f"w_base_{part}", [P, KT * DM]) for part in ("high", "low"))
        m.y_high, m.y_low = (sbuf(f"y_{part}", [P, 2, DM]) for part in ("high", "low"))
        convolve(nc, t, m)
        feed_forward(nc, t, m)


def bank(m, i, w=512):
    return m.psum[:, i * 512:i * 512 + w]


def turns_off(nc, link, turn_count, angle, quarter, dst, add):
    link(nc.vector.tensor_scalar(turn_count, angle, 1.0 / TWO_PI, quarter, ALU.mult, ALU.add))
    link(nc.vector.tensor_scalar(turn_count, turn_count, MAGIC, MAGIC, ALU.add, ALU.subtract))
    link(nc.vector.scalar_tensor_tensor(dst, turn_count, -PI_A, angle, ALU.mult, ALU.add))
    link(nc.vector.scalar_tensor_tensor(dst, turn_count, -PI_B, dst, ALU.mult, ALU.add))
    link(nc.vector.scalar_tensor_tensor(dst, turn_count, -PI_C, dst, ALU.mult, ALU.add))
    link(nc.vector.tensor_scalar(dst, dst, add, PI_LOW, ALU.add, ALU.min))
    return nc.vector.tensor_scalar(dst, dst, -PI_LOW, None, ALU.max)


def exact(ap):
    return ap.bitcast(F32R)


def load_queries(sp, m, n, slot):
    sp.dma_start(m.qb[:, slot * HQ * S:(slot + 1) * HQ * S],
                 m.q_dram[bass.ds(n, 1), :, :].rearrange("o p n -> p (o n)")).then_inc(m.q_in[slot], 16)


def load_own_keys(sp, m, n, half):
    sp.dma_start(m.kg[:, half, NPP, :, :].rearrange("p h k -> p (h k)"),
                 m.k_dram[half, bass.ds(n, 1), :, :].rearrange("o p n -> p (o n)")).then_inc(m.own_k_in[half], 16)


def page_numbers(sp, m, regs, n):
    sp.reg_load(regs, m.pages[0:1, bass.ds(n * NPP, NPP)])
    return [sp.snap(r, min_val=0, max_val=PAGES - 1) for r in regs]


def load_pages(sp, t, m, pages, half):
    for g, page in enumerate(pages):
        sp.dma_start(m.kg[:, half, g, :, :].rearrange("p h k -> p (h k)"),
                     t["kT"][half, bass.ds(page, 1), :, :].rearrange("o p n -> p (o n)")).then_inc(m.k_in[half], 16)


def gather_rows(nc, pool, m, hb, n, half):
    nc.gpsimd.tensor_copy(m.idx_now[:, half, :], m.idx[:, half, bass.ds(n, 1), :].rearrange("p o k -> p (o k)")).then_inc(m.rows_ready, 1)
    pool.wait_ge(m.rows_ready, hb + 1)


def gather_block(pool, t, m, half, k):
    pool.indirect_dma_start(out=m.vg[:, half, k, :, :].rearrange("p h d -> p (h d)"), out_offset=None,
                            in_=t["v"].rearrange("a g k n -> (a g k) n"),
                            in_offset=bass.IndirectOffsetOnAxis(ap=m.idx_now[:, half, k:k + 1], axis=0)).then_inc(m.v_in[half], 16)


def load_own_values(pool, m, n, half):
    pool.dma_start(m.vg[0:S, half, KT, :, :].rearrange("p h d -> p (h d)"),
                   m.v_dram[half, bass.ds(n * S, S), :]).then_inc(m.v_in[half], 16)


def gather_values(nc, pool, t, m, hb, n, half):
    gather_rows(nc, pool, m, hb, n, half)
    apart(pool, m)
    for k in range(KT):
        gather_block(pool, t, m, half, k)
    load_own_values(pool, m, n, half)


def project_all(nc, t, m):
    sem = m.sem
    CQ = HQ * D // 512
    CK = HK * D // 512
    CH = CQ + 2 * CK
    PAIR = 2 * TILES
    VU = CK * TILES
    UNITS = (CQ + CK) * TILES
    ITERS = CQ // 2
    LAG = 3
    RING = 4
    SPLIT_AT = (0, 1, 3, 4)
    H2 = D // 2
    AW = TILES * H2
    qb, wk = m.qb, m.wk
    scope = ExitStack()

    def region(name, shape):
        return scope.enter_context(nc.sbuf_tensor(name, [P] + shape, F32))

    x_high, x_low = region("x_high", [TILES, DM]), region("x_low", [TILES, DM])
    w_high, w_low = region("w1_high", [2, KT * 512]), region("w1_low", [2, KT * 512])
    w_raw = m.vg[:, :, :, :, :].rearrange("p a b c d -> p (a b c d)")[:, 0:2 * KT * 512].rearrange("p (s n) -> p s n", s=2)
    x_raw = m.kg[:, :, :, :, :].rearrange("p a b c d -> p (a b c d)")[:, 0:TILES * DM].rearrange("p (t n) -> p t n", t=TILES)
    rope_t = region("rope_tables", [4, TILES, D])
    raw, roped = region("raw", [RING, 512]), region("roped", [RING, 512])
    stage_q, stage_v = region("stage_q", [RING, 512]), region("stage_v", [RING, 512])
    prod_s, junk = region("prod_s", [2, 512]), region("junk", [512])
    ang = [qb[:, i * AW:(i + 1) * AW] for i in range(4)]
    cs = wk[:, 0:2 * AW].rearrange("p (w n) -> p w n", w=2)
    normw = wk[:, 2 * AW:2 * AW + 2 * D].rearrange("p (w d) -> p w d", w=2)
    cfreq = wk[:, 1536:1536 + H2]
    csid = wk[:, 1600:1601]
    eps_rms = wk[:, 1602:1603]
    ssq, rms, rinv = (wk[:, 1616 + 16 * i:1632 + 16 * i] for i in range(3))
    pages_b = wk[:, 2048:2048 + B * NPP].bitcast(I32)
    lens_i = wk[:, 2560:2560 + B].bitcast(I32)
    pos_i = wk[:, 2600:2600 + TILES].bitcast(I32)
    len2_i = wk[:, 2608:2608 + TILES].bitcast(I32)
    len2b_i = wk[:, 2616:2616 + B].bitcast(I32)
    poscol = wk[:, 2660:2660 + TILES]

    tables_in = sem("tables_in")
    x_in = [sem(f"x_in{i}") for i in range(TILES)]
    w_in = [sem("w_in0"), sem("w_in1")]
    w_first_in = [sem(f"w_first_in{k}") for k in range(KT)]
    x_high_ready, x_low_ready = sem("x_high_ready"), sem("x_low_ready")
    w_high_ready, w_low_ready = sem("w_high_ready"), sem("w_low_ready")
    vector_order, scalar_order = sem("vector_order1"), sem("scalar_order1")
    angles_ready, trig_ready = sem("angles_ready"), sem("trig_ready")
    projected = sem("projected")
    released = sem("released")
    norms_ready = sem("norms_ready")
    rotated = sem("rotated")
    scaled = sem("scaled")
    turned = sem("turned")
    staged = sem("staged")
    m.q_out = q_out = [sem(f"q_out{i}") for i in range(RING)]
    v_out = [sem(f"v_out{i}") for i in range(RING)]
    m.q_out_all = 16 + 16 * UNITS // RING

    def stored(unit):
        return 16 + 16 * (unit // RING + 1)
    TABLES = 16 * (8 + 2 * BPT + 2)

    def chunk_of(it, i):
        return CK + 2 * it + i // TILES

    with scope, nc.Block() as block:
        @block.sync
        def _(sp):
            for i in range(RING):
                sp.sem_inc(q_out[i], 16)
                sp.sem_inc(v_out[i], 16)

            def load_weights(c, slot):
                sp.dma_start(w_raw[:, slot, :], t["w1"][bass.ds(c, 1), :, :].rearrange("o p n -> p (o n)")).then_inc(w_in[slot], 16)

            def load_x(tile):
                sp.dma_start(x_raw[:, tile, :], t["xT"][tile, :, :]).then_inc(x_in[tile], 16)

            load_x(0)
            for k in range(KT):
                cols = slice(k * 512, (k + 1) * 512)
                sp.dma_start(w_raw[:, 0, cols], t["w1"][0, :, cols]).then_inc(w_first_in[k], 16)
            for tile in range(1, TILES):
                load_x(tile)
            load_weights(1, 1)
            regs = [sp.alloc_register(f"first_page{i}") for i in range(NPP)]
            for u in range(VU):
                if u == TILES:
                    sp.wait_ge(x_low_ready, TILES)
                    sp.wait_ge(tables_in, TABLES)
                    first_pages = page_numbers(sp, m, regs, 0)
                    load_pages(sp, t, m, first_pages, 0)
                if u == TILES + 4:
                    load_pages(sp, t, m, first_pages, 1)
                if u % TILES == 1:
                    c = u // TILES + 2
                    sp.wait_ge(w_low_ready, KT * (c - 1))
                    load_weights(c, c % 2)
                sp.wait_ge(released, u + 1 + LEAD)
                sp.dma_start(m.v_dram[u // TILES, (u % TILES) * P:(u % TILES + 1) * P, :], stage_v[:, u % RING, :]).then_inc(v_out[u % RING], 16)

            def iteration(it, keys):
                for i in range(PAIR):
                    tile, c = i % TILES, 2 * it + i // TILES
                    if tile == 1 and not keys:
                        sp.wait_ge(w_low_ready, KT * (c + CK + 1))
                        load_weights(c + CK + 2, (CK + i // TILES) % 2)
                    sp.wait_ge(staged, PAIR * it + i + 1 + LEAD)
                    src = stage_q[:, i % RING, :].rearrange("p (b n) -> p b n", b=BPT)
                    rows = slice(tile * BPT, (tile + 1) * BPT)
                    dst = m.k_dram[i // TILES, rows, :, :] if keys else m.q_dram[rows, :, bass.ds(c * P, P)]
                    sp.dma_start(dst.rearrange("b p n -> p b n"), src).then_inc(q_out[i % RING], 16)

            with sp.Fori(0, ITERS) as it:
                iteration(it, False)
            iteration(ITERS, True)
            for i in range(RING):
                sp.wait_ge(v_out[i], 16 + 16 * VU // RING)

        @block.gpsimd
        def _(pool):
            pool.sem_inc(scaled, LEAD)
            pool.dma_start(m.ident, t["consts"][:, C_ID:C_ID + P]).then_inc(tables_in, 16)
            for b in range(BPT):
                for dst, name in ((pos_i, "lens"), (len2_i, "lens2")):
                    pool.dma_start(dst[b * S:(b + 1) * S, :],
                                   bass.AP(t[name].tensor, b, [[0, S], [BPT, TILES]])).then_inc(tables_in, 16)
            pool.dma_start(csid, t["consts"][:, C_S:C_S + 1]).then_inc(tables_in, 16)
            pool.dma_start(cfreq, t["consts"][:, C_FREQ:C_FREQ + H2]).then_inc(tables_in, 16)
            for w, name in enumerate(("q_norm", "k_norm")):
                pool.dma_start(normw[:, w, :], row_of(t[name], D)).then_inc(tables_in, 16)
            pool.dma_start(lens_i, row_of(t["lens"], B)).then_inc(tables_in, 16)
            pool.dma_start(len2b_i, row_of(t["lens2"], B)).then_inc(tables_in, 16)
            pool.dma_start(pages_b, row_of(t["table"], B * NPP)).then_inc(tables_in, 16)
            pool.dma_start(m.keys, t["consts"][:, C_KEY:C_KEY + L]).then_inc(tables_in, 16)
            pool.dma_start(m.pages[:, :], bass.AP(t["table"].tensor, 0, [[0, 1], [1, B * NPP]])).then_inc(tables_in, 16)
            def norm(it, i):
                pool.wait_ge(rotated, PAIR * it + i + 1 + LEAD)
                pool.wait_ge(turned, PAIR * it + i + 1 - RING + LEAD)
                apart(pool, m)
                g = i % RING
                for h in range(4):
                    ins = nc.gpsimd.tensor_scalar(roped[:, g, h * P:(h + 1) * P], raw[:, g, h * P:(h + 1) * P],
                                                  rinv[:, 4 * g + h:4 * g + h + 1], 1.0, ALU.mult, ALU.mult)
                ins.then_inc(scaled, 1)

            with pool.Fori(0, ITERS) as it:
                for i in range(PAIR):
                    norm(it, i)
            for i in range(PAIR):
                norm(ITERS, i)
                if i == RING:
                    pool.wait_ge(q_out[0], stored(PAIR * ITERS))
                    load_queries(pool, m, 0, 0)
                    load_own_keys(pool, m, 0, 0)
                if i == 2 * RING:
                    load_queries(pool, m, 1, 1)
                if i == TILES:
                    pool.wait_ge(w_low_ready, KT * CH)
                    for done in v_out:
                        pool.wait_ge(done, 16 + 16 * VU // RING)
                    gather_rows(nc, pool, m, 0, 0, 0)
                    load_own_values(pool, m, 0, 0)
                if TILES < i <= TILES + KT:
                    apart(pool, m)
                    gather_block(pool, t, m, 0, i - TILES - 1)
                if i == TILES + RING + 1:
                    pool.wait_ge(q_out[0], stored(PAIR * ITERS + TILES))
                    load_own_keys(pool, m, 0, 1)

        @block.scalar
        def _(act):
            for s in (released, norms_ready, staged):
                act.sem_inc(s, LEAD)

            def split_x(tile):
                act.wait_ge(x_in[tile], 16)
                nc.scalar.activation(exact(x_high[:, tile, :]), x_raw[:, tile, :], ACT.Copy).then_inc(x_high_ready, 1)

            def split_weights(uses, slot, k):
                if uses is None:
                    act.wait_ge(w_first_in[k], 16)
                else:
                    act.wait_ge(w_in[slot], 16 * uses)
                cols = slice(k * 512, (k + 1) * 512)
                nc.scalar.activation(exact(w_high[:, slot, cols]), w_raw[:, slot, cols], ACT.Copy).then_inc(w_high_ready, 1)

            split_x(0)
            for k in range(KT):
                split_weights(None, 0, k)
            for tile in range(1, TILES // 2):
                split_x(tile)
            for u in range(VU):
                act.wait_ge(projected, u + 1 + LEAD)
                act.wait_ge(v_out[u % RING], 16 * (u // RING) + 16)
                nc.scalar.activation(stage_v[:, u % RING, :], bank(m, u % RING), ACT.Copy).then_inc(released, 1)
                if u < TILES // 2:
                    split_x(u + TILES // 2)
                c, tile = u // TILES, u % TILES
                at = (3, 4, 5, 6) if c == 0 else SPLIT_AT
                if tile in at:
                    split_weights(1, (c + 1) % 2, at.index(tile))
                if u == VU // 2 + 2:
                    act.wait_ge(angles_ready, 1)
                    nc.scalar.activation(cs[:, 0, :], ang[1], ACT.Sin).then_inc(trig_ready, 1)
                    act.wait_ge(angles_ready, 2)
                    nc.scalar.activation(cs[:, 1, :], ang[2], ACT.Sin).then_inc(trig_ready, 1)
            link = link_on(act, scalar_order)

            def release(it, i, last):
                r, g = PAIR * it + i, i % RING
                act.wait_ge(projected, VU + r + 1 + LEAD)
                act.wait_ge(scaled, r + 1 - RING + LEAD)
                nc.scalar.activation(raw[:, g, :], bank(m, g), ACT.Copy).then_inc(released, 1)
                act.wait_ge(released, VU + r + 1 + LEAD)
                for h in range(4):
                    ins = nc.scalar.activation(junk[:, h * P:(h + 1) * P], raw[:, g, h * P:(h + 1) * P],
                                               ACT.Square, accum_out=ssq[:, 4 * g + h:4 * g + h + 1])
                link(ins)
                nc.scalar.activation(rms[:, 4 * g:4 * g + 4], ssq[:, 4 * g:4 * g + 4], ACT.Sqrt,
                                     scale=1.0 / D, bias=eps_rms).then_inc(norms_ready, 1)
                if i % TILES in SPLIT_AT and not (last and i >= TILES):
                    c = CK + i // TILES + 1
                    split_weights(it + (c // 2 + c % 2), c % 2, SPLIT_AT.index(i % TILES))

            def stage(it, i):
                act.wait_ge(turned, PAIR * it + i + 1 + LEAD)
                act.wait_ge(q_out[i % RING], (PAIR // RING * it + i // RING) * 16 + 16)
                nc.scalar.activation(
                    stage_q[:, i % RING, :].rearrange("p (b h s) -> p h b s", b=BPT, h=4),
                    bank(m, 4 + i % RING).rearrange("p (h b s) -> p h b s", h=4, b=BPT), ACT.Copy).then_inc(staged, 1)

            def iteration(it, last):
                for i in range(PAIR):
                    ahead = i + LAG
                    if ahead < PAIR:
                        release(it, ahead, last)
                    elif not last:
                        release(it + 1, ahead - PAIR, False)
                    stage(it, i)

            for i in range(LAG):
                release(0, i, False)
            with act.Fori(0, ITERS) as it:
                link.begin(it, PAIR)
                iteration(it, False)
            link.end(ITERS)
            iteration(ITERS, True)

        @block.vector
        def _(dve):
            dve.sem_inc(rotated, LEAD)
            link = link_on(dve, vector_order)

            def split_x(tile):
                dve.wait_ge(x_high_ready, tile + 1)
                nc.vector.tensor_tensor(exact(x_low[:, tile, :]), x_raw[:, tile, :], x_high[:, tile, :], ALU.subtract).then_inc(x_low_ready, 1)

            def split_weights(c, slot, k):
                dve.wait_ge(w_high_ready, KT * c + k + 1)
                cols = slice(k * 512, (k + 1) * 512)
                nc.vector.tensor_tensor(exact(w_low[:, slot, cols]), w_raw[:, slot, cols], w_high[:, slot, cols], ALU.subtract).then_inc(w_low_ready, 1)

            split_x(0)
            for k in range(KT):
                split_weights(0, 0, k)
            for tile in range(1, TILES):
                split_x(tile)
            dve.wait_ge(tables_in, TABLES)
            nc.vector.memset(eps_rms, EPS_RMS)
            nc.vector.tensor_copy(m.lens, lens_i)
            nc.vector.tensor_copy(m.lens2, len2b_i)
            nc.vector.tensor_copy(m.lens2_rows, len2_i)
            link(nc.vector.tensor_scalar(poscol, pos_i, csid, None, ALU.add))
            by_quarter = pages_b.rearrange("p (b k r) -> p b k r", b=B, r=BPT)
            for r in range(BPT):
                rows = slice(r * S, (r + 1) * S)
                link(nc.vector.tensor_scalar(m.idx[rows, 0, :, :], by_quarter[rows, :, :, r], float(PSIZE), csid[rows, :],
                                             ALU.mult, ALU.add))
            nc.vector.tensor_scalar(m.idx[:, 1, :, :], m.idx[:, 0, :, :], float(PAGES * PSIZE), None, ALU.add)
            link(nc.vector.tensor_tensor(ang[0].rearrange("p (t d) -> p t d", t=TILES),
                                         poscol.unsqueeze(2).broadcast_to([P, TILES, H2]),
                                         cfreq.unsqueeze(1).broadcast_to([P, TILES, H2]), ALU.mult))
            for k in range(KT):
                split_weights(1, 1, k)
            for quarter, dst in ((0.0, ang[1]), (0.25, ang[2])):
                turns_off(nc, link, ang[3], ang[0], quarter, dst, quarter * TWO_PI).then_inc(angles_ready, 1)
            dve.wait_ge(trig_ready, 2)
            sin, cos = (cs[:, i, :].rearrange("p (t d) -> p t d", t=TILES) for i in range(2))
            for w in range(2):
                for lo in range(2):
                    own = normw[:, w, lo * H2:(lo + 1) * H2].unsqueeze(1).broadcast_to([P, TILES, H2])
                    other = normw[:, w, (1 - lo) * H2:(2 - lo) * H2].unsqueeze(1).broadcast_to([P, TILES, H2])
                    nc.vector.tensor_tensor(rope_t[:, 2 * w, :, lo * H2:(lo + 1) * H2], cos, own, ALU.mult)
                    link(nc.vector.tensor_tensor(rope_t[:, 2 * w + 1, :, lo * H2:(lo + 1) * H2], sin, other, ALU.mult))
                half_s = rope_t[:, 2 * w + 1, :, 0:H2]
                link(nc.vector.tensor_scalar(half_s, half_s, -1.0, None, ALU.mult))
            for k in range(KT):
                split_weights(2, 0, k)

            def rotate(it, i, w):
                r, tile, g = PAIR * it + i, i % TILES, i % RING
                dve.wait_ge(released, VU + r + 1 + LEAD)
                rot = raw[:, g, :].rearrange("p (h d) -> p h d", h=4)
                ps = prod_s[:, i % 2, :].rearrange("p (h d) -> p h d", h=4)
                cos_t, sin_t = (rope_t[:, 2 * w + n, tile:tile + 1, :] for n in range(2))
                nc.vector.tensor_tensor(ps[:, :, 0:H2], rot[:, :, H2:D], sin_t[:, :, 0:H2].broadcast_to([P, 4, H2]), ALU.mult)
                link(nc.vector.tensor_tensor(ps[:, :, H2:D], rot[:, :, 0:H2], sin_t[:, :, H2:D].broadcast_to([P, 4, H2]), ALU.mult))
                dve.wait_ge(norms_ready, r + 1 + LEAD)
                nc.vector.reciprocal(rinv[:, 4 * g:4 * g + 4], rms[:, 4 * g:4 * g + 4])
                link(nc.vector.tensor_tensor(rot, rot, cos_t.broadcast_to([P, 4, D]), ALU.mult))
                nc.vector.tensor_tensor(raw[:, g, :], raw[:, g, :], prod_s[:, i % 2, :], ALU.add).then_inc(rotated, 1)

            def iteration(it, w):
                for i in range(PAIR):
                    rotate(it, i, w)
                    if i % TILES in SPLIT_AT and not (w == 1 and i >= TILES):
                        c = chunk_of(it, i) + 1
                        split_weights(c, (CK + i // TILES + 1) % 2, SPLIT_AT.index(i % TILES))

            with dve.Fori(0, ITERS) as it:
                link.begin(it, 2 * PAIR)
                iteration(it, 0)
            link.end(ITERS)
            iteration(ITERS, 1)

        @block.tensor
        def _(pe):
            pe.sem_inc(projected, LEAD)
            pe.sem_inc(turned, LEAD)

            def project(u, tile, slot, c, first):
                if first:
                    pe.wait_ge(x_low_ready, tile + 1)
                if tile == 0 and not first:
                    pe.wait_ge(w_low_ready, KT * c + KT)
                pe.wait_ge(released, u + 1 - RING + LEAD)
                out = bank(m, tile % RING)
                for k in range(KT):
                    if first and tile == 0:
                        pe.wait_ge(w_low_ready, k + 1)
                    xk, wk_ = slice(k * P, (k + 1) * P), slice(k * 512, (k + 1) * 512)
                    nc.tensor.matmul(out, exact(x_high[:, tile, xk]), exact(w_high[:, slot, wk_]), start=(k == 0), stop=False)
                    nc.tensor.matmul(out, exact(x_high[:, tile, xk]), exact(w_low[:, slot, wk_]), start=False, stop=False)
                    ins = nc.tensor.matmul(out, exact(x_low[:, tile, xk]), exact(w_high[:, slot, wk_]), start=False, stop=(k == KT - 1))
                ins.then_inc(projected, 1)

            def rope_unit(it, i):
                project(VU + PAIR * it + i, i % TILES, (CK + i // TILES) % 2, chunk_of(it, i), False)

            def turn(it, i):
                r = PAIR * it + i
                pe.wait_ge(scaled, r + 1 + LEAD)
                pe.wait_ge(staged, r + 1 - RING + LEAD)
                for h in range(4):
                    ins = nc.tensor.transpose(bank(m, 4 + i % RING)[:, h * P:(h + 1) * P],
                                              roped[:, i % RING, h * P:(h + 1) * P], m.ident)
                ins.then_inc(turned, 1)

            def iteration(it, last):
                for i in range(PAIR):
                    ahead = i + LAG
                    if ahead < PAIR:
                        rope_unit(it, ahead)
                    elif not last:
                        rope_unit(it + 1, ahead - PAIR)
                    turn(it, i)

            for u in range(VU):
                project(u, u % TILES, u // TILES, u // TILES, u < TILES)
            for i in range(LAG):
                rope_unit(0, i)
            pe.wait_ge(tables_in, TABLES)
            with pe.Fori(0, ITERS) as it:
                iteration(it, False)
            iteration(ITERS, True)


def attend_pages(nc, t, m):
    sem = m.sem
    kg, vg, k_in, v_in, q_in = m.kg, m.vg, m.k_in, m.v_in, m.q_in
    q_t = m.qb[:, :].rearrange("p (s h n) -> p s h n", s=2, h=HK)
    tiles = m.wk[:, 0:8 * LA].rearrange("p (s n) -> p s n", s=8)
    mask, masked, probs = tiles[:, 0:2], tiles[:, 2:4], tiles[:, 4:8]
    probs_t = m.wk[:, 8 * LA:].rearrange("p (s n) -> p s n", s=2)
    out_t = m.big[:, :].rearrange("p (h n) -> p h n", h=HQ)
    row_max, bias, row_sum, inv_sum = (m.small[:, 128 + 4 * i:132 + 4 * i] for i in range(4))
    UNITS = B * HK
    PER = 16
    ITERS = UNITS // PER

    vector_order = sem("vector_order2")
    scored = sem("scored")
    maxed = sem("maxed")
    biased = sem("biased")
    exped = sem("exped")
    inverted = sem("inverted")
    normed = sem("normed")
    p_turned = sem("p_turned")
    p_copied = sem("p_copied")
    summed = sem("summed")
    stored = sem("stored")
    K_DMAS, V_DMAS = 16 * NPP, 16 * (KT + 1)

    FIRST = (NPP + 2) // 2

    def scores_bank(j):
        o = (j % 2) * 1024 + 512 - FIRST * PSIZE
        return m.psum[:, o:o + LA]

    with nc.Block() as block:
        @block.sync
        def _(sp):
            regs = [sp.alloc_register(f"page{i}") for i in range(NPP)]

            def keys(n):
                for half in range(2):
                    sp.wait_ge(scored, (2 * n + half) * HALF - HALF + LEAD)
                    if half == 0:
                        pages = page_numbers(sp, m, regs, n)
                    load_pages(sp, t, m, pages, half)

            with sp.Fori(1, B) as n:
                keys(n)
            for i in range(2):
                sp.dma_start(m.wo_raw[:, i, :], t["wo"][i, :, :]).then_inc(m.wo_in[i], 16)

        @block.gpsimd
        def _(pool):
            gather_values(nc, pool, t, m, 1, 0, 1)
            for done in m.q_out:
                pool.wait_ge(done, m.q_out_all)

            def batch(n, slot, with_queries):
                if with_queries:
                    pool.wait_ge(scored, n * HK - HK + LEAD)
                    load_queries(pool, m, n, slot)
                for half in range(2):
                    pool.wait_ge(scored, (2 * n + half) * HALF - HALF + LEAD)
                    load_own_keys(pool, m, n, half)
                    pool.wait_ge(summed, (2 * n + half) * HALF - HALF + LEAD)
                    gather_values(nc, pool, t, m, 2 * n + half, n, half)

            batch(1, 1, False)
            with pool.Fori(1, ITERS) as it:
                batch(2 * it, 0, True)
                batch(2 * it + 1, 1, True)

        @block.tensor
        def _(pe):
            for s in (scored, p_turned, summed):
                pe.sem_inc(s, LEAD)

            def scores(it, j):
                u, slot, h = PER * it + j, (j // HALF) % 2, j % HALF
                if j % HK == 0:
                    pe.wait_ge(q_in[(j // HK) % 2], 16 * it + 16)
                if j % HALF == 0:
                    pe.wait_ge(k_in[slot], (2 * it + j // HK) * K_DMAS + K_DMAS)
                    pe.wait_ge(m.own_k_in[slot], (2 * it + j // HK) * 16 + 16)
                pe.wait_ge(maxed, u + 1 - 2 + LEAD)
                lhs = q_t[:, (j // HK) % 2, j % HK, :]
                first = FIRST * PSIZE
                nc.tensor.matmul(scores_bank(j)[:, 0:first], lhs, kg[:, slot, 0:FIRST, h, :], start=True, stop=True)
                nc.tensor.matmul(scores_bank(j)[:, first:LA], lhs, kg[:, slot, FIRST:NPP + 1, h, :], start=True, stop=True).then_inc(scored, 1)

            def turn(u, j):
                pe.wait_ge(normed, u + 1 + LEAD)
                pe.wait_ge(p_copied, u + LEAD)
                for k in range(KT):
                    nc.tensor.transpose(bank(m, 4)[:, k * P:(k + 1) * P], probs[:, j % 4, k * P:(k + 1) * P], m.ident)
                nc.tensor.transpose(bank(m, 5)[0:S, 0:P], probs[:, j % 4, L:LA], m.ident).then_inc(p_turned, 1)

            def output(it, u, j):
                slot, h = (j // HALF) % 2, j % HALF
                if j % HALF == 0:
                    pe.wait_ge(v_in[slot], (2 * it + j // HK) * V_DMAS + V_DMAS)
                pe.wait_ge(p_copied, u + 1 + LEAD)
                pe.wait_ge(stored, u + 1 - 2 + LEAD)
                for k in range(KT):
                    nc.tensor.matmul(bank(m, 6 + j % 2)[:, 0:P], vg[:, slot, k, h, :], probs_t[:, j % 2, k * P:(k + 1) * P],
                                     start=(k == 0), stop=False)
                nc.tensor.matmul(bank(m, 6 + j % 2)[:, 0:P], vg[0:S, slot, KT, h, :], probs_t[0:S, j % 2, L:L + P],
                                 start=False, stop=True).then_inc(summed, 1)

            def iteration(it, first):
                for j in range(PER):
                    scores(it, j)
                    if not (first and j < 2):
                        turn(PER * it + j - 2, (j - 2) % PER)
                    if not (first and j < 3):
                        output(it if j >= 3 else it - 1, PER * it + j - 3, (j - 3) % PER)

            iteration(0, True)
            with pe.Fori(1, ITERS) as it:
                iteration(it, False)
            output(ITERS - 1, UNITS - 3, PER - 3)
            turn(UNITS - 2, PER - 2)
            output(ITERS - 1, UNITS - 2, PER - 2)
            turn(UNITS - 1, PER - 1)
            output(ITERS - 1, UNITS - 1, PER - 1)

        @block.vector
        def _(dve):
            for s in (maxed, biased, inverted, normed):
                dve.sem_inc(s, LEAD)
            link = link_on(dve, vector_order)
            link(nc.vector.memset(mask[:, :, L:LA], 0.0))

            def normalise(u, j):
                dve.wait_ge(exped, u + 1 + LEAD)
                nc.vector.reciprocal(inv_sum[:, j % 4:j % 4 + 1], row_sum[:, j % 4:j % 4 + 1]).then_inc(inverted, 1)
                dve.wait_ge(inverted, u + 1 + LEAD)
                nc.vector.tensor_scalar(probs[:, j % 4, :], probs[:, j % 4, :], inv_sum[:, j % 4:j % 4 + 1], None,
                                        ALU.mult).then_inc(normed, 1)

            def iteration(it, first):
                link.begin(0 if first else it - 1, 2)
                for j in range(PER):
                    u = PER * it + j
                    if j % HK == 0:
                        n = 2 * it + j // HK
                        link(nc.vector.tensor_scalar(mask[:, j // HK, 0:L], m.keys, m.lens[:, bass.ds(n, 1)], NEG, ALU.is_ge, ALU.mult))
                    dve.wait_ge(scored, u + 1 + LEAD)
                    dve.wait_ge(exped, u + 1 - 2 + LEAD)
                    apart(dve, m)
                    nc.vector.tensor_tensor_reduce(out=masked[:, j % 2, :], in0=scores_bank(j), in1=mask[:, j // HK, :], scale=1.0,
                                                   scalar=-3.0e38, op0=ALU.add, op1=ALU.max,
                                                   accum_out=row_max[:, j % 4:j % 4 + 1]).then_inc(maxed, 1)
                    dve.wait_ge(maxed, u + 1 + LEAD)
                    nc.vector.tensor_scalar(bias[:, j % 4:j % 4 + 1], row_max[:, j % 4:j % 4 + 1], -SCALE, None, ALU.mult).then_inc(biased, 1)
                    if not (first and j < 1):
                        normalise(u - 1, (j - 1) % PER)

            iteration(0, True)
            link.end(1)
            with dve.Fori(1, ITERS) as it:
                iteration(it, False)
            normalise(UNITS - 1, PER - 1)

        @block.scalar
        def _(act):
            for s in (exped, p_copied, stored):
                act.sem_inc(s, LEAD)

            def exponentials(u, j):
                act.wait_ge(biased, u + 1 + LEAD)
                act.wait_ge(p_turned, u + 1 - 4 + LEAD)
                nc.scalar.activation(probs[:, j % 4, :], masked[:, j % 2, :], ACT.Exp, bias=bias[:, j % 4:j % 4 + 1], scale=SCALE,
                                     accum_out=row_sum[:, j % 4:j % 4 + 1]).then_inc(exped, 1)

            def copy_turned(u, j):
                act.wait_ge(p_turned, u + 1 + LEAD)
                act.wait_ge(summed, u + 1 - 2 + LEAD)
                nc.scalar.activation(probs_t[:, j % 2, 0:L], bank(m, 4), ACT.Copy)
                nc.scalar.activation(probs_t[0:S, j % 2, L:L + P], bank(m, 5)[0:S, 0:P], ACT.Copy).then_inc(p_copied, 1)

            def store(n, u, j):
                act.wait_ge(summed, u + 1 + LEAD)
                h = j % HK
                nc.scalar.activation(out_t[:, h * REP:(h + 1) * REP, bass.ds(n * S, S)],
                                     bank(m, 6 + j % 2)[:, 0:P].rearrange("p (g s) -> p g s", g=REP), ACT.Copy).then_inc(stored, 1)

            def iteration(it, first):
                for j in range(PER):
                    u = PER * it + j
                    if not (first and j < 2):
                        copy_turned(u - 2, (j - 2) % PER)
                    exponentials(u, j)
                    if not (first and j < 4):
                        store(2 * it + (j - 4) // HK, u - 4, (j - 4) % PER)

            iteration(0, True)
            with act.Fori(1, ITERS) as it:
                iteration(it, False)
            store(B - 1, UNITS - 4, PER - 4)
            copy_turned(UNITS - 2, PER - 2)
            store(B - 1, UNITS - 3, PER - 3)
            copy_turned(UNITS - 1, PER - 1)
            store(B - 1, UNITS - 2, PER - 2)
            store(B - 1, UNITS - 1, PER - 1)


def project_out(nc, t, m):
    sem = m.sem
    RING = 3
    scope = ExitStack()

    def parts(name, cols):
        return scope.enter_context(nc.sbuf_tensor(name, [P, RING, cols], F32))

    wo_high, wo_low, out_high, out_low = parts("wo_high", DM), parts("wo_low", DM), parts("out_high", TOK), parts("out_low", TOK)
    out_t = m.big[:, :].rearrange("p (h n) -> p h n", h=HQ)
    m.cond_t = m.big[:, 0:KT * TOK].rearrange("p (k n) -> p k n", k=KT)
    o = KT * TOK
    m.w_qkv = m.big[:, o:o + KT * 3 * DM].rearrange("p (k n) -> p k n", k=KT)
    o += KT * 3 * DM
    m.alibi = m.big[:, o:o + NH2 * S]
    o += NH2 * S
    m.x = m.big[:, o:o + TILES * DM].rearrange("p (t n) -> p t n", t=TILES)
    o += TILES * DM
    m.w_out = m.big[:, o:o + KT * DM].rearrange("p (k n) -> p k n", k=KT)
    o += KT * DM
    m.own_from = o
    FREED = -(-o // TOK)
    m.own_in = sem("own_in")
    HT = TOK // 512
    ssm_in = sem("ssm_in")
    high_ready, low_ready = sem("high_ready"), sem("low_ready")
    head_done = sem("head_done")
    cond_copied = sem("cond_copied")
    gen_v, gen_s = sem("gen_vector"), sem("gen_scalar")

    c = [m.wk[:, 32 * i:32 * i + 32] for i in range(40)]
    log_dt, log_a, a_im, c_re, c_im = c[0:5]
    dt, a_re, re, im, half_re, half_im = c[5:11]
    th, em1, sh, ch, cosm1, e_re, e_im, den, g_re, g_im = c[11:21]
    t0, t1, w_re, w_im, f1, f2, arg_s, arg_c, cnt = c[21:30]
    tab = m.wk[:, 1280:1280 + 128]
    lag_a, lag_b, quarter = tab[:, 0:SA], tab[:, SA:SA + SB2], tab[:, 64:65]
    quarter_angle = tab[:, 65:66]
    m.fac_a = m.wk[:, 1408:1408 + S * SA]
    m.fac_b = m.qb[:, 0:S * SB2]
    mag_b, ang_b, cnt_b = (m.wk[:, 1920 + 1024 * i:2944 + 1024 * i] for i in range(3))
    PEELED, PER = 8, 6
    LOOPS = (HQ - PEELED) // PER
    gen = {}
    mag_a, ang_a, cnt_a = (m.qb[:, 1024:1536], m.wk[:, 4992:5504], m.qb[:, 1536:2048])

    with scope, nc.Block() as block:
        @block.sync
        def _(sp):
            with sp.Fori(1, HQ // 2) as it:
                for i in range(2):
                    sp.wait_ge(low_ready, 2 * it + i - 2 + 1)
                    sp.dma_start(m.wo_raw[:, i, :], t["wo"][bass.ds(2 * it + i, 1), :, :].rearrange("o p n -> p (o n)")).then_inc(m.wo_in[i], 16)
            sp.wait_ge(head_done, FREED)
            sp.dma_start(m.w_qkv, t["w_qkv"]).then_inc(m.own_in, 16)
            sp.dma_start(m.alibi, t["consts"][:, C_ALIBI:C_ALIBI + NH2 * S]).then_inc(m.own_in, 16)
            sp.dma_start(m.w_out, t["w_out"]).then_inc(m.own_in, 16)
            sp.dma_start(m.x, t["x"].rearrange("(t p) n -> p t n", p=P)).then_inc(m.own_in, 16)

        @block.gpsimd
        def _(pool):
            pool.dma_start(log_dt, row_of(t["log_dt"], S)).then_inc(ssm_in, 16)
            for dst, name in ((log_a, "log_a"), (a_im, "a_imag"), (c_re, "c_re"), (c_im, "c_im")):
                pool.dma_start(dst, t[name]).then_inc(ssm_in, 16)
            pool.dma_start(tab[:, 0:SA + SB2], t["consts"][:, C_LA:C_LB + SB2]).then_inc(ssm_in, 16)
            pool.dma_start(quarter, t["consts"][:, C_QTR:C_QTR + 1]).then_inc(ssm_in, 16)

            def split(h, i, n):
                pool.wait_ge(high_ready, 2 * h + 1)
                out_row = out_t[:, bass.ds(h, 1), :].rearrange("p o n -> p (o n)")
                nc.gpsimd.tensor_tensor(exact(out_low[:, n, :]), out_row, out_high[:, n, :], ALU.subtract)
                pool.wait_ge(high_ready, 2 * h + 2)
                if isinstance(h, int) and h == 2:
                    pool.wait_ge(low_ready, 2)
                nc.gpsimd.tensor_tensor(exact(wo_low[:, n, :]), m.wo_raw[:, i, :], wo_high[:, n, :], ALU.subtract).then_inc(low_ready, 1)

            for h in range(2, PEELED):
                split(h, h % 2, h % RING)
            with pool.Fori(0, LOOPS) as it:
                for j in range(PER):
                    split(PER * it + (PEELED + j), (PEELED + j) % 2, (PEELED + j) % RING)
            pool.wait_ge(ssm_in, 16 * 7)

        @block.tensor
        def _(pe):
            def multiply(h, n, first, last):
                pe.wait_ge(low_ready, h + 1)
                for j in range(KT):
                    cols = slice(j * P, (j + 1) * P)
                    for weights, outs in ((wo_high, (out_high, out_low)), (wo_low, (out_high,))):
                        for o in outs:
                            for half in range(HT):
                                ins = nc.tensor.matmul(bank(m, j * HT + half), exact(weights[:, n, cols]),
                                                       exact(o[:, n, half * 512:(half + 1) * 512]),
                                                       start=first and weights is wo_high and o is out_high,
                                                       stop=last and weights is wo_low)
                ins.then_inc(head_done, 1)

            for h in range(PEELED):
                multiply(h, h % RING, h == 0, False)
            with pe.Fori(0, LOOPS - 1) as it:
                for j in range(PER):
                    multiply(PER * it + (PEELED + j), (PEELED + j) % RING, False, False)
            for h in range(HQ - PER, HQ):
                multiply(h, h % RING, False, h == HQ - 1)

        @block.vector
        def _(dve):
            link = link_on(dve, gen_v)
            at = gen
            tt, ts, stt = nc.vector.tensor_tensor, nc.vector.tensor_scalar, nc.vector.scalar_tensor_tensor

            def mark(name):
                at[name] = link.count()

            def per_s(x, n):
                return x.unsqueeze(2).broadcast_to([P, S, n])

            def lags(x, n):
                return x.unsqueeze(1).broadcast_to([P, S, n])

            def grid(x, n):
                return x.rearrange("p (s n) -> p s n", s=S)

            for h in range(2):
                dve.wait_ge(high_ready, 2 * h + 1)
                nc.vector.tensor_tensor(exact(out_low[:, h, :]), out_t[:, h, :], out_high[:, h, :], ALU.subtract)
                dve.wait_ge(high_ready, 2 * h + 2)
                nc.vector.tensor_tensor(exact(wo_low[:, h, :]), m.wo_raw[:, h, :], wo_high[:, h, :], ALU.subtract).then_inc(low_ready, 1)
            dve.wait_ge(ssm_in, 16 * 7)
            dve.wait_ge(gen_s, 2)
            link(tt(re, a_re, dt, ALU.mult))
            link(ts(re, re, -1.0, None, ALU.mult))
            link(tt(im, a_im, dt, ALU.mult))
            link(ts(half_re, re, 0.5, None, ALU.mult))
            mark("half_re")
            link(tt(grid(mag_b, SB2), per_s(re, SB2), lags(lag_b, SB2), ALU.mult))
            mark("mag_b")
            link(tt(grid(mag_a, SA), per_s(re, SA), lags(lag_a, SA), ALU.mult))
            mark("mag_a")
            link(ts(half_im, im, 0.5, None, ALU.mult))
            link(turns_off(nc, link, cnt, half_im, 0.0, arg_s, 0.0))
            mark("sh")
            link(turns_off(nc, link, cnt, half_im, 0.25, arg_c, 0.25 * TWO_PI))
            mark("ch")
            link(ts(quarter_angle, quarter, TWO_PI, None, ALU.mult))
            link(tt(grid(ang_b, SB2), per_s(im, SB2), lags(lag_b, SB2), ALU.mult))
            link(turns_off(nc, link, cnt_b, ang_b, quarter, ang_b, quarter_angle))
            mark("ang_b")
            link(tt(grid(ang_a, SA), per_s(im, SA), lags(lag_a, SA), ALU.mult))
            link(turns_off(nc, link, cnt_a, ang_a, 0.25, ang_a, 0.25 * TWO_PI))
            mark("ang_a")
            dve.wait_ge(gen_s, 7)
            link(ts(t0, th, -1.0, 1.0, ALU.mult, ALU.add))
            link(nc.vector.reciprocal(t0, t0))
            link(ts(t1, th, 2.0, None, ALU.mult))
            link(tt(em1, t1, t0, ALU.mult))
            link(tt(cosm1, sh, sh, ALU.mult))
            link(ts(cosm1, cosm1, -2.0, None, ALU.mult))
            link(ts(t0, em1, 1.0, None, ALU.add))
            link(tt(t1, cosm1, t0, ALU.mult))
            link(tt(e_re, em1, t1, ALU.add))
            link(tt(t1, sh, ch, ALU.mult))
            link(tt(t1, t1, t0, ALU.mult))
            link(ts(e_im, t1, 2.0, None, ALU.mult))
            link(tt(t0, a_re, a_re, ALU.mult))
            link(tt(t1, a_im, a_im, ALU.mult))
            link(tt(den, t0, t1, ALU.add))
            link(nc.vector.reciprocal(den, den))
            link(tt(t0, e_re, a_re, ALU.mult))
            link(tt(t1, e_im, a_im, ALU.mult))
            link(tt(g_re, t1, t0, ALU.subtract))
            link(tt(g_re, g_re, den, ALU.mult))
            link(tt(t0, e_re, a_im, ALU.mult))
            link(tt(t1, e_im, a_re, ALU.mult))
            link(tt(g_im, t0, t1, ALU.add))
            link(stt(g_im, g_im, -1.0, den, ALU.mult, ALU.mult))
            link(tt(t0, c_re, g_re, ALU.mult))
            link(tt(t1, c_im, g_im, ALU.mult))
            link(tt(w_re, t0, t1, ALU.subtract))
            link(tt(t0, c_re, g_im, ALU.mult))
            link(tt(t1, c_im, g_re, ALU.mult))
            link(tt(w_im, t0, t1, ALU.add))
            lo, hi = slice(0, SSM_N), slice(SSM_N, P)
            link(ts(f1[lo, :], w_re[lo, :], 2.0, None, ALU.mult))
            link(ts(f2[lo, :], w_im[lo, :], -2.0, None, ALU.mult))
            link(ts(f1[hi, :], w_im[hi, :], -2.0, None, ALU.mult))
            link(ts(f2[hi, :], w_re[hi, :], -2.0, None, ALU.mult))
            dve.wait_ge(gen_s, 9)
            link(tt(m.fac_b, m.fac_b, mag_b, ALU.mult))
            link(tt(grid(cnt_b[:, 0:S * SA], SA), grid(mag_a, SA), per_s(f1, SA), ALU.mult))
            link(tt(grid(ang_a, SA), per_s(im, SA), lags(lag_a, SA), ALU.mult))
            link(turns_off(nc, link, cnt_a, ang_a, 0.0, ang_a, 0.0))
            mark("ang_a2")
            dve.wait_ge(gen_s, 10)
            link(tt(grid(cnt_a, SA), grid(cnt_a, SA), per_s(f2, SA), ALU.mult))
            link(tt(cnt_b[:, 0:S * SA], cnt_b[:, 0:S * SA], cnt_a, ALU.add))
            link(tt(m.fac_a, m.fac_a, cnt_b[:, 0:S * SA], ALU.mult))
            dve.wait_ge(head_done, HQ)
            for n in range(1, KT * HT, 2):
                link(nc.vector.tensor_copy(m.cond_t[:, n // HT, (n % HT) * 512:(n % HT) * 512 + 512], bank(m, n)))

        @block.scalar
        def _(act):
            def f(n, dst, src, func):
                act.wait_ge(gen_v, n)
                nc.scalar.activation(dst, src, func).then_inc(gen_s, 1)

            def split(h, i, n, uses):
                if isinstance(h, int) and h < RING:
                    pass
                else:
                    act.wait_ge(head_done, h + 1 - RING)
                out_row = out_t[:, bass.ds(h, 1), :].rearrange("p o n -> p (o n)")
                nc.scalar.activation(exact(out_high[:, n, :]), out_row, ACT.Copy).then_inc(high_ready, 1)
                act.wait_ge(m.wo_in[i], 16 * uses)
                nc.scalar.activation(exact(wo_high[:, n, :]), m.wo_raw[:, i, :], ACT.Copy).then_inc(high_ready, 1)

            functions = [
                (),
                (("half_re", th, half_re, ACT.Tanh), ("mag_b", m.fac_b, mag_b, ACT.Exp), ("mag_a", m.fac_a, mag_a, ACT.Exp)),
                (("sh", sh, arg_s, ACT.Sin), ("ch", ch, arg_c, ACT.Sin)),
                (),
                (("ang_b", mag_b, ang_b, ACT.Sin),),
                (("ang_a", mag_a, ang_a, ACT.Sin),),
                (),
                (("ang_a2", cnt_a, ang_a, ACT.Sin),),
            ]
            split(0, 0, 0, 1)
            act.wait_ge(ssm_in, 16 * 7)
            nc.scalar.activation(dt, log_dt, ACT.Exp).then_inc(gen_s, 1)
            nc.scalar.activation(a_re, log_a, ACT.Exp).then_inc(gen_s, 1)
            for h in range(PEELED):
                if h:
                    split(h, h % 2, h % RING, h // 2 + 1)
                for name, dst, src, func in functions[h]:
                    f(gen[name], dst, src, func)
            with act.Fori(0, LOOPS) as it:
                for j in range(PER):
                    split(PER * it + (PEELED + j), (PEELED + j) % 2, (PEELED + j) % RING, PER // 2 * it + ((PEELED + j) // 2 + 1))
            act.wait_ge(head_done, HQ)
            for n in range(0, KT * HT, 2):
                nc.scalar.activation(m.cond_t[:, n // HT, (n % HT) * 512:(n % HT) * 512 + 512], bank(m, n), ACT.Copy).then_inc(cond_copied, 1)
            act.wait_ge(cond_copied, KT * HT // 2)


def toeplitz(sp, m, s, slot):
    src = bass.AP(m.lag_dram.tensor, s * (L + P), [[1, P], [1, L]])
    sp.dma_start(m.toep[:, slot, :], src).then_inc(m.toep_in[slot], 16)


def attend_own(nc, t, m):
    sem = m.sem
    o = m.own_from
    region = {}
    for name, cols in (("ct", DM), ("qkv", 3 * DM), ("norm", 2 * DM), ("qT", DM), ("kT", DM), ("keys", 4 * 8 * P),
                       ("vals", 4 * 8 * 64), ("aT", DM), ("um", DM), ("umT", KT * TOK)):
        region[name] = m.big[:, o:o + cols]
        o += cols
    soft = m.qb[:, S * SB2:S * SB2 + NH2 * S]
    scope = ExitStack()

    def parts(name, shape):
        return tuple(scope.enter_context(nc.sbuf_tensor(f"{name}_{part}", [P] + shape, F32)) for part in ("high", "low"))

    wqk_high, wqk_low = parts("w_qk", [2, KT, DM])
    ct_high, ct_low = parts("ct", [KT * P])
    assert o <= HQ * TOK
    alibi = m.alibi.rearrange("p (h k) -> p h k", h=NH2)
    m.toep = m.big[:, 0:TOEP * L].rearrange("p (s n) -> p s n", s=TOEP)
    m.toep_in = [sem(f"toep_in{i}") for i in range(TOEP)]
    m.y_t = region["keys"].rearrange("p (k n) -> p k n", k=KT)
    m.um_t = region["umT"].rearrange("p (k n) -> p k n", k=KT)
    ct = region["ct"].rearrange("p (k n) -> p k n", k=KT)
    qkv = region["qkv"].rearrange("p (c n) -> p c n", c=3)
    norm = region["norm"].rearrange("p (c n) -> p c n", c=2)
    q_t, k_t = (region[n].rearrange("p (k n) -> p k n", k=KT) for n in ("qT", "kT"))
    key_blocks = region["keys"].rearrange("p (k b h n) -> p k b h n", k=KT, b=BPT, h=8)
    val_blocks = region["vals"].rearrange("p (b g h d) -> p b g h d", b=BPT, g=8, h=4)
    a_t = region["aT"].rearrange("p (k n) -> p k n", k=KT)
    w_out = m.w_out
    um = region["um"]
    o = 0
    def cols(n):
        nonlocal o
        o += n
        return m.wk[:, 2048 + o - n:2048 + o]
    stats, mv, var, std, rstd, hmax, hsum, hinv = cols(12), cols(4), cols(2), cols(2), cols(2), cols(NH2), cols(NH2), cols(NH2)
    head_mask, ln, eps = cols(8), cols(4 * KT), cols(1)
    ln = ln.rearrange("p (w k) -> p w k", w=4)
    stats = stats.rearrange("p (c n) -> p c n", c=2)
    lags = cols(S * SB2)
    skip, last_row = cols(S), cols(1)
    zero = cols(P)
    pexp, p_t = cols(NH2 * S), cols(NH2 * S)
    assert 2048 + o <= 8 * LA + 2 * 5 * P

    parts_in = sem("parts_in4")
    lag_ready, lag_out, zeroed = sem("lag_ready"), sem("lag_out"), sem("zeroed")
    lag_made = sem("lag_made")
    vector_order, scalar_order, pool_order = sem("vector_order4"), sem("scalar_order4"), sem("pool_order4")
    tile_in = sem("tile_in")
    ct_high_ready = sem("ct_high_ready")
    wqk_high_ready, wqk_low_ready = sem("wqk_high_ready"), sem("wqk_low_ready")
    made = sem("made")
    clipped = sem("clipped")
    var_ready, std_ready = sem("var_ready"), sem("std_ready")
    normed = sem("ln_normed")
    qk_turned = sem("qk_turned")
    q_scaled, k_scaled = sem("q_scaled"), sem("k_scaled")
    blocks_v, blocks_p, blocks_a = sem("key_blocks_v"), sem("key_blocks_p"), sem("key_blocks_a")
    vals_ready = sem("vals_ready")
    scored = sem("scored4")
    shifted = sem("shifted")
    exped = sem("exped4")
    probs_ready = sem("probs_ready")
    p_turned, p_copied = sem("p_turned4"), sem("p_copied4")
    attended, att_copied = sem("attended"), sem("att_copied")
    out_ready, x_ready = sem("out_ready4"), sem("x_ready")
    masked = sem("um_masked")
    um_turned, um_copied = sem("um_turned"), sem("um_copied")
    PARTS = 16 * 4
    BLOCKS_V, BLOCKS_P, BLOCKS_A = range(0, 4), range(4, 6), range(6, 8)
    QKV, SC, TR, AO = 0, 3, 5, 7

    with scope, nc.Block() as block:
        @block.sync
        def _(sp):
            sp.dma_start(head_mask, t["consts"][:, C_HM:C_HM + 8]).then_inc(parts_in, 16)
            sp.dma_start(ln.rearrange("p w k -> p (w k)"), t["ln"].rearrange("p w k -> p (w k)")).then_inc(parts_in, 16)
            sp.dma_start(skip, row_of(t["d_skip"], S)).then_inc(parts_in, 16)
            sp.dma_start(last_row, t["consts"][:, C_LAST:C_LAST + 1]).then_inc(parts_in, 16)
            sp.wait_ge(lag_made, 1)
            sp.dma_start(m.lag_dram[:, 0:L].rearrange("s (a b) -> a s b", a=SA), lags[0:SA, :].rearrange("p (s b) -> p s b", s=S)).then_inc(lag_out, 16)
            sp.dma_start(m.lag_dram[:, L:L + P], zero[0:S, :]).then_inc(lag_out, 16)
            sp.wait_ge(lag_out, 32)
            sp.wait_ge(made, 3 * TILES + LEAD)
            for i in range(TOEP):
                toeplitz(sp, m, i, i)

        @block.gpsimd
        def _(pool):
            pool.sem_inc(tile_in, LEAD)
            pool.sem_inc(blocks_p, LEAD)
            pool.wait_ge(parts_in, PARTS)
            pool.wait_ge(m.own_in, 16 * 4)

            def hidden(tile):
                if not isinstance(tile, int):
                    pool.wait_ge(made, 3 * tile + LEAD)
                hidden_states = m.cond_t[:, :, bass.ds(tile * P, P)]
                nc.gpsimd.tensor_copy(ct, hidden_states)
                nc.gpsimd.tensor_copy(exact(ct_high[:, :].rearrange("p (k n) -> p k n", k=KT)), hidden_states).then_inc(ct_high_ready, 1)
                pool.wait_ge(ct_high_ready, tile)
                nc.gpsimd.tensor_tensor(exact(ct_low[:, :]), ct.rearrange("p k n -> p (k n)"), ct_high[:, :], ALU.subtract).then_inc(tile_in, 1)

            def blocks(tile):
                pool.wait_ge(k_scaled, tile + 1 + LEAD)
                pool.wait_ge(scored, tile + LEAD)
                apart(pool, m)
                for h in BLOCKS_P:
                    ins = nc.gpsimd.tensor_scalar(key_blocks[:, :, :, h, :], k_t.rearrange("p k (b n) -> p k b n", b=BPT),
                                                  head_mask[:, h:h + 1], 1.0, ALU.mult, ALU.mult)
                ins.then_inc(blocks_p, 1)

            hidden(1)
            blocks(0)
            with pool.Fori(1, TILES - 1) as tile:
                hidden(tile + 1)
                blocks(tile)
            blocks(TILES - 1)

        @block.tensor
        def _(pe):
            for s in (made, qk_turned, scored, p_turned, attended, out_ready, um_turned):
                pe.sem_inc(s, LEAD)
            def project(tile, parts):
                first = isinstance(tile, int)
                if not first:
                    pe.wait_ge(tile_in, tile + LEAD)
                for part in parts:
                    c = min(part, 2)
                    if part < 3:
                        pe.wait_ge(clipped, 3 * tile + c + 1 - 3 + LEAD)
                    for k in range(KT) if c < 2 else range(0, KT - 1) if part == 2 else range(KT - 1, KT):
                        rows = slice(k * P, (k + 1) * P)
                        if c < 2 and not first:
                            nc.tensor.matmul(bank(m, QKV + c), exact(ct_high[:, rows]), exact(wqk_high[:, c, k, :]), start=(k == 0), stop=False)
                            nc.tensor.matmul(bank(m, QKV + c), exact(ct_high[:, rows]), exact(wqk_low[:, c, k, :]), start=False, stop=False)
                            ins = nc.tensor.matmul(bank(m, QKV + c), exact(ct_low[:, rows]), exact(wqk_high[:, c, k, :]), start=False, stop=(k == KT - 1))
                        else:
                            ins = nc.tensor.matmul(bank(m, QKV + c), m.cond_t[:, k, 0:P] if first else ct[:, k, :],
                                                   m.w_qkv[:, k, c * DM:(c + 1) * DM], start=(k == 0), stop=(k == KT - 1))
                    if part != 2:
                        ins.then_inc(made, 1)

            def turn_qk(tile):
                pe.wait_ge(normed, 2 * tile + 2 + LEAD)
                pe.wait_ge(p_copied, 2 * tile + LEAD)
                for c in range(2):
                    for k in range(KT):
                        ins = nc.tensor.transpose(bank(m, TR + c)[:, k * P:(k + 1) * P], norm[:, c, k * P:(k + 1) * P], m.ident)
                ins.then_inc(qk_turned, 1)

            def score(tile):
                pe.wait_ge(q_scaled, tile + 1 + LEAD)
                pe.wait_ge(blocks_v, tile + 1 + LEAD)
                pe.wait_ge(blocks_p, tile + 1 + LEAD)
                pe.wait_ge(blocks_a, tile + 1 + LEAD)
                pe.wait_ge(shifted, tile + LEAD)
                for b in range(BPT):
                    for k in range(KT):
                        ins = nc.tensor.matmul(bank(m, SC + k // 2)[b * S:(b + 1) * S, (k % 2) * 256:(k % 2) * 256 + 256],
                                               q_t[:, k, b * S:(b + 1) * S], key_blocks[:, k, b, :, :], start=True, stop=True,
                                               skip_group_check=True)
                ins.then_inc(scored, 1)

            def turn_probs(tile):
                pe.wait_ge(probs_ready, tile + 1 + LEAD)
                for g in range(8):
                    ins = nc.tensor.transpose(bank(m, TR + g // 4)[:, (g % 4) * P:(g % 4 + 1) * P], pexp[:, g * P:(g + 1) * P], m.ident)
                    if g % 4 == 3:
                        ins.then_inc(p_turned, 1)

            def attend(tile):
                pe.wait_ge(vals_ready, tile + 1 + LEAD)
                pe.wait_ge(um_copied, tile + LEAD)
                for half in range(2):
                    pe.wait_ge(p_copied, 2 * tile + half + 1 + LEAD)
                    for b in range(BPT):
                        for g in range(4 * half, 4 * half + 4):
                            r = 64 * (g % 2)
                            ins = nc.tensor.matmul(bank(m, AO)[r:r + 64, (g // 2) * P + b * S:(g // 2) * P + (b + 1) * S],
                                                   val_blocks[:, b, g, :, :].rearrange("p h d -> p (h d)"),
                                                   p_t[:, g * P + b * S:g * P + (b + 1) * S], start=True, stop=True, skip_group_check=True)
                ins.then_inc(attended, 1)

            def output(tile):
                pe.wait_ge(att_copied, tile + 1 + LEAD)
                for k in range(KT):
                    ins = nc.tensor.matmul(bank(m, AO), a_t[:, k, :], w_out[:, k, :], start=(k == 0), stop=(k == KT - 1))
                ins.then_inc(out_ready, 1)

            def turn_um(tile):
                pe.wait_ge(masked, tile + 1 + LEAD)
                for k in range(KT):
                    ins = nc.tensor.transpose(bank(m, AO)[:, k * P:(k + 1) * P], um[:, k * P:(k + 1) * P], m.ident)
                ins.then_inc(um_turned, 1)

            pe.wait_ge(m.own_in, 16 * 4)
            project(0, (0, 1))
            for s in range(S):
                ins = nc.tensor.matmul(bank(m, QKV + 3 + s // 16)[0:SA, (s % 16) * SB2:(s % 16 + 1) * SB2],
                                       m.fac_a[:, s * SA:(s + 1) * SA], m.fac_b[:, s * SB2:(s + 1) * SB2], start=True, stop=True)
            ins.then_inc(lag_ready, 1)
            project(0, (2,))
            turn_qk(0)
            project(0, (3,))
            pe.wait_ge(lag_made, 1)
            score(0)
            pe.wait_ge(wqk_low_ready, 2 * KT)
            with pe.Fori(0, TILES - 1) as tile:
                project(tile + 1, (0, 1, 2))
                turn_probs(tile)
                project(tile + 1, (3,))
                attend(tile)
                turn_qk(tile + 1)
                output(tile)
                score(tile + 1)
                turn_um(tile)
            turn_probs(TILES - 1)
            attend(TILES - 1)
            output(TILES - 1)
            turn_um(TILES - 1)

        @block.scalar
        def _(act):
            for s in (std_ready, q_scaled, blocks_a, exped, p_copied, vals_ready, um_copied):
                act.sem_inc(s, LEAD)
            link = link_on(act, scalar_order)
            act.wait_ge(parts_in, PARTS)
            act.wait_ge(m.own_in, 16 * 4)
            for c in range(2):
                for k in range(KT):
                    nc.scalar.activation(exact(wqk_high[:, c, k, :]), m.w_qkv[:, k, c * DM:(c + 1) * DM], ACT.Copy).then_inc(wqk_high_ready, 1)
            act.wait_ge(zeroed, 1)

            def roots(tile):
                act.wait_ge(var_ready, tile + 1 + LEAD)
                nc.scalar.activation(std, var, ACT.Sqrt).then_inc(std_ready, 1)

            def values(tile):
                act.wait_ge(clipped, 3 * tile + 3 + LEAD)
                act.wait_ge(attended, tile + LEAD)
                for b in range(BPT):
                    for h in range(4):
                        src = qkv[b * S:(b + 1) * S, 2, :].rearrange("p (g h d) -> p g h d", g=8, h=4)[:, :, h, :]
                        ins = nc.scalar.activation(val_blocks[h * S:(h + 1) * S, b, :, h, :], src, ACT.Copy)
                ins.then_inc(vals_ready, 1)

            def scale_queries(tile):
                act.wait_ge(qk_turned, tile + 1 + LEAD)
                act.wait_ge(scored, tile + LEAD)
                for k in range(KT):
                    ins = nc.scalar.activation(q_t[:, k, :], bank(m, TR)[:, k * P:(k + 1) * P], ACT.Identity,
                                               scale=ln[:, 0, k:k + 1], bias=ln[:, 1, k:k + 1])
                ins.then_inc(q_scaled, 1)

            def blocks(tile):
                act.wait_ge(k_scaled, tile + 1 + LEAD)
                for h in BLOCKS_A:
                    ins = nc.scalar.activation(key_blocks[:, :, :, h, :], k_t.rearrange("p k (b n) -> p k b n", b=BPT),
                                               ACT.Copy, scale=head_mask[:, h:h + 1])
                ins.then_inc(blocks_a, 1)

            def exponentials(tile):
                act.wait_ge(shifted, tile + 1 + LEAD)
                nc.scalar.activation(pexp, soft, ACT.Exp).then_inc(exped, 1)

            def copy_probs(tile):
                for half in range(2):
                    act.wait_ge(p_turned, 2 * tile + half + 1 + LEAD)
                    nc.scalar.activation(p_t[:, half * 512:(half + 1) * 512], bank(m, TR + half), ACT.Copy).then_inc(p_copied, 1)

            def copy_attended(tile):
                act.wait_ge(attended, tile + 1 + LEAD)
                nc.scalar.activation(a_t.rearrange("p k n -> p (k n)"), bank(m, AO), ACT.Copy).then_inc(att_copied, 1)

            def copy_um(tile):
                act.wait_ge(um_turned, tile + 1 + LEAD)
                nc.scalar.activation(m.um_t.rearrange("p k (s b) -> p k s b", b=B)[:, :, :, bass.ds(tile * BPT, BPT)].rearrange("p k s b -> p (k s) b"),
                                     bank(m, AO).rearrange("p (k b s) -> p k s b", k=KT, b=BPT), ACT.Copy).then_inc(um_copied, 1)

            roots(0)
            scale_queries(0)
            blocks(0)
            values(0)
            exponentials(0)
            with act.Fori(0, TILES - 1) as tile:
                copy_probs(tile)
                roots(tile + 1)
                copy_attended(tile)
                scale_queries(tile + 1)
                blocks(tile + 1)
                values(tile + 1)
                copy_um(tile)
                exponentials(tile + 1)
            copy_probs(TILES - 1)
            copy_attended(TILES - 1)
            copy_um(TILES - 1)

        @block.vector
        def _(dve):
            for s in (clipped, var_ready, normed, k_scaled, blocks_v, shifted, probs_ready, att_copied, x_ready, masked):
                dve.sem_inc(s, LEAD)
            tt, ts = nc.vector.tensor_tensor, nc.vector.tensor_scalar
            link = link_on(dve, vector_order)
            nc.vector.memset(region["vals"], 0.0).then_inc(zeroed, 1)
            for c in range(2):
                for k in range(KT):
                    dve.wait_ge(wqk_high_ready, KT * c + k + 1)
                    nc.vector.tensor_tensor(exact(wqk_low[:, c, k, :]), m.w_qkv[:, k, c * DM:(c + 1) * DM], wqk_high[:, c, k, :],
                                            ALU.subtract).then_inc(wqk_low_ready, 1)
            dve.wait_ge(parts_in, PARTS)
            dve.wait_ge(m.own_in, 16 * 4)
            link(nc.vector.memset(zero, 0.0))

            def clip(tile, c):
                dve.wait_ge(made, 3 * tile + c + 1 + LEAD)
                if c == 2:
                    dve.wait_ge(vals_ready, tile + LEAD)
                ts(qkv[:, c, :], bank(m, QKV + c), CLIP, -CLIP, ALU.min, ALU.max).then_inc(clipped, 1)

            def layer_norm(tile):
                dve.wait_ge(clipped, 3 * tile + 2 + LEAD)
                nc.vector.bn_stats(stats[:, 0, :], qkv[:, 0, :])
                link(nc.vector.bn_stats(stats[:, 1, :], qkv[:, 1, :]))
                apart(dve, m)
                nc.vector.bn_aggr(mv[:, 0:2], stats[:, 0, :])
                link(nc.vector.bn_aggr(mv[:, 2:4], stats[:, 1, :]))
                apart(dve, m)
                ts(var, mv.rearrange("p (c n) -> p c n", c=2)[:, :, 1], EPS_LN, None, ALU.add).then_inc(var_ready, 1)
                dve.wait_ge(std_ready, tile + 1 + LEAD)
                link(nc.vector.reciprocal(rstd, std))
                dve.wait_ge(qk_turned, tile + LEAD)
                for c in range(2):
                    ts(norm[:, c, :], qkv[:, c, :], mv[:, 2 * c:2 * c + 1], rstd[:, c:c + 1], ALU.subtract, ALU.mult).then_inc(normed, 1)

            def scale_keys(tile):
                dve.wait_ge(qk_turned, tile + 1 + LEAD)
                dve.wait_ge(blocks_p, tile + LEAD)
                dve.wait_ge(blocks_a, tile + LEAD)
                for k in range(KT):
                    ins = ts(k_t[:, k, :], bank(m, TR + 1)[:, k * P:(k + 1) * P], ln[:, 2, k:k + 1], ln[:, 3, k:k + 1], ALU.mult, ALU.add)
                ins.then_inc(k_scaled, 1)
                dve.wait_ge(k_scaled, tile + 1 + LEAD)
                dve.wait_ge(scored, tile + LEAD)
                for h in BLOCKS_V:
                    ins = ts(key_blocks[:, :, :, h, :], k_t.rearrange("p k (b n) -> p k b n", b=BPT), head_mask[:, h:h + 1], None, ALU.mult)
                ins.then_inc(blocks_v, 1)

            s3 = soft.rearrange("p (h k) -> p h k", h=NH2)
            e3 = pexp.rearrange("p (h k) -> p h k", h=NH2)

            def shift(tile):
                dve.wait_ge(scored, tile + 1 + LEAD)
                for i in range(2):
                    half = slice(i * 512, (i + 1) * 512)
                    ins = nc.vector.scalar_tensor_tensor(soft[:, half], bank(m, SC + i), SCALE2, m.alibi[:, half], ALU.mult, ALU.add)
                link(ins)
                link(nc.vector.tensor_reduce(hmax, s3, AX.X, ALU.max))
                tt(s3, s3, hmax.unsqueeze(2).broadcast_to([P, NH2, S]), ALU.subtract).then_inc(shifted, 1)

            def normalise(tile):
                dve.wait_ge(exped, tile + 1 + LEAD)
                link(nc.vector.tensor_reduce(hsum, e3, AX.X, ALU.add))
                link(nc.vector.reciprocal(hinv, hsum))
                tt(e3, e3, hinv.unsqueeze(2).broadcast_to([P, NH2, S]), ALU.mult).then_inc(probs_ready, 1)

            def residual(tile):
                dve.wait_ge(out_ready, tile + 1 + LEAD)
                row = m.x[:, bass.ds(tile, 1), :].rearrange("p o n -> p (o n)")
                link(tt(row, row, bank(m, AO), ALU.add))
                nc.vector.scalar_tensor_tensor(um, m.keys, m.lens2_rows[:, bass.ds(tile, 1)], row, ALU.is_lt, ALU.mult).then_inc(masked, 1)

            clip(0, 0)
            clip(0, 1)
            layer_norm(0)
            dve.wait_ge(lag_ready, 1)
            for i in range(2):
                link(nc.vector.tensor_copy(lags[0:SA, i * 512:(i + 1) * 512], bank(m, 3 + i)[0:SA, :]))
            lag0 = lags[0:SA, :].rearrange("p (s b) -> p s b", s=S)[:, :, SB2 - 1]
            nc.vector.scalar_tensor_tensor(lag0, skip[0:SA, :], last_row[0:SA, :], lag0, ALU.mult, ALU.add).then_inc(lag_made, 1)
            scale_keys(0)
            clip(0, 2)
            shift(0)
            with dve.Fori(0, TILES - 1) as tile:
                link.begin(tile, 8)
                clip(tile + 1, 0)
                normalise(tile)
                clip(tile + 1, 1)
                layer_norm(tile + 1)
                clip(tile + 1, 2)
                scale_keys(tile + 1)
                residual(tile)
                shift(tile + 1)
            link.end(TILES - 1)
            normalise(TILES - 1)
            residual(TILES - 1)


def convolve(nc, t, m):
    sem = m.sem
    RING = 8
    rev = m.wk[:, 0:KT]
    mask = m.wk[:, 128:128 + KT * B].rearrange("p (k b) -> p k b", k=KT)
    rev_in = sem("rev_in")
    o = m.own_from
    raw = m.big[:, o:o + KT * DM]; o += KT * DM
    m.w_rl = m.big[:, o:o + KT * RL].rearrange("p (k n) -> p k n", k=KT); o += KT * RL
    m.lora_b = m.big[:, o:o + DM]; o += DM
    m.b_base = m.big[:, o:o + DM]; o += DM
    m.b_router = m.big[:, o:o + EXP]
    m.ffn_in = sem("ffn_in")
    weights_in, high_ready, low_ready = sem("ffn_weights_in"), sem("ffn_high_ready"), sem("ffn_low_ready")
    convolved, copied, order = sem("convolved"), sem("conv_copied"), sem("vector_order5")
    u_t = m.um_t.rearrange("p k (s b) -> p k s b", b=B)
    y_t = m.y_t.rearrange("p k (b s) -> p k b s", b=B)

    with nc.Block() as block:
        @block.sync
        def _(sp):
            sp.dma_start(rev, t["consts"][:, C_REV:C_REV + KT]).then_inc(rev_in, 16)
            sp.dma_start(raw, t["w_base"].rearrange("p k n -> p (k n)")).then_inc(weights_in, 16)
            for dst, src in ((m.w_rl, t["w_rl"]), (m.lora_b, t["lora_b"]), (m.b_base, row_of(t["b_base"], DM)), (m.b_router, row_of(t["b_router"], EXP))):
                sp.dma_start(dst, src).then_inc(m.ffn_in, 16)
            for i in range(S - TOEP):
                sp.wait_ge(convolved, i + 1)
                toeplitz(sp, m, TOEP + i, i)

        @block.scalar
        def _(act):
            act.wait_ge(weights_in, 16)
            for piece in range(KT):
                cols = slice(piece * DM, (piece + 1) * DM)
                nc.scalar.activation(exact(m.base_high[:, cols]), raw[:, cols], ACT.Copy).then_inc(high_ready, 1)

        @block.gpsimd
        def _(pool):
            for piece in range(KT):
                cols = slice(piece * DM, (piece + 1) * DM)
                pool.wait_ge(high_ready, piece + 1)
                nc.gpsimd.tensor_tensor(exact(m.base_low[:, cols]), raw[:, cols], m.base_high[:, cols], ALU.subtract).then_inc(low_ready, 1)
            pool.wait_ge(low_ready, KT)

        @block.tensor
        def _(pe):
            with pe.Fori(0, S // TOEP) as it:
                for group in range(TOEP // RING):
                    for d in range(KT):
                        for i in range(RING):
                            slot = group * RING + i
                            s = TOEP * it + slot
                            if d == 0:
                                pe.wait_ge(m.toep_in[slot], 16 * it + 16)
                                pe.wait_ge(copied, s + 1 - RING + LEAD)
                            ins = nc.tensor.matmul(bank(m, i)[:, d * B:KT * B], m.toep[:, slot, L - (d + 1) * P:L - d * P],
                                                   u_t[:, 0:KT - d, bass.ds(s, 1), :].rearrange("p k o b -> p k (o b)"),
                                                   start=(d == 0), stop=(d == KT - 1), skip_group_check=True)
                            if d == KT - 1:
                                ins.then_inc(convolved, 1)

        @block.vector
        def _(dve):
            dve.sem_inc(copied, LEAD)
            link = link_on(dve, order)
            dve.wait_ge(rev_in, 16)
            link(nc.vector.tensor_tensor(mask, rev.unsqueeze(2).broadcast_to([P, KT, B]), m.lens2.unsqueeze(1).broadcast_to([P, KT, B]), ALU.is_lt))
            with dve.Fori(0, S // RING) as it:
                for i in range(RING):
                    s = RING * it + i
                    dve.wait_ge(convolved, s + 1)
                    nc.vector.tensor_tensor(y_t[:, :, :, bass.ds(s, 1)].rearrange("p k b o -> p k (b o)"),
                                            bank(m, i)[:, 0:KT * B].rearrange("p (k b) -> p k b", k=KT), mask, ALU.mult).then_inc(copied, 1)
            dve.wait_ge(copied, S + LEAD)


def feed_forward(nc, t, m):
    sem = m.sem
    o = 0
    def cols(n, slots=2):
        nonlocal o
        o += n * slots
        return m.wk[:, o - n * slots:o].rearrange("p (s n) -> p s n", s=slots)
    y_tile, rest, lora_t = cols(DM), cols(DM), cols(P)
    lora_w = cols(P)
    logits, tau, weights = cols(EXP), cols(2), cols(EXP)
    pairs, pair_sums, count, sums, taus = cols(EXP * EXP), cols(EXP * EXP), cols(EXP), cols(EXP), cols(EXP)
    result = m.qb[:, 0:2 * DM].rearrange("p (s n) -> p s n", s=2)
    order = sem("vector_order6")
    y_ready = sem("y_tile_ready")
    y_high_ready, y_low_ready = sem("y_high_ready"), sem("y_low_ready")
    routed, based = sem("routed"), sem("based")
    weighted = sem("weighted")
    l_turned, l_copied, summed = sem("l_turned"), sem("l_copied"), sem("summed6")
    finished = sem("finished")
    out_done = [sem("out_done0"), sem("out_done1")]

    with nc.Block() as block:
        @block.scalar
        def _(act):
            for s in (y_ready, y_high_ready, l_copied):
                act.sem_inc(s, LEAD)

            def fetch(tile, j):
                act.wait_ge(based, tile + 1 - 2 + LEAD)
                nc.scalar.activation(y_tile[:, j, :].rearrange("p (k n) -> p k n", k=KT), m.y_t[:, :, bass.ds(tile * P, P)],
                                     ACT.Copy).then_inc(y_ready, 1)
                nc.scalar.activation(exact(m.y_high[:, j, :].rearrange("p (k n) -> p k n", k=KT)), m.y_t[:, :, bass.ds(tile * P, P)],
                                     ACT.Copy).then_inc(y_high_ready, 1)

            def lora(tile, j):
                act.wait_ge(l_turned, tile + 1 + LEAD)
                act.wait_ge(summed, tile + 1 - 2 + LEAD)
                nc.scalar.activation(lora_t[:, j, :], bank(m, 6 + j)[:, 0:P], ACT.Copy).then_inc(l_copied, 1)

            def iteration(it, last):
                fetch(2 * it + 1, 1)
                lora(2 * it, 0)
                if not last:
                    fetch(2 * it + 2, 0)
                lora(2 * it + 1, 1)

            fetch(0, 0)
            with act.Fori(0, TILES // 2 - 1) as it:
                iteration(it, False)
            iteration(TILES // 2 - 1, True)

        @block.gpsimd
        def _(pool):
            pool.sem_inc(y_low_ready, LEAD)
            with pool.Fori(0, TILES // 2) as it:
                for j in range(2):
                    tile = 2 * it + j
                    pool.wait_ge(y_high_ready, tile + 1 + LEAD)
                    nc.gpsimd.tensor_tensor(exact(m.y_low[:, j, :].rearrange("p (k n) -> p k n", k=KT)), m.y_t[:, :, bass.ds(tile * P, P)],
                                            m.y_high[:, j, :].rearrange("p (k n) -> p k n", k=KT), ALU.subtract).then_inc(y_low_ready, 1)

        @block.tensor
        def _(pe):
            for s in (routed, based, l_turned, summed):
                pe.sem_inc(s, LEAD)

            def route(tile, j):
                pe.wait_ge(y_ready, tile + 1 + LEAD)
                for k in range(KT):
                    ins = nc.tensor.matmul(bank(m, 4 + j)[:, 0:RL], y_tile[:, j, k * P:(k + 1) * P], m.w_rl[:, k, :],
                                           start=(k == 0), stop=(k == KT - 1))
                ins.then_inc(routed, 1)

            def base(tile, j):
                pe.wait_ge(y_low_ready, tile + 1 + LEAD)
                pe.wait_ge(finished, tile + 1 - 2 + LEAD)
                for k in range(KT):
                    rows, cols = slice(k * P, (k + 1) * P), slice(k * DM, (k + 1) * DM)
                    nc.tensor.matmul(bank(m, 2 * j), exact(m.y_high[:, j, rows]), exact(m.base_high[:, cols]), start=(k == 0), stop=False)
                    nc.tensor.matmul(bank(m, 2 * j), exact(m.y_high[:, j, rows]), exact(m.base_low[:, cols]), start=False, stop=False)
                    ins = nc.tensor.matmul(bank(m, 2 * j), exact(m.y_low[:, j, rows]), exact(m.base_high[:, cols]), start=False, stop=False)
                ins.then_inc(based, 1)

            def turn(tile, j):
                pe.wait_ge(weighted, tile + 1 + LEAD)
                nc.tensor.transpose(bank(m, 6 + j)[:, 0:P], lora_w[:, j, :], m.ident).then_inc(l_turned, 1)

            def lora(tile, j):
                pe.wait_ge(l_copied, tile + 1 + LEAD)
                nc.tensor.matmul(bank(m, 2 * j), lora_t[:, j, :], m.lora_b, start=False, stop=True).then_inc(summed, 1)

            def iteration(it, last):
                for j in range(2):
                    tile = 2 * it + j
                    base(tile, j)
                    turn(tile, j)
                    if not (last and j == 1):
                        route(tile + 1, 1 - j)
                    lora(tile, j)

            pe.wait_ge(m.ffn_in, 16 * 4)
            route(0, 0)
            with pe.Fori(0, TILES // 2 - 1) as it:
                iteration(it, False)
            iteration(TILES // 2 - 1, True)

        @block.vector
        def _(dve):
            for s in (weighted, finished):
                dve.sem_inc(s, LEAD)
            tt, ts = nc.vector.tensor_tensor, nc.vector.tensor_scalar
            link = link_on(dve, order)
            dve.wait_ge(m.ffn_in, 16 * 4)
            def route_weights(tile, j):
                dve.wait_ge(routed, tile + 1 + LEAD)
                z, w = logits[:, j, :], weights[:, j, :]
                pair = pairs[:, j, :].rearrange("p (i k) -> p i k", i=EXP)
                psum_ = pair_sums[:, j, :].rearrange("p (i k) -> p i k", i=EXP)
                link(tt(z, bank(m, 4 + j)[:, 0:EXP], m.b_router, ALU.add))
                zk, zi = z.unsqueeze(1).broadcast_to([P, EXP, EXP]), z.unsqueeze(2).broadcast_to([P, EXP, EXP])
                link(tt(pair, zk, zi, ALU.is_ge))
                tt(psum_, pair, zk, ALU.mult)
                link(nc.vector.tensor_reduce(count[:, j, :], pair, AX.X, ALU.add))
                link(nc.vector.tensor_reduce(sums[:, j, :], psum_, AX.X, ALU.add))
                link(nc.vector.reciprocal(count[:, j, :], count[:, j, :]))
                link(nc.vector.scalar_tensor_tensor(taus[:, j, :], sums[:, j, :], -1.0, count[:, j, :], ALU.add, ALU.mult))
                link(nc.vector.tensor_reduce(tau[:, j, 0:1], taus[:, j, :], AX.X, ALU.max))
                link(ts(w, z, tau[:, j, 0:1], 0.0, ALU.subtract, ALU.max))
                tt(lora_w[:, j, :].rearrange("p (e r) -> p e r", e=EXP), bank(m, 4 + j)[:, EXP:RL].rearrange("p (e r) -> p e r", e=EXP),
                   w.unsqueeze(2).broadcast_to([P, EXP, RANK]), ALU.mult).then_inc(weighted, 1)

            def finish(tile, j, it):
                row = m.x[:, bass.ds(tile, 1), :].rearrange("p o n -> p (o n)")
                link(tt(rest[:, j, :], row, m.b_base, ALU.add))
                dve.wait_ge(summed, tile + 1 + LEAD)
                dve.wait_ge(out_done[j], 16 * it + 16)
                tt(result[:, j, :], rest[:, j, :], bank(m, 2 * j), ALU.add).then_inc(finished, 1)

            def iteration(it, last):
                route_weights(2 * it + 1, 1)
                finish(2 * it, 0, it)
                if not last:
                    route_weights(2 * it + 2, 0)
                finish(2 * it + 1, 1, it)

            route_weights(0, 0)
            with dve.Fori(0, TILES // 2 - 1) as it:
                link.begin(it, 2 * 9)
                iteration(it, False)
            link.end(TILES // 2 - 1)
            iteration(TILES // 2 - 1, True)

        @block.sync
        def _(sp):
            for s in out_done:
                sp.sem_inc(s, 16)
            with sp.Fori(0, TILES // 2) as it:
                for j in range(2):
                    sp.wait_ge(finished, 2 * it + j + 1 + LEAD)
                    sp.dma_start(t["out"][bass.ds((2 * it + j) * P, P), :], result[:, j, :]).then_inc(out_done[j], 16)
            for s in out_done:
                sp.wait_ge(s, 16 * (TILES // 2) + 16)


def layouts(i):
    def kt(w):
        return w.reshape(w.shape[0], KT, P).transpose(2, 1, 0)

    x = i["x"].reshape(TOK, DM)
    back = i["L0_ffn_W_base"][:, :].reshape(DM, KT, P)[:, :, ::-1].transpose(2, 1, 0)
    router = i["L0_ffn_W_router"].reshape(EXP, KT, P)[:, :, ::-1].transpose(2, 1, 0)
    lora = i["L0_ffn_lora_A"].transpose(0, 2, 1).reshape(ER, KT, P)[:, :, ::-1].transpose(2, 1, 0)
    twice = lambda a: np.concatenate([a, a], 0)
    return {
        "x": x,
        "xT": x.reshape(TILES, P, KT, P).transpose(0, 3, 2, 1).reshape(TILES, P, DM),
        "table": i["itok_Bx16_0_63"], "lens": i["itok_B_207_1644"], "lens2": i["itok_B_8_3872"],
        "w1": kt(np.concatenate([i["L0_cond_Wv"], i["L0_cond_Wq"], i["L0_cond_Wk"]], 0)).reshape(P, KT, -1, 512)
              .transpose(2, 0, 1, 3).reshape(-1, P, KT * 512),
        "q_norm": i["L0_cond_q_norm_w"], "k_norm": i["L0_cond_k_norm_w"],
        "kT": i["L0_cond_k_cache"].reshape(PAGES, PSIZE, 2, HALF, D).transpose(2, 0, 4, 3, 1).reshape(2, PAGES, D, HALF * PSIZE),
        "v": i["L0_cond_v_cache"].reshape(PAGES, PSIZE, 2, HALF * D).transpose(2, 0, 1, 3),
        "wo": i["L0_cond_Wo"].reshape(DM, HQ, D).transpose(1, 2, 0),
        "w_qkv": kt(i["L0_attn_w_qkv"]), "w_out": kt(i["L0_attn_w_out"]),
        "ln": np.stack([i["L0_attn_" + n].reshape(KT, P).T for n in ("q_ln_w", "q_ln_b", "k_ln_w", "k_ln_b")], 1),
        "log_dt": i["L0_cond2_log_dt"], "log_a": twice(i["L0_cond2_log_A_real"].T), "a_imag": twice(i["L0_cond2_A_imag"].T),
        "c_re": twice(i["L0_cond2_C"][:, :, 0].T), "c_im": twice(i["L0_cond2_C"][:, :, 1].T), "d_skip": i["L0_cond2_D"],
        "w_base": back, "b_base": i["L0_ffn_b_base"], "w_rl": np.concatenate([router, lora], 2),
        "b_router": i["L0_ffn_b_router"], "lora_b": i["L0_ffn_lora_B"].reshape(ER, DM),
        "consts": constants(),
    }


def kernel(**inputs):
    import concourse.bacc as _bacc
    from concourse.bass_utils import run_bass_kernel_spmd as _run

    nc = _bacc.Bacc("TRN2", target_bir_lowering=False, num_devices=1)
    arrays = {n: np.ascontiguousarray(a) for n, a in layouts({n: np.asarray(a) for n, a in inputs.items()}).items()}
    t = {n: nc.dram_tensor("in_" + n, a.shape, mybir.dt.from_np(a.dtype), kind="ExternalInput").ap() for n, a in arrays.items()}
    t["out"] = nc.dram_tensor("out_x", [TOK, DM], F32, kind="ExternalOutput").ap()
    build(nc, t)
    r = _run(nc, [{"in_" + n: a for n, a in arrays.items()}], core_ids=[0])
    return r.results[0]["out_x"].reshape(B, S, DM)
```
